# Optimizing a Trainium2 kernel written in Bass

```python
import numpy as np
import jax
import jax.numpy as jnp

def _softmax(x, axis=-1):
    return jax.nn.softmax(x, axis=axis)

def _gelu(x):
    return jax.nn.gelu(x, approximate=True)

def _silu(x):
    return jax.nn.silu(x)

def _sigmoid(x):
    return jax.nn.sigmoid(x)

def _layernorm(x, axis=-1, eps=1e-05):
    m = jnp.mean(x, axis=axis, keepdims=True)
    v = jnp.var(x, axis=axis, keepdims=True)
    return (x - m) / jnp.sqrt(v + eps)

def _scatter_add(tgt, idx, src, axis=0):
    return tgt.at[idx].add(src)

def _segment_sum(src, seg, n):
    return jax.ops.segment_sum(src, seg, n)
kernel_name = 'mk_gnn_resnorm_d4_gnn_r64_bb629c'

def setup_inputs(seed: int=0):
    np.random.seed(seed)
    _w = jnp.asarray

    def _rec_inputs():
        import jax
        import jax.numpy as jnp
        _gk = jax.random.key(seed)
        x = -0.000202 + 1 * jax.random.normal(jax.random.fold_in(_gk, 1), (50000, 128), jnp.float32)
        src = jax.random.randint(jax.random.fold_in(_gk, 2), (25000,), 0, 50000, jnp.int32)
        dst = jnp.minimum((50000 * jax.random.uniform(jax.random.fold_in(_gk, 3), (25000,)) ** 2.0).astype(jnp.int32), 49999)
        _o = jnp.argsort(dst, stable=True)
        src = src[_o]
        dst = dst[_o]
        edge_attr_128 = -6.47781e-05 + 0.999943 * jax.random.normal(jax.random.fold_in(_gk, 12), (25000, 128), jnp.float32)
        return (x, src, dst, edge_attr_128)
    x, src, dst, edge_attr_128 = _rec_inputs()

    def _L0_gnn_setup():
        import jax, jax.numpy as jnp
        import numpy as np
        N_NODES, N_EDGES, N_INC = (50000, 10000, 12500)
        IN_C, HID_C, OUT_C = (128, 128, 128)
        EPS = 1e-05

        def _hconv(x, W, b, node_idx, edge_idx, hw):
            x = x @ W.T
            D = jax.ops.segment_sum(hw[edge_idx], node_idx, num_segments=N_NODES)
            Dinv = jnp.where(D > 0, 1.0 / D, 0.0)
            Bdeg = jax.ops.segment_sum(jnp.ones_like(edge_idx, dtype=x.dtype), edge_idx, num_segments=N_EDGES)
            Binv = jnp.where(Bdeg > 0, 1.0 / Bdeg, 0.0)
            e = jax.ops.segment_sum(Binv[edge_idx][:, None] * x[node_idx], edge_idx, num_segments=N_EDGES)
            out = jax.ops.segment_sum(Dinv[node_idx][:, None] * e[edge_idx], node_idx, num_segments=N_NODES)
            return out + b
        key = jax.random.key(seed)
        ks = jax.random.split(key, 6)
        x = jax.random.normal(ks[0], (N_NODES, IN_C), jnp.float32)
        node_idx = jax.random.randint(ks[1], (N_INC,), 0, N_NODES)
        edge_idx = jax.random.randint(ks[2], (N_INC,), 0, N_EDGES)
        hyperedge_index = jnp.stack([node_idx, edge_idx])
        hyperedge_weight = jnp.ones((N_EDGES,), jnp.float32)
        s1 = 1.0 / np.sqrt(IN_C)
        s2 = 1.0 / np.sqrt(HID_C)
        W1 = jax.random.uniform(ks[3], (HID_C, IN_C), jnp.float32, -s1, s1)
        b1 = jnp.zeros((HID_C,), jnp.float32)
        gamma = jnp.ones((HID_C,), jnp.float32)
        beta = jnp.zeros((HID_C,), jnp.float32)
        W2 = jax.random.uniform(ks[4], (OUT_C, HID_C), jnp.float32, -s2, s2)
        b2 = jnp.zeros((OUT_C,), jnp.float32)
        return dict(x=x, hyperedge_index=hyperedge_index, hyperedge_weight=hyperedge_weight, W1=W1, b1=b1, gamma=gamma, beta=beta, W2=W2, b2=b2)
    _L0_gnn_all = _L0_gnn_setup()
    _L0_gnn_in = {k: v for k, v in _L0_gnn_all.items() if k in ('hyperedge_weight', 'W1', 'b1', 'gamma', 'beta', 'W2', 'b2')}
    del _L0_gnn_all

    def _L1_gnn_setup():
        import jax, jax.numpy as jnp
        import numpy as np
        N, E = (50000, 12500)
        IN_F, HID, OUT, HEADS = (128, 64, 128, 4)
        NEG_SLOPE = 0.2

        def _gat_layer(x, W, a_src, a_dst, b, src, dst, heads, out_c):
            n = x.shape[0]
            h = (x @ W).reshape(n, heads, out_c)
            alpha_s = jnp.einsum('nhc,hc->nh', h, a_src)
            alpha_d = jnp.einsum('nhc,hc->nh', h, a_dst)
            e = jax.nn.leaky_relu(alpha_s[src] + alpha_d[dst], NEG_SLOPE)
            m = jax.ops.segment_max(e, dst, num_segments=n)
            ex = jnp.exp(e - m[dst])
            denom = jax.ops.segment_sum(ex, dst, num_segments=n)
            alpha = ex / denom[dst]
            out = jax.ops.segment_sum(alpha[:, :, None] * h[src], dst, num_segments=n)
            return out.reshape(n, heads * out_c) + b
        key = jax.random.key(seed)
        ks = jax.random.split(key, 10)
        s = 0.05
        return {'x': jax.random.normal(ks[0], (N, IN_F), dtype=jnp.float32), 'edge_index': jax.random.randint(ks[1], (2, E), 0, N, dtype=jnp.int64), 'W1': jax.random.normal(ks[2], (IN_F, HEADS * HID), dtype=jnp.float32) * s, 'att_src1': jax.random.normal(ks[3], (HEADS, HID), dtype=jnp.float32) * s, 'att_dst1': jax.random.normal(ks[4], (HEADS, HID), dtype=jnp.float32) * s, 'b1': jnp.zeros((HEADS * HID,), dtype=jnp.float32), 'W2': jax.random.normal(ks[5], (HEADS * HID, OUT), dtype=jnp.float32) * s, 'att_src2': jax.random.normal(ks[6], (1, OUT), dtype=jnp.float32) * s, 'att_dst2': jax.random.normal(ks[7], (1, OUT), dtype=jnp.float32) * s, 'b2': jnp.zeros((OUT,), dtype=jnp.float32)}
    _L1_gnn_all = _L1_gnn_setup()
    _L1_gnn_in = {k: v for k, v in _L1_gnn_all.items() if k in ('W1', 'att_src1', 'att_dst1', 'b1', 'W2', 'att_src2', 'att_dst2', 'b2')}
    del _L1_gnn_all

    def _L2_gnn_setup():
        import jax, jax.numpy as jnp
        import numpy as np
        N_NODES = 50000
        N_EDGES = 9375
        D = 128
        EPS = 1e-05

        def layer_norm(x, gamma, beta):
            mu = jnp.mean(x, axis=-1, keepdims=True)
            var = jnp.mean(jnp.square(x - mu), axis=-1, keepdims=True)
            return (x - mu) * jax.lax.rsqrt(var + EPS) * gamma + beta
        key = jax.random.key(seed)
        ks = jax.random.split(key, 12)
        s = 1.0 / np.sqrt(D)
        return {'h': jax.random.normal(ks[0], (N_NODES, D), dtype=jnp.float32), 'src': jax.random.randint(ks[1], (N_EDGES,), 0, N_NODES), 'dst': jax.random.randint(ks[2], (N_EDGES,), 0, N_NODES), 'W_pre': jax.random.uniform(ks[3], (D, D), jnp.float32, -s, s), 'b_pre': jax.random.uniform(ks[4], (D,), jnp.float32, -s, s), 'W1': jax.random.uniform(ks[5], (D, D), jnp.float32, -s, s), 'b1': jax.random.uniform(ks[6], (D,), jnp.float32, -s, s), 'W2': jax.random.uniform(ks[7], (D, D), jnp.float32, -s, s), 'b2': jax.random.uniform(ks[8], (D,), jnp.float32, -s, s), 'gamma': jnp.ones((D,), jnp.float32), 'beta': jnp.zeros((D,), jnp.float32)}
    _L2_gnn_all = _L2_gnn_setup()
    _L2_gnn_in = {k: v for k, v in _L2_gnn_all.items() if k in ('W_pre', 'b_pre', 'W1', 'b1', 'W2', 'b2', 'gamma', 'beta')}
    del _L2_gnn_all

    def _L3_gnn_setup():
        import jax, jax.numpy as jnp
        import numpy as np
        LOG2 = float(np.log(2.0))

        def ssp(x):
            return jax.nn.softplus(x) - LOG2

        def linear(x, W, b):
            return x @ W.T + b
        N, E, H, F = (100000, 25000, 128, 128)
        key = jax.random.key(seed)
        ks = jax.random.split(key, 14)
        s = 1.0 / np.sqrt(H)
        inp = {'h': jax.random.normal(ks[0], (N, H), dtype=jnp.float32), 'e': jax.random.normal(ks[1], (E, F), dtype=jnp.float32), 'W_node': jax.random.uniform(ks[2], (H, H), minval=-s, maxval=s), 'b_node': jax.random.uniform(ks[3], (H,), minval=-s, maxval=s), 'W_e1': jax.random.uniform(ks[4], (H, F), minval=-s, maxval=s), 'b_e1': jax.random.uniform(ks[5], (H,), minval=-s, maxval=s), 'W_e2': jax.random.uniform(ks[6], (H, H), minval=-s, maxval=s), 'b_e2': jax.random.uniform(ks[7], (H,), minval=-s, maxval=s), 'W_fc1': jax.random.uniform(ks[8], (H, H), minval=-s, maxval=s), 'b_fc1': jax.random.uniform(ks[9], (H,), minval=-s, maxval=s), 'W_fc2': jax.random.uniform(ks[10], (H, H), minval=-s, maxval=s), 'b_fc2': jax.random.uniform(ks[11], (H,), minval=-s, maxval=s), 'src': jax.random.randint(ks[12], (E,), 0, N, dtype=jnp.int32), 'dst': jax.random.randint(ks[13], (E,), 0, N, dtype=jnp.int32)}
        return inp
    _L3_gnn_all = _L3_gnn_setup()
    _L3_gnn_in = {k: v for k, v in _L3_gnn_all.items() if k in ('W_node', 'b_node', 'W_e1', 'b_e1', 'W_e2', 'b_e2', 'W_fc1', 'b_fc1', 'W_fc2', 'b_fc2')}
    del _L3_gnn_all
    return {'x': x, 'src': src, 'dst': dst, 'edge_attr_128': edge_attr_128, 'L0_gnn_hyperedge_weight': _L0_gnn_in['hyperedge_weight'], 'L0_gnn_W1': _L0_gnn_in['W1'], 'L0_gnn_b1': _L0_gnn_in['b1'], 'L0_gnn_gamma': _L0_gnn_in['gamma'], 'L0_gnn_beta': _L0_gnn_in['beta'], 'L0_gnn_W2': _L0_gnn_in['W2'], 'L0_gnn_b2': _L0_gnn_in['b2'], 'L1_gnn_W1': _L1_gnn_in['W1'], 'L1_gnn_att_src1': _L1_gnn_in['att_src1'], 'L1_gnn_att_dst1': _L1_gnn_in['att_dst1'], 'L1_gnn_b1': _L1_gnn_in['b1'], 'L1_gnn_W2': _L1_gnn_in['W2'], 'L1_gnn_att_src2': _L1_gnn_in['att_src2'], 'L1_gnn_att_dst2': _L1_gnn_in['att_dst2'], 'L1_gnn_b2': _L1_gnn_in['b2'], 'L2_gnn_W_pre': _L2_gnn_in['W_pre'], 'L2_gnn_b_pre': _L2_gnn_in['b_pre'], 'L2_gnn_W1': _L2_gnn_in['W1'], 'L2_gnn_b1': _L2_gnn_in['b1'], 'L2_gnn_W2': _L2_gnn_in['W2'], 'L2_gnn_b2': _L2_gnn_in['b2'], 'L2_gnn_gamma': _L2_gnn_in['gamma'], 'L2_gnn_beta': _L2_gnn_in['beta'], 'L3_gnn_W_node': _L3_gnn_in['W_node'], 'L3_gnn_b_node': _L3_gnn_in['b_node'], 'L3_gnn_W_e1': _L3_gnn_in['W_e1'], 'L3_gnn_b_e1': _L3_gnn_in['b_e1'], 'L3_gnn_W_e2': _L3_gnn_in['W_e2'], 'L3_gnn_b_e2': _L3_gnn_in['b_e2'], 'L3_gnn_W_fc1': _L3_gnn_in['W_fc1'], 'L3_gnn_b_fc1': _L3_gnn_in['b_fc1'], 'L3_gnn_W_fc2': _L3_gnn_in['W_fc2'], 'L3_gnn_b_fc2': _L3_gnn_in['b_fc2']}

def reference(x, src, dst, edge_attr_128, L0_gnn_hyperedge_weight, L0_gnn_W1, L0_gnn_b1, L0_gnn_gamma, L0_gnn_beta, L0_gnn_W2, L0_gnn_b2, L1_gnn_W1, L1_gnn_att_src1, L1_gnn_att_dst1, L1_gnn_b1, L1_gnn_W2, L1_gnn_att_src2, L1_gnn_att_dst2, L1_gnn_b2, L2_gnn_W_pre, L2_gnn_b_pre, L2_gnn_W1, L2_gnn_b1, L2_gnn_W2, L2_gnn_b2, L2_gnn_gamma, L2_gnn_beta, L3_gnn_W_node, L3_gnn_b_node, L3_gnn_W_e1, L3_gnn_b_e1, L3_gnn_W_e2, L3_gnn_b_e2, L3_gnn_W_fc1, L3_gnn_b_fc1, L3_gnn_W_fc2, L3_gnn_b_fc2):
    import jax
    import jax.numpy as jnp

    def _L0_gnn_ref(x, hyperedge_index, hyperedge_weight, W1, b1, gamma, beta, W2, b2):
        import jax, jax.numpy as jnp
        import numpy as np
        N_NODES, N_EDGES, N_INC = (50000, 10000, 12500)
        IN_C, HID_C, OUT_C = (128, 128, 128)
        EPS = 1e-05

        def _hconv(x, W, b, node_idx, edge_idx, hw):
            x = x @ W.T
            D = jax.ops.segment_sum(hw[edge_idx], node_idx, num_segments=N_NODES)
            Dinv = jnp.where(D > 0, 1.0 / D, 0.0)
            Bdeg = jax.ops.segment_sum(jnp.ones_like(edge_idx, dtype=x.dtype), edge_idx, num_segments=N_EDGES)
            Binv = jnp.where(Bdeg > 0, 1.0 / Bdeg, 0.0)
            e = jax.ops.segment_sum(Binv[edge_idx][:, None] * x[node_idx], edge_idx, num_segments=N_EDGES)
            out = jax.ops.segment_sum(Dinv[node_idx][:, None] * e[edge_idx], node_idx, num_segments=N_NODES)
            return out + b
        node_idx, edge_idx = (hyperedge_index[0], hyperedge_index[1])
        h = _hconv(x, W1, b1, node_idx, edge_idx, hyperedge_weight)
        mu = h.mean(axis=0)
        var = h.var(axis=0)
        h = gamma * (h - mu) * jax.lax.rsqrt(var + EPS) + beta
        return _hconv(h, W2, b2, node_idx, edge_idx, hyperedge_weight)

    def _L1_gnn_ref(x, edge_index, W1, att_src1, att_dst1, b1, W2, att_src2, att_dst2, b2):
        import jax, jax.numpy as jnp
        import numpy as np
        N, E = (50000, 12500)
        IN_F, HID, OUT, HEADS = (128, 64, 128, 4)
        NEG_SLOPE = 0.2

        def _gat_layer(x, W, a_src, a_dst, b, src, dst, heads, out_c):
            n = x.shape[0]
            h = (x @ W).reshape(n, heads, out_c)
            alpha_s = jnp.einsum('nhc,hc->nh', h, a_src)
            alpha_d = jnp.einsum('nhc,hc->nh', h, a_dst)
            e = jax.nn.leaky_relu(alpha_s[src] + alpha_d[dst], NEG_SLOPE)
            m = jax.ops.segment_max(e, dst, num_segments=n)
            ex = jnp.exp(e - m[dst])
            denom = jax.ops.segment_sum(ex, dst, num_segments=n)
            alpha = ex / denom[dst]
            out = jax.ops.segment_sum(alpha[:, :, None] * h[src], dst, num_segments=n)
            return out.reshape(n, heads * out_c) + b
        n = x.shape[0]
        loop = jnp.arange(n, dtype=edge_index.dtype)
        src = jnp.concatenate([edge_index[0], loop])
        dst = jnp.concatenate([edge_index[1], loop])
        h = _gat_layer(x, W1, att_src1, att_dst1, b1, src, dst, HEADS, HID)
        h = jax.nn.elu(h)
        out = _gat_layer(h, W2, att_src2, att_dst2, b2, src, dst, 1, OUT)
        return out

    def _L2_gnn_ref(h, src, dst, W_pre, b_pre, W1, b1, W2, b2, gamma, beta):
        import jax, jax.numpy as jnp
        import numpy as np
        N_NODES = 50000
        N_EDGES = 9375
        D = 128
        EPS = 1e-05

        def layer_norm(x, gamma, beta):
            mu = jnp.mean(x, axis=-1, keepdims=True)
            var = jnp.mean(jnp.square(x - mu), axis=-1, keepdims=True)
            return (x - mu) * jax.lax.rsqrt(var + EPS) * gamma + beta
        h = h @ W_pre + b_pre
        agg = jax.ops.segment_sum(h[src], dst, num_segments=N_NODES)
        h_new = jax.nn.relu(jax.nn.relu(agg @ W1 + b1) @ W2 + b2)
        return layer_norm(h + h_new, gamma, beta)

    def _L3_gnn_ref(h, e, W_node, b_node, W_e1, b_e1, W_e2, b_e2, W_fc1, b_fc1, W_fc2, b_fc2, src, dst):
        import jax, jax.numpy as jnp
        import numpy as np
        LOG2 = float(np.log(2.0))

        def ssp(x):
            return jax.nn.softplus(x) - LOG2

        def linear(x, W, b):
            return x @ W.T + b
        N = h.shape[0]
        hn = linear(h, W_node, b_node)
        ef = ssp(linear(e, W_e1, b_e1))
        ef = ssp(linear(ef, W_e2, b_e2))
        m = hn[src] * ef
        agg = jax.ops.segment_sum(m, dst, num_segments=N)
        out = ssp(linear(agg, W_fc1, b_fc1))
        out = linear(out, W_fc2, b_fc2)
        return out
    edge_index = jnp.stack([src, dst])
    x = _layernorm(x + _L0_gnn_ref(x, edge_index, L0_gnn_hyperedge_weight, L0_gnn_W1, L0_gnn_b1, L0_gnn_gamma, L0_gnn_beta, L0_gnn_W2, L0_gnn_b2), axis=-1)
    x = _layernorm(x + _L1_gnn_ref(x, edge_index, L1_gnn_W1, L1_gnn_att_src1, L1_gnn_att_dst1, L1_gnn_b1, L1_gnn_W2, L1_gnn_att_src2, L1_gnn_att_dst2, L1_gnn_b2), axis=-1)
    x = _layernorm(x + _L2_gnn_ref(x, src, dst, L2_gnn_W_pre, L2_gnn_b_pre, L2_gnn_W1, L2_gnn_b1, L2_gnn_W2, L2_gnn_b2, L2_gnn_gamma, L2_gnn_beta), axis=-1)
    x = _layernorm(x + _L3_gnn_ref(x, edge_attr_128, L3_gnn_W_node, L3_gnn_b_node, L3_gnn_W_e1, L3_gnn_b_e1, L3_gnn_W_e2, L3_gnn_b_e2, L3_gnn_W_fc1, L3_gnn_b_fc1, L3_gnn_W_fc2, L3_gnn_b_fc2, src, dst), axis=-1)
    return x

_drawn_inputs = setup_inputs


def setup_inputs(seed=0):
    import zlib

    import numpy as np

    out = dict(_drawn_inputs(seed))
    spreads = {'L0_gnn_hyperedge_weight': (1.0, 0.2),
     'L0_gnn_b1': (0.0, 2.0),
     'L0_gnn_gamma': (1.0, 0.2),
     'L0_gnn_beta': (0.0, 0.385),
     'L0_gnn_b2': (0.0, 0.1),
     'L1_gnn_b1': (0.0, 0.1),
     'L1_gnn_b2': (0.0, 0.1),
     'L2_gnn_gamma': (1.0, 0.2),
     'L2_gnn_beta': (0.0, 0.1)}
    factors = {'edge_attr_128': 8.0,
     'L1_gnn_att_src1': 6.504,
     'L1_gnn_att_dst1': 200.0,
     'L1_gnn_att_src2': 8.0,
     'L1_gnn_att_dst2': 200.0,
     'L2_gnn_b1': 3.238,
     'L3_gnn_W_node': 8.0,
     'L3_gnn_b_node': 8.0,
     'L3_gnn_W_e1': 8.0,
     'L3_gnn_b_e1': 59.991,
     'L3_gnn_W_e2': 8.0,
     'L3_gnn_b_e2': 200.0,
     'L3_gnn_W_fc1': 8.0,
     'L3_gnn_b_fc1': 3.47,
     'L3_gnn_W_fc2': 3.564}
    for name, (base, spread) in spreads.items():
        noise = np.random.default_rng([zlib.crc32(name.encode()), seed]).standard_normal(out[name].shape)
        drawn = base * np.exp(spread * noise) if base else spread * noise
        out[name] = jnp.asarray(drawn.astype(out[name].dtype))
    for name, factor in factors.items():
        out[name] = (out[name] * factor).astype(out[name].dtype)
    return out
```

```python
from contextlib import ExitStack

import concourse.bass as bass
from concourse import mybir

F32 = mybir.dt.float32
I32 = mybir.dt.int32
ALU = mybir.AluOpType
ACT = mybir.ActivationFunctionType
AX_X = mybir.AxisListType.X

P = 128
N_NODES = 50000
N_HYPER = 10000
C = 128
HEADS = 4
HID = 64
HC = HEADS * HID
TILES_PER_GROUP = U = 4
SLOTS = 2
NP_ = 50176
NODE_GROUPS = NP_ // (P * U)
EDGE_TILES = 200
EDGE_GROUPS = EDGE_TILES // U
EP = EDGE_TILES * P
SORT_F = 256
SORT_N = P * SORT_F
HALF_T = EDGE_TILES // 2
H2W = 132
SKIP = 1000000.0
NEG = -1.0e30
SLOPE = 0.2
EPS = 1e-5
LOG2 = 0.6931471805599453
SPLIT = 17664
ENC_NEG = float(0x8000 + SPLIT)
ENC_ADD = float(0x80 - SPLIT)


def done(q):
    return q + 1 + SLOTS


def behind(q):
    return q + SLOTS


def free(q):
    return q + 1


class Phase:

    def __init__(self, nc, name):
        self.nc, self.name, self.ctx, self.own_sems = nc, name, ExitStack(), []

    def __enter__(self):
        self.ctx.__enter__()
        return self

    def __exit__(self, *a):
        self.ctx.__exit__(*a)
        self.nc.clear_and_free_semaphores(self.own_sems)
        self.nc.all_engine_barrier()

    def sb(self, name, shape, dt=F32):
        return self.ctx.enter_context(self.nc.sbuf_tensor(f"{self.name}_{name}", shape, dt))

    def ps(self, name, shape):
        return self.ctx.enter_context(self.nc.psum_tensor(f"{self.name}_{name}", shape, F32))

    def sem(self, name):
        self.own_sems.append(self.nc.alloc_semaphore(f"{self.name}_{name}"))
        return self.own_sems[-1]

    def sems(self, name, n=SLOTS):
        return [self.sem(f"{name}{i}") for i in range(n)]

    def block(self):
        return self.ctx.enter_context(self.nc.Block())


def groups_of(table, g0=0):
    return table.rearrange("(g u p) w -> g p u w", u=U, p=P)


def prime_stores(f, stored, n, ident):
    spare = f.sb("spare", [1, SLOTS, 16])
    def issue(eng):
        for s in range(SLOTS):
            eng.dma_start(spare[:, s, :], ident[0:1, 0:16]).then_inc(stored[s], 16 * n)
    return issue


def gather(pool, out, table, index):
    return pool.indirect_dma_start(out, None, table, bass.IndirectOffsetOnAxis(ap=index, axis=0))


def scatter(pool, table, index, rows, values):
    return pool.indirect_dma_start(table, bass.IndirectOffsetOnAxis(ap=index, axis=0), values, None,
                                   bounds_check=rows - 1, oob_is_err=False)


def sort_phase(nc, T, A):
    with Phase(nc, "sort") as f:
        raw = f.sb("raw", [P, 3, SORT_F], I32)
        keyf = f.sb("keyf", [P, 2, SORT_F])
        offs = f.sb("offs", [P, 2, SORT_F])
        top = f.sb("top", [P, 2, SORT_F], I32)
        words = f.sb("words", [P, 2, 3 * SORT_F])
        signs = f.sb("signs", [P, 8, SORT_F])
        signs_t = f.sb("signs_t", [P, 7, P])
        ident = f.sb("ident", [P, P])
        turned = f.ps("turned", [P, 2, 512])
        loaded, stage, turn, out = f.sem("loaded"), f.sem("stage"), f.sem("turn"), f.sem("out")
        block = f.block()
        turns = []

        @block.sync
        def _(sp):
            sp.dma_start(raw[:, 0, :], A["dst"]).then_inc(loaded, 16)
            sp.dma_start(raw[:, 1, :], A["src"]).then_inc(loaded, 16)
            sp.dma_start(raw[:, 2, :], A["edge_no"]).then_inc(loaded, 16)
            sp.dma_start(signs[:], A["sort_signs"]).then_inc(loaded, 16)
            sp.dma_start(signs_t[:], A["sort_signs_t"]).then_inc(loaded, 16)
            sp.dma_start(ident[:], A["ident"]).then_inc(loaded, 16)

        @block.vector
        def _(dve):
            n = 0

            def step(*ins):
                nonlocal n
                for x in ins:
                    x.then_inc(stage, 1)
                n += len(ins)
                dve.wait_ge(stage, n)

            dve.wait_ge(loaded, 96)
            step(dve.tensor_copy(keyf[:], raw[:, 0:2, :]))
            step(dve.tensor_scalar(offs[:], keyf[:], float(SPLIT), ENC_NEG, ALU.is_lt, ALU.mult))
            step(dve.scalar_tensor_tensor(top[:], keyf[:], ENC_ADD, offs[:], ALU.add, ALU.add))
            w0 = words[:, 0, :].bitcast(I32).rearrange("p (a f) -> p a f", a=3)
            step(*[dve.scalar_tensor_tensor(w0[:, a, :], top[:, k, :], 16, raw[:, pay, :],
                                            ALU.logical_shift_left, ALU.bitwise_or)
                   for a, k, pay in ((0, 0, 2), (1, 0, 1), (2, 1, 0))])
            cur = 0

            def compare(d):
                nonlocal cur
                a = words[:, cur, :].rearrange("p (g t d) -> p g t d", t=2, d=d)
                b = words[:, 1 - cur, :].rearrange("p (g t d) -> p g t d", t=2, d=d)
                step(dve.tensor_tensor(b[:, :, 0, :], a[:, :, 0, :], a[:, :, 1, :], ALU.min),
                     dve.tensor_tensor(b[:, :, 1, :], a[:, :, 0, :], a[:, :, 1, :], ALU.max))
                cur = 1 - cur

            turn_no = 0

            def turn_over(mask):
                nonlocal turn_no, cur
                turns.append((cur, n))
                turn_no += 1
                dve.wait_ge(turn, turn_no)
                new = words[:, 1 - cur, :]
                if mask is None:
                    step(dve.tensor_copy(new[:, 0:512], turned[:, 0, :]),
                         dve.tensor_copy(new[:, 512:768], turned[:, 1, 0:256]))
                else:
                    m = mask.unsqueeze(1)
                    step(dve.tensor_tensor(new[:, 0:512].rearrange("p (a q) -> p a q", q=P),
                                           turned[:, 0, :].rearrange("p (a q) -> p a q", q=P),
                                           m.to_broadcast([P, 4, P]), ALU.mult),
                         dve.tensor_tensor(new[:, 512:768].rearrange("p (a q) -> p a q", q=P),
                                           turned[:, 1, 0:256].rearrange("p (a q) -> p a q", q=P),
                                           m.to_broadcast([P, 2, P]), ALU.mult))
                cur = 1 - cur

            for level in range(1, 9):
                a = words[:, cur, :].rearrange("p (a f) -> p a f", a=3)
                b = words[:, 1 - cur, :].rearrange("p (a f) -> p a f", a=3)
                step(dve.tensor_tensor(b, a, signs[:, level - 1, :].unsqueeze(1).to_broadcast([P, 3, SORT_F]),
                                       ALU.mult))
                cur = 1 - cur
                for m in reversed(range(level)):
                    compare(1 << m)
            for level in range(9, 16):
                turn_over(signs_t[:, level - 9, :])
                for m in reversed(range(level - 8)):
                    compare(1 << m)
                turn_over(None)
                for m in reversed(range(8)):
                    compare(1 << m)
            f.final, f.final_n = cur, n

        @block.tensor
        def _(pe):
            for buf, n in turns:
                pe.wait_ge(stage, n)
                for b in range(6):
                    t = pe.transpose(turned[:, b // 4, (b % 4) * P:(b % 4 + 1) * P],
                                     words[:, buf, b * P:(b + 1) * P], ident[:])
                t.then_inc(turn, 1)

        @block.scalar
        def _(act):
            act.wait_ge(stage, f.final_n)
            act.dma_start(T["sorted"], words[:, f.final, :]).then_inc(out, 16)
            act.wait_ge(out, 16)


def constants():
    import numpy as np
    j = np.arange(SORT_N).reshape(P, SORT_F)

    def sgn(k):
        return np.where((j >> k) & 1, -1.0, 1.0) if k else np.ones(j.shape)

    full = [sgn(k) * sgn(k - 1) if k > 1 else sgn(1) for k in range(1, 16)]
    signs = np.stack(full[:8], 1).astype(np.float32)
    signs_t = np.broadcast_to(np.stack([m[:, 0] for m in full[8:]])[None], (P, 7, P)).astype(np.float32)
    return {
        "edge_no": j.astype(np.int32),
        "sort_signs": signs,
        "sort_signs_t": np.ascontiguousarray(signs_t),
        "ident": np.eye(P, dtype=np.float32),
        "is_last": (j % P == P - 1).astype(np.float32),
        "later": (np.arange(EDGE_TILES).reshape(2, HALF_T).T[:, :, None] > np.arange(EDGE_TILES)).astype(np.float32),
    }



KD, SF, KS, SM = range(4)
SRC, SCD, SCE, PERM, DST, HYP, SCS, NOD, SRCO = range(9)


class Tables:

    def __init__(self, nc, ctx, ident_dram):
        self.ident_dram = ident_dram

        def sb(name, shape, dt=F32):
            return ctx.enter_context(nc.sbuf_tensor(name, shape, dt))

        self.colf = sb("colf", [P, 4, EDGE_TILES])
        self.coli = sb("coli", [P, 9, EDGE_TILES], I32)
        self.joins = sb("joins", [HALF_T, 2, 2, EDGE_TILES])
        self.ident = sb("identity", [P, P])
        self.hw = sb("hw_col", [P, EDGE_TILES])
        self.ws = sb("w_src", [P, EDGE_TILES, HEADS])
        self.wd = sb("w_self", [P, EDGE_TILES, HEADS])
        self.wt = sb("w_total", [P, EDGE_TILES, HEADS])
        self.affine = sb("affine", [P, 2, C])
        self.affine_sums = sb("affine_sums", [P, 2, U * C])
        self.W1 = sb("W1", [P, HC])
        self.WA = sb("WA", [P, 2 * HEADS])
        self.W2x = sb("W2x", [P, 2, H2W])
        self.b1col = sb("b1col", [P, 2])
        self.b0 = sb("b0", [P, C])
        self.b2 = sb("b2", [P, C])
        self.c2 = sb("c2", [P, C])
        self.c3 = sb("c3", [P, C])


def index_phase(nc, T, A, S):
    with Phase(nc, "index") as f:
        words = f.sb("words", [P, 3, SORT_F], I32)
        bits = f.sb("bits", [P, 3, 2, SORT_F], I32)
        key = f.sb("key", [P, 3, SORT_F])
        off = f.sb("off", [P, 3, SORT_F])
        prv = f.sb("prv", [P, 2, SORT_F])
        nxt = f.sb("nxt", [P, 2, SORT_F])
        new = f.sb("new", [P, 2, SORT_F])
        rep = f.sb("rep", [P, 2, SORT_F])
        tmp = f.sb("tmp", [P, 2, SORT_F])
        is_last = f.sb("is_last", [P, SORT_F])
        arr = f.sb("arr", [P, 12, SORT_F])
        guard = f.sb("guard", [1, 2])
        zeros = f.sb("zeros", [80, 2000])
        later = f.sb("later", [HALF_T, 2, EDGE_TILES])
        last_row = f.sb("last_row", [HALF_T, 2, EDGE_TILES])
        first_col = f.sb("first_col", [HALF_T, 2, 2])
        eq = f.sb("eq", [HALF_T, 2, 2, EDGE_TILES])
        psT = f.ps("turned", [P, 4, 512])
        filled, loaded, stage, kept, back, tile_keys, turned = (f.sem(n) for n in (
            "filled", "loaded", "stage", "kept", "back", "tile_keys", "turned"))
        block = f.block()
        marks = {}

        @block.vector
        def _(dve):
            n = 0

            def step(*ins):
                nonlocal n
                for x in ins:
                    x.then_inc(stage, 1)
                n += len(ins)
                dve.wait_ge(stage, n)

            step(dve.memset(guard[:], -1.0), dve.memset(zeros[:], 0.0))
            marks["guard"] = n
            dve.wait_ge(loaded, 16 * 5)
            step(dve.tensor_scalar(bits[:, :, 0, :], words[:], 16, None, ALU.logical_shift_right),
                 dve.tensor_scalar(bits[:, :, 1, :], words[:], 0xFFFF, None, ALU.bitwise_and))
            step(dve.tensor_scalar(off[:], bits[:, :, 0, :], 32768.0, ENC_NEG, ALU.is_ge, ALU.mult))
            step(dve.scalar_tensor_tensor(key[:], bits[:, :, 0, :], -ENC_ADD, off[:], ALU.add, ALU.subtract))
            marks["key"] = n
            dve.wait_ge(back, 16 * 4)
            kk = key[:, 1:3, :]
            step(dve.tensor_tensor(new[:], kk, prv[:], ALU.not_equal),
                 dve.tensor_tensor(rep[:], kk, nxt[:], ALU.not_equal))
            step(dve.tensor_tensor(rep[:], rep[:], is_last[:].unsqueeze(1).to_broadcast([P, 2, SORT_F]), ALU.max))
            def tiles(x, o):
                return x[:, o, :].rearrange("p (h e) -> p h e", h=2)
            step(*[dve.tensor_tensor(tiles(tmp, o), tiles(key, o + 1),
                                     tiles(prv, o)[:, :, 0:1].to_broadcast([P, 2, P]), ALU.not_equal)
                   for o in range(2)])
            step(dve.tensor_tensor(rep[:], rep[:], tmp[:], ALU.mult))
            step(dve.tensor_copy(arr[:, 0, :], key[:, 1, :]),
                 dve.tensor_copy(arr[:, 1, :], new[:, 0, :]),
                 dve.tensor_copy(arr[:, 2, :], key[:, 2, :]),
                 dve.scalar_tensor_tensor(arr[:, 3, :], key[:, 2, :], float(N_NODES), rep[:, 1, :],
                                          ALU.is_lt, ALU.mult),
                 dve.tensor_copy(arr[:, 4, :], bits[:, 1, 1, :]),
                 dve.scalar_tensor_tensor(arr[:, 5, :], key[:, 1, :], -SKIP, rep[:, 0, :], ALU.add, ALU.mult),
                 dve.scalar_tensor_tensor(tmp[:, 0, :], key[:, 1, :], float(N_HYPER), rep[:, 0, :],
                                          ALU.is_lt, ALU.mult),
                 dve.tensor_copy(arr[:, 7, :], bits[:, 0, 1, :]),
                 dve.tensor_copy(arr[:, 8, :], key[:, 1, :]),
                 dve.tensor_scalar(arr[:, 9, :], bits[:, 2, 1, :], float(N_HYPER - 1), None, ALU.min),
                 dve.scalar_tensor_tensor(arr[:, 10, :], key[:, 2, :], -SKIP, rep[:, 1, :], ALU.add, ALU.mult),
                 dve.tensor_copy(arr[:, 11, :], key[:, 2, :]))
            step(dve.scalar_tensor_tensor(arr[:, 6, :], key[:, 1, :], -SKIP, tmp[:, 0, :], ALU.add, ALU.mult))
            step(*[dve.tensor_scalar(arr[:, a, :], arr[:, a, :], SKIP, None, ALU.add) for a in (5, 6, 10)])
            marks["arr"] = n
            dve.wait_ge(tile_keys, 16 * 4)
            for o in range(2):
                step(*[dve.tensor_scalar(eq[:, o, c, :], last_row[:, o, :], first_col[:, o, c:c + 1], None,
                                         ALU.is_equal) for c in range(2)])
            step(*[dve.tensor_tensor(S.joins[:, o, :, :], eq[:, o, :, :], later[:], ALU.mult)
                   for o in range(2)])
            for a in range(12):
                dve.wait_ge(turned, a + 1)
                col = S.colf[:, a, :] if a < 4 else S.coli[:, a - 4, :]
                dve.tensor_copy(col.rearrange("e (p h) -> e h p", h=2),
                                psT[:, a % 4, 0:2 * P].rearrange("e (h p) -> e h p", h=2)[:, :, 0:HALF_T]
                                ).then_inc(stage, 1)
            marks["columns"] = n

        @block.tensor
        def _(pe):
            pe.wait_ge(stage, marks["arr"])
            for a in range(12):
                if a >= 4:
                    pe.wait_ge(stage, marks["columns"] + a - 3)
                for h in range(2):
                    t = pe.transpose(psT[:, a % 4, h * P:(h + 1) * P], arr[:, a, h * P:(h + 1) * P], S.ident[:])
                t.then_inc(turned, 1)

        @block.sync
        def _(sp):
            sp.dma_start(words[:], T["sorted"].bitcast(I32).rearrange("p (a f) -> p a f", a=3)).then_inc(loaded, 16)
            sp.dma_start(is_last[:], A["is_last"]).then_inc(loaded, 16)
            sp.dma_start(later[:], A["later"]).then_inc(loaded, 16)
            sp.dma_start(S.coli[:, SRCO, :], A["src_cols"]).then_inc(loaded, 16)
            sp.dma_start(S.ident[:], A["ident"]).then_inc(loaded, 16)
            sp.wait_ge(stage, marks["guard"])
            e_rows = T["E"].rearrange("(p r) c -> p (r c)", p=80)
            for k in range(N_HYPER * C // (80 * 2000)):
                sp.dma_start(e_rows[:, k * 2000:(k + 1) * 2000], zeros[:]).then_inc(filled, 16)
            for o in range(2):
                sp.dma_start(T["keys"][o:o + 1, 0:1], guard[:, 0:1]).then_inc(kept, 16)
                sp.dma_start(T["keys"][o:o + 1, SORT_N + 1:SORT_N + 2], guard[:, 1:2]).then_inc(kept, 16)
            sp.wait_ge(stage, marks["key"])
            for o in range(2):
                sp.dma_start(T["keys"][o, 1:SORT_N + 1].rearrange("(p f) -> p f", p=P),
                             key[:, o + 1, :]).then_inc(kept, 16)
                with nc.allow_non_contiguous_dma(reason="two keys per partition"):
                    for h in range(2):
                        sp.dma_start(T["last"][o].rearrange("(p h) -> p h", h=2)[:, h:h + 1],
                                     key[:, o + 1, h * P + P - 1:h * P + P]).then_inc(kept, 16)
            sp.wait_ge(kept, 16 * 10)
            sp.wait_ge(filled, N_HYPER * C // (80 * 2000) * 16)
            for o in range(2):
                sp.dma_start(prv[:, o, :], T["keys"][o, 0:SORT_N].rearrange("(p f) -> p f", p=P)
                             ).then_inc(back, 16)
                sp.dma_start(nxt[:, o, :], T["keys"][o, 2:SORT_N + 2].rearrange("(p f) -> p f", p=P)
                             ).then_inc(back, 16)
            for o in range(2):
                sp.dma_start(last_row[:, o, :], T["last"][o:o + 1, 0:EDGE_TILES].to_broadcast([HALF_T, EDGE_TILES])
                             ).then_inc(tile_keys, 16)
                with nc.allow_non_contiguous_dma(reason="first key of each tile"):
                    sp.dma_start(first_col[:, o, :],
                                 T["keys"][o, 1:1 + EDGE_TILES * P].rearrange("(c p e) -> p c e", p=HALF_T, e=P)
                                 [:, :, 0]).then_inc(tile_keys, 16)


def hw_phase(nc, T, A, S):
    with Phase(nc, "hw") as f:
        slot = f.sb("slot", [P, SLOTS, U], I32)
        got = f.sb("got", [P, SLOTS, U])
        picked, copied, tick = f.sem("picked"), f.sem("copied"), f.sem("tick")
        gathered = f.sems("gathered")
        block = f.block()

        @block.gpsimd
        def _(pool):
            pool.sem_inc(copied, SLOTS)
            with pool.Fori(0, EDGE_GROUPS // SLOTS) as i:
                for s in range(SLOTS):
                    q = i * SLOTS + s
                    pool.wait_ge(copied, free(q))
                    pool.tensor_copy(slot[:, s], S.coli[:, HYP, bass.ds(q * U, U)]).then_inc(picked, 1)
                    pool.wait_ge(picked, q + 1)
                    pool.sem_inc(tick, 1)
                    for u in range(U):
                        gather(pool, got[:, s, u:u + 1], A["hw"], slot[:, s, u:u + 1]).then_inc(gathered[s], 16)

        @block.vector
        def _(dve):
            with dve.Fori(0, EDGE_GROUPS // SLOTS) as i:
                for s in range(SLOTS):
                    q = i * SLOTS + s
                    dve.wait_ge(gathered[s], (i + 1) * (16 * U))
                    dve.tensor_copy(S.hw[:, bass.ds(q * U, U)], got[:, s]).then_inc(copied, 1)



def sum_pass(nc, T, S, name, order, table, idx, w, out, extra=None):
    key = (KD, KS)[order]
    with Phase(nc, name) as f:
        slot = f.sb("slot", [P, SLOTS, U], I32)
        v = f.sb("v", [P, SLOTS, U, w])
        krow = f.sb("krow", [P, SLOTS, U * P])
        same = f.sb("same", [P, SLOTS, U, P])
        sums = f.sb("sums", [P, SLOTS, U, w])
        acc = [f.ps(f"acc{s}", [P, U, 256]) for s in range(SLOTS)]
        picked, tick, ones_set = f.sem("picked"), f.sem("tick"), f.sem("ones_set")
        matched, summed, copied = f.sem("matched"), f.sem("summed"), f.sem("copied")
        gathered, keyed, stored = f.sems("gathered"), f.sems("keyed"), f.sems("stored")
        primed = prime_stores(f, stored, 1, S.ident_dram)
        block = f.block()
        wt = table.shape[1]
        iters = EDGE_GROUPS // SLOTS
        out_g = groups_of(out)

        @block.sync
        def _(sp):
            for m in (matched, summed, copied):
                sp.sem_inc(m, SLOTS)
            with sp.Fori(0, iters) as i:
                for s in range(SLOTS):
                    q = i * SLOTS + s
                    sp.wait_ge(matched, free(q))
                    sp.dma_start(krow[:, s], T["keys"][order:order + 1, bass.ds(q * (U * P) + 1, U * P)]
                                 .to_broadcast([P, U * P])).then_inc(keyed[s], 16)
            for s in range(SLOTS):
                sp.wait_ge(stored[s], 16 * (iters + 1))

        @block.gpsimd
        def _(pool):
            with pool.Fori(0, iters) as i:
                for s in range(SLOTS):
                    q = i * SLOTS + s
                    pool.wait_ge(summed, free(q))
                    pool.tensor_copy(slot[:, s], S.coli[:, idx, bass.ds(q * U, U)]).then_inc(picked, 1)
                    pool.wait_ge(picked, q + 1)
                    pool.sem_inc(tick, 1)
                    for u in range(U):
                        gather(pool, v[:, s, u, 0:wt], table, slot[:, s, u:u + 1]).then_inc(gathered[s], 16)

        @block.vector
        def _(dve):
            if extra == "ones":
                dve.memset(v[:, :, :, wt:wt + 1], 1.0).then_inc(ones_set, 1)
            with dve.Fori(0, iters) as i:
                for s in range(SLOTS):
                    q = i * SLOTS + s
                    dve.wait_ge(keyed[s], (i + 1) * 16)
                    dve.wait_ge(summed, free(q))
                    if extra == "hw":
                        dve.tensor_copy(v[:, s, :, wt], S.hw[:, bass.ds(q * U, U)])
                    dve.tensor_tensor(same[:, s], krow[:, s].rearrange("p (u e) -> p u e", u=U),
                                      S.colf[:, key, bass.ds(q * U, U)].unsqueeze(2).to_broadcast([P, U, P]),
                                      ALU.is_equal).then_inc(matched, 1)

        @block.tensor
        def _(pe):
            if extra == "ones":
                pe.wait_ge(ones_set, 1)
            with pe.Fori(0, iters) as i:
                for s in range(SLOTS):
                    q = i * SLOTS + s
                    pe.wait_ge(matched, done(q))
                    pe.wait_ge(gathered[s], (i + 1) * (16 * U))
                    pe.wait_ge(copied, free(q))
                    for u in range(U):
                        m = pe.matmul(acc[s][:, u, 0:w], same[:, s, u, :], v[:, s, u, :], start=True, stop=True)
                    m.then_inc(summed, 1)

        @block.scalar
        def _(act):
            primed(act)
            with act.Fori(0, iters) as i:
                for s in range(SLOTS):
                    q = i * SLOTS + s
                    act.wait_ge(summed, done(q))
                    act.wait_ge(stored[s], (i + 1) * 16)
                    act.activation(sums[:, s], acc[s][:, :, 0:w], ACT.Copy).then_inc(copied, 1)
                    act.wait_ge(copied, done(q))
                    act.dma_start(out_g[q], sums[:, s]).then_inc(stored[s], 16)


def fix_pass(nc, S, name, order, out, w):
    with Phase(nc, name) as f:
        first = f.sb("first", [HALF_T, 2, w])
        last = f.sb("last", [HALF_T, 2, w])
        full = f.sb("full", [HALF_T, 2, w])
        acc = f.ps("acc", [P, 2, 512])
        loaded, carried, added, stored = (f.sem(n) for n in ("loaded", "carried", "added", "stored"))
        block = f.block()
        rows = out.rearrange("(c p e) w -> p c e w", p=HALF_T, e=P)

        @block.sync
        def _(sp):
            sp.dma_start(first[:], rows[:, :, 0, :]).then_inc(loaded, 16)
            sp.dma_start(last[:], rows[:, :, P - 1, :]).then_inc(loaded, 16)
            sp.wait_ge(added, 1)
            sp.dma_start(rows[:, :, P - 1, :], full[:]).then_inc(stored, 16)
            sp.wait_ge(stored, 16)

        @block.tensor
        def _(pe):
            pe.wait_ge(loaded, 32)
            for c in range(2):
                for later in range(2):
                    m = pe.matmul(acc[0:HALF_T, c, 0:w], S.joins[:, order, later, c * HALF_T:(c + 1) * HALF_T],
                                  first[:, later, :], start=(later == 0), stop=(later == 1))
            m.then_inc(carried, 1)

        @block.vector
        def _(dve):
            dve.wait_ge(carried, 1)
            dve.tensor_tensor(full[:], last[:], acc[0:HALF_T, :, 0:w], ALU.add).then_inc(added, 1)



def bc_rows(row, n=U):
    return row.unsqueeze(1).to_broadcast([P, n, C])


class Rows:

    def __init__(self, f, S, dense, stores, groups=None):
        self.f, self.S, self.dense = f, S, dense
        self.iters = (groups or (NODE_GROUPS if dense else EDGE_GROUPS)) // SLOTS
        self.loaded = f.sems("loaded")
        self.gathered = f.sems("gathered")
        self.stored = f.sems("stored")
        self.used = f.sem("used")
        self.ready = f.sem("ready")
        self.picked, self.tick = f.sem("picked"), f.sem("tick")
        self.weights = f.sem("weights")
        self.stores = stores
        self.prime_stores = prime_stores(f, self.stored, stores, S.ident_dram)
        self.slot = f.sb("slot", [P, SLOTS, U], I32)
        self.slot_out = f.sb("slot_out", [P, SLOTS, U], I32)

    def prime(self, sp, sems):
        for m in (self.used, self.ready, *sems):
            sp.sem_inc(m, SLOTS)

    def load(self, sp, pairs):
        with sp.Fori(0, self.iters) as i:
            for s in range(SLOTS):
                q = i * SLOTS + s
                sp.wait_ge(self.used, free(q))
                for buf, table in pairs:
                    sp.dma_start(buf[:, s], table[q]).then_inc(self.loaded[s], 16)

    def finish(self, sp):
        for s in range(SLOTS):
            sp.wait_ge(self.stored[s], 16 * self.stores * (self.iters + 1))

    def pool_loop(self, pool, gathers=(), stores=(), scatters=()):
        S = self.S
        self.prime_stores(pool)
        with pool.Fori(0, self.iters) as i:
            for s in range(SLOTS):
                q = i * SLOTS + s
                for buf, table, idx, buf_used in gathers:
                    pool.wait_ge(buf_used, free(q))
                    pool.tensor_copy(self.slot[:, s], S.coli[:, idx, bass.ds(q * U, U)]).then_inc(self.picked, 1)
                    pool.wait_ge(self.picked, i * (2 * SLOTS) + (s + 1) if scatters else q + 1)
                    pool.sem_inc(self.tick, 1)
                    for u in range(U):
                        gather(pool, buf[:, s, u, :], table, self.slot[:, s, u:u + 1]
                               ).then_inc(self.gathered[s], 16)
            for s in range(SLOTS):
                q = i * SLOTS + s
                if stores:
                    pool.wait_ge(self.ready, done(q))
                    pool.sem_inc(self.tick, 1)
                    for buf, table in stores:
                        pool.dma_start(table[q], buf[:, s]).then_inc(self.stored[s], 16)
                for buf, table, idx, rows in scatters:
                    pool.wait_ge(self.stored[s], (i + 1) * (16 * U))
                    pool.tensor_copy(self.slot_out[:, s], S.coli[:, idx, bass.ds(q * U, U)]
                                     ).then_inc(self.picked, 1)
                    pool.wait_ge(self.picked, (i * (2 * SLOTS) + (SLOTS + s + 1)) if gathers else q + 1)
                    pool.sem_inc(self.tick, 1)
                    pool.wait_ge(self.ready, done(q))
                    pool.sem_inc(self.tick, 1)
                    for u in range(U):
                        scatter(pool, table, self.slot_out[:, s, u:u + 1], rows, buf[:, s, u, :]
                                ).then_inc(self.stored[s], 16)

    def wait_loads(self, eng, i, s, plain, gathers=0):
        if plain:
            eng.wait_ge(self.loaded[s], (i + 1) * (16 * plain))
        if gathers:
            eng.wait_ge(self.gathered[s], (i + 1) * (16 * U * gathers))

    def out_free(self, eng, i, s):
        eng.wait_ge(self.stored[s], (i + 1) * (16 * self.stores))


class LayerNorm:

    def __init__(self, f, name=""):
        self.stats = f.sb(f"stats{name}", [P, SLOTS, U, 6])
        self.mv = f.sb(f"mv{name}", [P, SLOTS, U, 2])
        self.std = f.sb(f"std{name}", [P, SLOTS, U])
        self.rstd = f.sb(f"rstd{name}", [P, SLOTS, U])
        self.eps = f.sb(f"eps{name}", [P, 1])
        self.z_ready, self.stats_ready, self.mv_ready, self.std_ready, self.rstd_ready, self.eps_set = (
            f.sem(f"{n}{name}") for n in ("z_ready", "stats_ready", "mv_ready", "std_ready", "rstd_ready",
                                          "eps_set"))
        self.sems = [self.z_ready, self.stats_ready, self.mv_ready, self.std_ready, self.rstd_ready]

    def setup(self, dve):
        dve.memset(self.eps[:], EPS).then_inc(self.eps_set, 1)

    def moments(self, dve, i, z, tick):
        for s in range(SLOTS):
            q = i * SLOTS + s
            dve.wait_ge(self.z_ready, done(q))
            for u in range(U):
                b = dve.bn_stats(self.stats[:, s, u, :], z[:, s, u, :])
            b.then_inc(self.stats_ready, 1)
        for s in range(SLOTS):
            q = i * SLOTS + s
            dve.wait_ge(self.stats_ready, done(q))
            dve.sem_inc(tick, 1)
            for u in range(U):
                b = dve.bn_aggr(self.mv[:, s, u, :], self.stats[:, s, u, :])
            b.then_inc(self.mv_ready, 1)

    def deviation(self, act, i):
        for s in range(SLOTS):
            q = i * SLOTS + s
            act.wait_ge(self.mv_ready, done(q))
            act.activation(self.std[:, s], self.mv[:, s, :, 1], ACT.Sqrt, bias=self.eps[:]
                           ).then_inc(self.std_ready, 1)

    def scale(self, dve, i, z, out, ready, out_free):
        for s in range(SLOTS):
            q = i * SLOTS + s
            dve.wait_ge(self.std_ready, done(q))
            dve.reciprocal(self.rstd[:, s], self.std[:, s]).then_inc(self.rstd_ready, 1)
        for s in range(SLOTS):
            q = i * SLOTS + s
            if out_free:
                out_free(dve, i, s)
            dve.wait_ge(self.rstd_ready, done(q))
            for u in range(U):
                b = dve.tensor_scalar(out[:, s, u, :], z[:, s, u, :], self.mv[:, s, u, 0:1],
                                      self.rstd[:, s, u:u + 1], ALU.subtract, ALU.mult)
            b.then_inc(ready, 1)


def hyper_rows(nc, T, S, name, raw, out, affine):
    with Phase(nc, name) as f:
        r = Rows(f, S, dense=False, stores=U)
        rows = f.sb("rows", [P, SLOTS, U, C + 1])
        inv = f.sb("inv", [P, SLOTS, U, 1])
        mean = f.sb("mean", [P, SLOTS, U, C])
        inverted, scaled, shifted = f.sem("inverted"), f.sem("scaled"), f.sem("shifted")
        block = f.block()

        @block.sync
        def _(sp):
            r.prime(sp, (inverted, scaled, shifted))
            r.load(sp, [(rows, groups_of(raw))])
            r.finish(sp)

        @block.gpsimd
        def _(pool):
            r.pool_loop(pool, scatters=[(mean, out, SCE, N_HYPER)])

        @block.vector
        def _(dve):
            with dve.Fori(0, r.iters) as i:
                for s in range(SLOTS):
                    dve.wait_ge(r.ready, free(i * SLOTS + s))
                for s in range(SLOTS):
                    q = i * SLOTS + s
                    r.wait_loads(dve, i, s, 1)
                    dve.reciprocal(inv[:, s], rows[:, s, :, C:C + 1]).then_inc(inverted, 1)
                for s in range(SLOTS):
                    q = i * SLOTS + s
                    dve.wait_ge(inverted, done(q))
                    r.out_free(dve, i, s)
                    m = dve.tensor_tensor(mean[:, s], rows[:, s, :, 0:C], inv[:, s].to_broadcast([P, U, C]),
                                          ALU.mult)
                    m.then_inc(r.used, 1)
                    if affine:
                        dve.wait_ge(r.used, done(q))
                        dve.tensor_tensor(mean[:, s], mean[:, s], bc_rows(S.affine[:, 0, :]), ALU.mult
                                          ).then_inc(scaled, 1)
                        dve.wait_ge(scaled, done(q))
                        dve.tensor_tensor(mean[:, s], mean[:, s], bc_rows(S.affine[:, 1, :]), ALU.add
                                          ).then_inc(shifted, 1)
                        dve.wait_ge(shifted, done(q))
                    dve.sem_inc(r.ready, 1) if affine else dve.wait_ge(r.used, done(q))
                    if not affine:
                        dve.sem_inc(r.ready, 1)


def node_rows(nc, T, A, S, name, raw, layer):
    with Phase(nc, name) as f:
        r = Rows(f, S, dense=False, stores=U)
        rows = f.sb("rows", [P, SLOTS, U, C + 1])
        own = f.sb("own", [P, SLOTS, U, C])
        pos = f.sb("pos", [P, SLOTS, U, 1])
        safe = f.sb("safe", [P, SLOTS, U, 1])
        inv = f.sb("inv", [P, SLOTS, U, 1])
        mean = f.sb("mean", [P, SLOTS, U, C])
        mean_t = f.sb("mean_t", [P, SLOTS, U * P])
        w = f.sb("w", [P, C])
        bias = f.sb("bias", [P, C])
        z = f.sb("z", [P, SLOTS, U, C])
        res = f.sb("res", [P, SLOTS, U, C])
        flagged = f.sb("flagged", [P, SLOTS, U, C])
        squares = f.sb("squares", [P, SLOTS, U, C])
        ones = f.sb("ones", [P, P])
        zeros = f.sb("zeros", [P, U * C])
        ps_t = [f.ps(f"ps_t{s}", [P, 512]) for s in range(SLOTS)]
        ps_o = [f.ps(f"ps_o{s}", [P, 512]) for s in range(SLOTS)]
        ps_sum = f.ps("ps_sum", [P, 512])
        ps_sq = f.ps("ps_sq", [P, 512])
        masked, inverted, scaled, turned, turned_out, product = (f.sem(n) for n in (
            "masked", "inverted", "scaled", "turned", "turned_out", "product"))
        flag_set, squared, counted, ones_set, summed = (f.sem(n) for n in (
            "flag_set", "squared", "counted", "ones_set", "summed"))
        ln = LayerNorm(f) if layer == 2 else None
        block = f.block()

        @block.sync
        def _(sp):
            sp.dma_start(w[:], A[f"L0_W{layer}T"]).then_inc(r.weights, 16)
            sp.dma_start(bias[:], A["L0_b2_rows"]).then_inc(r.weights, 16)
            sp.wait_ge(r.weights, 32)
            r.prime(sp, (masked, inverted, scaled, turned, turned_out, product, flag_set, squared, counted,
                         *(ln.sems if ln else ())))
            r.load(sp, [(rows, groups_of(raw))])
            r.finish(sp)

        @block.gpsimd
        def _(pool):
            if layer == 1:
                r.pool_loop(pool, scatters=[(res, T["X1"], SCS, NP_)])
            else:
                r.pool_loop(pool, gathers=[(own, A["x"], NOD, flag_set)], scatters=[(res, T["X1"], SCS, NP_)])

        @block.vector
        def _(dve):
            dve.memset(ones[:], 1.0).then_inc(ones_set, 1)
            dve.memset(zeros[:], 0.0).then_inc(ones_set, 1)
            if ln:
                ln.setup(dve)
            dve.wait_ge(r.weights, 32)
            with dve.Fori(0, r.iters) as i:
                for s in range(SLOTS):
                    dve.wait_ge(r.ready, free(i * SLOTS + s))
                for s in range(SLOTS):
                    q = i * SLOTS + s
                    r.wait_loads(dve, i, s, 1)
                    dve.tensor_scalar(pos[:, s], rows[:, s, :, C:C + 1], 0.0, None, ALU.is_gt)
                    dve.tensor_scalar(safe[:, s], rows[:, s, :, C:C + 1], 1.1754944e-38, None, ALU.max
                                      ).then_inc(masked, 1)
                for s in range(SLOTS):
                    q = i * SLOTS + s
                    dve.wait_ge(masked, done(q))
                    dve.reciprocal(inv[:, s], safe[:, s]).then_inc(inverted, 1)
                for s in range(SLOTS):
                    q = i * SLOTS + s
                    dve.wait_ge(inverted, done(q))
                    dve.tensor_tensor(safe[:, s], inv[:, s], pos[:, s], ALU.mult).then_inc(scaled, 1)
                for s in range(SLOTS):
                    q = i * SLOTS + s
                    dve.wait_ge(scaled, done(q))
                    dve.wait_ge(turned, free(q))
                    dve.tensor_tensor(mean[:, s], rows[:, s, :, 0:C], safe[:, s].to_broadcast([P, U, C]),
                                      ALU.mult).then_inc(r.used, 1)
                for s in range(SLOTS):
                    q = i * SLOTS + s
                    if layer == 1:
                        dve.wait_ge(product, done(q))
                        r.out_free(dve, i, s)
                        dve.tensor_copy(res[:, s], ps_o[s][:].rearrange("p (u c) -> p u c", u=U)
                                        ).then_inc(r.ready, 1)
                        dve.wait_ge(counted, free(q))
                        dve.tensor_tensor(flagged[:, s], ps_o[s][:].rearrange("p (u c) -> p u c", u=U),
                                          S.colf[:, SM, bass.ds(q * U, U)].unsqueeze(2).to_broadcast([P, U, C]),
                                          ALU.mult).then_inc(flag_set, 1)
                    else:
                        dve.wait_ge(product, done(q))
                        r.wait_loads(dve, i, s, 0, 1)
                        dve.tensor_tensor(z[:, s], ps_o[s][:].rearrange("p (u c) -> p u c", u=U), own[:, s],
                                          ALU.add).then_inc(flag_set, 1)
                        dve.wait_ge(flag_set, done(q))
                        dve.tensor_tensor(z[:, s], z[:, s], bc_rows(bias[:]), ALU.add).then_inc(ln.z_ready, 1)
                if ln:
                    ln.moments(dve, i, z, r.tick)
                    ln.scale(dve, i, z, res, r.ready, r.out_free)

        @block.tensor
        def _(pe):
            pe.wait_ge(r.weights, 32)
            pe.wait_ge(ones_set, 2)
            if layer == 1:
                for p in (ps_sum, ps_sq):
                    pe.matmul(p[:], ones[:], zeros[:], start=True, stop=False, skip_group_check=True)
            with pe.Fori(0, r.iters) as i:
                for s in range(SLOTS):
                    q = i * SLOTS + s
                    pe.wait_ge(r.used, done(q))
                    for u in range(U):
                        t = pe.transpose(ps_t[s][:, u * P:(u + 1) * P], mean[:, s, u, :], S.ident[:])
                    t.then_inc(turned, 1)
                for s in range(SLOTS):
                    q = i * SLOTS + s
                    pe.wait_ge(turned_out, done(q))
                    pe.wait_ge(flag_set, free(q))
                    for u in range(U):
                        t = pe.matmul(ps_o[s][:, u * C:(u + 1) * C], mean_t[:, s, u * P:(u + 1) * P], w[:],
                                      start=True, stop=True)
                    t.then_inc(product, 1)
                if layer == 1:
                    for s in range(SLOTS):
                        q = i * SLOTS + s
                        pe.wait_ge(squared, done(q))
                        pe.matmul(ps_sum[:], ones[:], flagged[:, s].rearrange("p u c -> p (u c)"),
                                  start=False, stop=False, skip_group_check=True)
                        pe.matmul(ps_sq[:], ones[:], squares[:, s].rearrange("p u c -> p (u c)"),
                                  start=False, stop=False, skip_group_check=True).then_inc(counted, 1)

        @block.scalar
        def _(act):
            if ln:
                act.wait_ge(ln.eps_set, 1)
            with act.Fori(0, r.iters) as i:
                for s in range(SLOTS):
                    q = i * SLOTS + s
                    act.wait_ge(turned, done(q))
                    act.wait_ge(product, free(q))
                    act.activation(mean_t[:, s], ps_t[s][:], ACT.Copy).then_inc(turned_out, 1)
                if layer == 1:
                    for s in range(SLOTS):
                        q = i * SLOTS + s
                        act.wait_ge(flag_set, done(q))
                        act.wait_ge(counted, free(q))
                        act.activation(squares[:, s], flagged[:, s], ACT.Square).then_inc(squared, 1)
                else:
                    ln.deviation(act, i)
            if layer == 1:
                act.wait_ge(counted, r.iters * SLOTS + SLOTS)
                act.activation(S.affine_sums[:, 0, :], ps_sum[:], ACT.Copy).then_inc(summed, 1)
                act.activation(S.affine_sums[:, 1, :], ps_sq[:], ACT.Copy).then_inc(summed, 1)


def batch_norm(nc, A, S):
    with Phase(nc, "bn") as f:
        rows = f.sb("rows", [P, 3, C])
        tot = f.sb("tot", [P, 2, C])
        mean = f.sb("mean", [P, 2, C])
        sq = f.sb("sq", [P, C])
        var = f.sb("var", [P, C])
        std = f.sb("std", [P, C])
        inv = f.sb("inv", [P, C])
        mu = f.sb("mu", [P, C])
        eps = f.sb("eps", [P, 1])
        loaded, stage, rooted = f.sem("loaded"), f.sem("stage"), f.sem("rooted")
        block = f.block()
        marks = {}

        @block.sync
        def _(sp):
            for k, n in enumerate(("L0_b1_rows", "L0_gamma_rows", "L0_beta_rows")):
                sp.dma_start(rows[:, k, :], A[n]).then_inc(loaded, 16)

        @block.vector
        def _(dve):
            n = 0

            def step(x):
                nonlocal n
                x.then_inc(stage, 1)
                n += 1
                dve.wait_ge(stage, n)

            step(dve.memset(eps[:], EPS))
            step(dve.tensor_reduce(tot[:], S.affine_sums[:].rearrange("p k (u c) -> p k c u", u=U), AX_X, ALU.add))
            step(dve.tensor_scalar(mean[:], tot[:], 1.0 / N_NODES, None, ALU.mult))
            step(dve.tensor_tensor(sq[:], mean[:, 0, :], mean[:, 0, :], ALU.mult))
            step(dve.tensor_tensor(var[:], mean[:, 1, :], sq[:], ALU.subtract))
            step(dve.tensor_scalar(var[:], var[:], 0.0, None, ALU.max))
            marks["var"] = n
            dve.wait_ge(rooted, 1)
            dve.wait_ge(loaded, 48)
            step(dve.reciprocal(inv[:], std[:]))
            step(dve.tensor_tensor(S.affine[:, 0, :], rows[:, 1, :], inv[:], ALU.mult))
            step(dve.tensor_tensor(mu[:], mean[:, 0, :], rows[:, 0, :], ALU.add))
            step(dve.tensor_tensor(mu[:], rows[:, 0, :], mu[:], ALU.subtract))
            step(dve.tensor_tensor(mu[:], mu[:], S.affine[:, 0, :], ALU.mult))
            step(dve.tensor_tensor(S.affine[:, 1, :], mu[:], rows[:, 2, :], ALU.add))

        @block.scalar
        def _(act):
            act.wait_ge(stage, marks["var"])
            act.activation(std[:], var[:], ACT.Sqrt, bias=eps[:]).then_inc(rooted, 1)


def plain_norm(nc, S, name, adds, bias, out):
    with Phase(nc, name) as f:
        r = Rows(f, S, dense=True, stores=1)
        bufs = [f.sb(f"in{k}", [P, SLOTS, U, t.shape[1]]) for k, t in enumerate(adds)]
        z = f.sb("z", [P, SLOTS, U, C])
        res = f.sb("res", [P, SLOTS, U, C])
        ln = LayerNorm(f)
        added = f.sem("added")
        block = f.block()

        @block.sync
        def _(sp):
            r.prime(sp, (added, *ln.sems))
            r.load(sp, [(b, groups_of(t)) for b, t in zip(bufs, adds)])
            r.finish(sp)

        @block.gpsimd
        def _(pool):
            r.pool_loop(pool, stores=[(res, groups_of(out))])

        @block.vector
        def _(dve):
            ln.setup(dve)
            with dve.Fori(0, r.iters) as i:
                for s in range(SLOTS):
                    dve.wait_ge(r.ready, free(i * SLOTS + s))
                for s in range(SLOTS):
                    q = i * SLOTS + s
                    r.wait_loads(dve, i, s, len(adds))
                    dve.tensor_tensor(z[:, s], bufs[0][:, s, :, 0:C], bc_rows(bias), ALU.add
                                      ).then_inc(added if len(adds) == 2 else ln.z_ready, 1)
                for s in range(SLOTS):
                    q = i * SLOTS + s
                    if len(adds) == 2:
                        dve.wait_ge(added, done(q))
                        dve.tensor_tensor(z[:, s], z[:, s], bufs[1][:, s, :, 0:C], ALU.add).then_inc(ln.z_ready, 1)
                    dve.wait_ge(ln.z_ready, done(q))
                    dve.sem_inc(r.used, 1)
                ln.moments(dve, i, z, r.tick)
                ln.scale(dve, i, z, res, r.ready, r.out_free)

        @block.scalar
        def _(act):
            act.wait_ge(ln.eps_set, 1)
            with act.Fori(0, r.iters) as i:
                ln.deviation(act, i)


def weights_phase(nc, A, S):
    with Phase(nc, "weights") as f:
        att1 = f.sb("att1", [P, 2, HC])
        att2 = f.sb("att2", [P, 2, C])
        prod1 = f.sb("prod1", [P, 2, HC])
        prod2 = f.sb("prod2", [P, 2, 2, C])
        cols = f.sb("cols", [P, 2])
        w = f.sb("w", [P, 2, C])
        rows = f.sb("rows", [P, 3, C])
        hid = f.sb("hid", [P, 2])
        absx = f.sb("absx", [P, 1])
        ex = f.sb("ex", [P, 1])
        lg = f.sb("lg", [P, 1])
        spread = f.sb("spread", [P, 2, P])
        one = f.sb("one", [P, 1])
        acc = f.ps("acc", [P, 2, C])
        loaded, stage, logs, multiplied = f.sem("loaded"), f.sem("stage"), f.sem("logs"), f.sem("multiplied")
        block = f.block()
        marks = {}

        @block.sync
        def _(sp):
            for out, src in ((S.W1[:], A["L1_W1"]), (S.W2x[:, :, 0:C], A["L1_W2"]), (S.b1col[:], A["L1_b1_cols"]),
                             (att1[:, 0, :], A["L1_as1"]), (att1[:, 1, :], A["L1_ad1"]),
                             (att2[:, 0, :], A["L1_as2"]), (att2[:, 1, :], A["L1_ad2"]),
                             (cols[:, 0:1], A["L2_b1_col"]), (cols[:, 1:2], A["L3_bfc1_col"]),
                             (w[:, 0, :], A["L2_W2"]), (w[:, 1, :], A["L3_Wfc2T"]),
                             (rows[:, 0, :], A["L2_b2_rows"]), (rows[:, 1, :], A["L2_bpre_rows"]),
                             (rows[:, 2, :], A["L3_bfc2_rows"]), (S.b0[:], A["L0_b2_rows"]),
                             (S.b2[:], A["L1_b2_rows"])):
                sp.dma_start(out, src).then_inc(loaded, 16)

        @block.vector
        def _(dve):
            n = 0

            def step(*ins):
                nonlocal n
                for x in ins:
                    x.then_inc(stage, 1)
                n += len(ins)
                dve.wait_ge(stage, n)

            dve.wait_ge(loaded, 16 * 16)
            step(dve.memset(one[:], 1.0), dve.memset(S.W2x[:, :, C + 2:H2W], 0.0))
            marks["one"] = n
            step(*[dve.tensor_tensor(prod1[:, k, :], S.W1[:], att1[:, k, :], ALU.mult) for k in range(2)],
                 *[dve.tensor_tensor(prod2[:, k, :, :], S.W2x[:, :, 0:C],
                                     att2[:, k, :].unsqueeze(1).to_broadcast([P, 2, C]), ALU.mult)
                   for k in range(2)])
            step(*[dve.tensor_reduce(S.WA[:, k * HEADS:(k + 1) * HEADS],
                                     prod1[:, k, :].rearrange("p (h c) -> p h c", h=HEADS), AX_X, ALU.add)
                   for k in range(2)],
                 *[dve.tensor_reduce(S.W2x[:, :, C + k:C + k + 1], prod2[:, k, :, :], AX_X, ALU.add)
                   for k in range(2)])
            step(dve.tensor_scalar(hid[:], cols[:], 0.0, None, ALU.max))
            dve.wait_ge(logs, 3)
            step(dve.scalar_tensor_tensor(hid[:, 1:2], lg[:], -LOG2, hid[:, 1:2], ALU.add, ALU.add))
            step(dve.tensor_copy(spread[:], hid[:].unsqueeze(2).to_broadcast([P, 2, P])))
            marks["spread"] = n
            dve.wait_ge(multiplied, 1)
            step(dve.tensor_tensor(S.c2[:], acc[:, 0, :], rows[:, 0, :], ALU.add),
                 dve.tensor_tensor(S.c3[:], acc[:, 1, :], rows[:, 2, :], ALU.add))
            step(dve.tensor_scalar(S.c2[:], S.c2[:], 0.0, None, ALU.max))
            step(dve.tensor_tensor(S.c2[:], S.c2[:], rows[:, 1, :], ALU.add))

        @block.scalar
        def _(act):
            act.wait_ge(stage, marks["one"])
            act.activation(absx[:], cols[:, 1:2], ACT.Abs).then_inc(logs, 1)
            act.wait_ge(logs, 1)
            act.activation(ex[:], absx[:], ACT.Exp, scale=-1.0).then_inc(logs, 1)
            act.wait_ge(logs, 2)
            act.activation(lg[:], ex[:], ACT.Ln, bias=one[:]).then_inc(logs, 1)

        @block.tensor
        def _(pe):
            pe.wait_ge(stage, marks["spread"])
            for k in range(2):
                m = pe.matmul(acc[:, k, :], spread[:, k, :], w[:, k, :], start=True, stop=True)
            m.then_inc(multiplied, 1)



def gat_rows(nc, T, S, name, dense):
    with Phase(nc, name) as f:
        r = Rows(f, S, dense, stores=2 if dense else U)
        w_in = C if dense else HC + HEADS
        rows = f.sb("rows", [P, SLOTS, U, w_in])
        x_t = f.sb("x_t", [P, SLOTS, U * P])
        inv = f.sb("inv", [P, SLOTS, U, HEADS])
        den = f.sb("den", [P, SLOTS, U, HEADS])
        mean = f.sb("mean", [P, SLOTS, U, HC])
        aa = f.sb("aa", [P, SLOTS, U, 2 * HEADS])
        pos = f.sb("pos", [P, SLOTS, 2, U * P])
        neg = f.sb("neg", [P, SLOTS, 2, U * P])
        elu = f.sb("elu", [P, SLOTS, 2, U * P])
        res = f.sb("res", [P, SLOTS, U, H2W])
        ps_t = f.ps("ps_t", [P, U * P])
        ps_a = f.ps("ps_a", [P, 512])
        ps_h = f.ps("ps_h", [P, 2, U * P])
        ps_o = f.ps("ps_o", [P, U, 256])
        x_ready, hidden, aa_out, relued, clipped, exped, elu_ready, product, safe, inverted, normed = (
            f.sem(n) for n in ("x_ready", "hidden", "aa_out", "relued", "clipped", "exped", "elu_ready",
                               "product", "safe", "inverted", "normed"))
        block = f.block()

        @block.sync
        def _(sp):
            r.prime(sp, (x_ready, hidden, aa_out, relued, clipped, exped, elu_ready, product, safe, inverted,
                         normed))
            r.load(sp, [(rows, groups_of(T["X1"] if dense else T["RAW260"]))])
            r.finish(sp)

        @block.gpsimd
        def _(pool):
            if dense:
                r.pool_loop(pool, stores=[(res, groups_of(T["H2"])), (aa, groups_of(T["AA"]))])
            else:
                r.pool_loop(pool, scatters=[(res, T["H2"], SCD, NP_)])

        @block.tensor
        def _(pe):
            with pe.Fori(0, r.iters) as i:
                for s in range(SLOTS):
                    q = i * SLOTS + s
                    if dense:
                        r.wait_loads(pe, i, s, 1)
                        pe.wait_ge(x_ready, behind(q))
                        for u in range(U):
                            t = pe.transpose(ps_t[:, u * P:(u + 1) * P], rows[:, s, u, :], S.ident[:])
                        t.then_inc(r.used, 1)
                for s in range(SLOTS):
                    q = i * SLOTS + s
                    pe.wait_ge(relued, behind(q))
                    pe.wait_ge(clipped, behind(q))
                    if dense:
                        pe.wait_ge(aa_out, behind(q))
                        pe.wait_ge(x_ready, done(q))
                        for u in range(U):
                            pe.matmul(ps_a[:, u * 8:(u + 1) * 8], x_t[:, s, u * P:(u + 1) * P], S.WA[:],
                                      start=True, stop=True)
                        for c in range(2):
                            t = pe.matmul(ps_h[:, c, :], S.W1[:, c * P:(c + 1) * P], x_t[:, s], start=True, stop=True)
                    else:
                        pe.wait_ge(normed, done(q))
                        for c in range(2):
                            for u in range(U):
                                t = pe.transpose(ps_h[:, c, u * P:(u + 1) * P],
                                                 mean[:, s, u, c * P:(c + 1) * P], S.ident[:])
                    t.then_inc(hidden, 1)
                for s in range(SLOTS):
                    q = i * SLOTS + s
                    pe.wait_ge(elu_ready, done(q))
                    pe.wait_ge(r.ready, behind(q))
                    for u in range(U):
                        for c in range(2):
                            t = pe.matmul(ps_o[:, u, 0:H2W], elu[:, s, c, u * P:(u + 1) * P], S.W2x[:, c, :],
                                          start=(c == 0), stop=(c == 1))
                    t.then_inc(product, 1)

        @block.vector
        def _(dve):
            with dve.Fori(0, r.iters) as i:
                for s in range(SLOTS):
                    dve.wait_ge(elu_ready, free(i * SLOTS + s))
                if not dense:
                    for s in range(SLOTS):
                        q = i * SLOTS + s
                        r.wait_loads(dve, i, s, 1)
                        dve.tensor_scalar(den[:, s], rows[:, s, :, HC:HC + HEADS], 1e-30, None, ALU.max
                                          ).then_inc(safe, 1)
                    for s in range(SLOTS):
                        q = i * SLOTS + s
                        dve.wait_ge(safe, done(q))
                        dve.reciprocal(inv[:, s], den[:, s]).then_inc(inverted, 1)
                    for s in range(SLOTS):
                        q = i * SLOTS + s
                        dve.wait_ge(inverted, done(q))
                        dve.wait_ge(hidden, free(q))
                        for u in range(U):
                            t = dve.tensor_tensor(mean[:, s, u, :].rearrange("p (h c) -> p h c", h=HEADS),
                                                  rows[:, s, u, 0:HC].rearrange("p (h c) -> p h c", h=HEADS),
                                                  inv[:, s, u, :].unsqueeze(2).to_broadcast([P, HEADS, HID]),
                                                  ALU.mult)
                        t.then_inc(normed, 1)
                        dve.wait_ge(normed, done(q))
                        dve.sem_inc(r.used, 1)
                for s in range(SLOTS):
                    q = i * SLOTS + s
                    dve.wait_ge(hidden, done(q))
                    if dense:
                        r.out_free(dve, i, s)
                        dve.tensor_copy(aa[:, s].rearrange("p u k -> p (u k)"), ps_a[:, 0:U * 8]).then_inc(aa_out, 1)
                    dve.wait_ge(exped, free(q))
                    for c in range(2):
                        t = dve.tensor_scalar(neg[:, s, c, :], ps_h[:, c, :], S.b1col[:, c:c + 1], 0.0,
                                              ALU.add, ALU.min)
                    t.then_inc(clipped, 1)
                for s in range(SLOTS):
                    q = i * SLOTS + s
                    dve.wait_ge(exped, done(q))
                    dve.wait_ge(product, free(q))
                    dve.scalar_tensor_tensor(elu[:, s].rearrange("p c r -> p (c r)"),
                                             neg[:, s].rearrange("p c r -> p (c r)"), -1.0,
                                             pos[:, s].rearrange("p c r -> p (c r)"), ALU.add, ALU.add
                                             ).then_inc(elu_ready, 1)

        @block.scalar
        def _(act):
            with act.Fori(0, r.iters) as i:
                if dense:
                    for s in range(SLOTS):
                        q = i * SLOTS + s
                        act.wait_ge(r.used, done(q))
                        act.wait_ge(hidden, free(q))
                        act.activation(x_t[:, s], ps_t[:], ACT.Copy).then_inc(x_ready, 1)
                for s in range(SLOTS):
                    q = i * SLOTS + s
                    act.wait_ge(clipped, done(q))
                    act.wait_ge(elu_ready, free(q))
                    for c in range(2):
                        t = act.activation(pos[:, s, c, :], ps_h[:, c, :], ACT.Relu, bias=S.b1col[:, c:c + 1])
                    t.then_inc(relued, 1)
                for s in range(SLOTS):
                    q = i * SLOTS + s
                    act.wait_ge(clipped, done(q))
                    act.wait_ge(elu_ready, free(q))
                    act.activation(neg[:, s].rearrange("p c r -> p (c r)"),
                                   neg[:, s].rearrange("p c r -> p (c r)"), ACT.Exp).then_inc(exped, 1)
                for s in range(SLOTS):
                    q = i * SLOTS + s
                    act.wait_ge(product, done(q))
                    r.out_free(act, i, s)
                    act.activation(res[:, s], ps_o[:, :, 0:H2W], ACT.Copy).then_inc(r.ready, 1)


def attention_phase(nc, T, S, name, H, table, scale, offset):
    ET, HT = EDGE_TILES, HALF_T
    tw = table.shape[1]
    with Phase(nc, name) as f:
        base = f.sb("base", [P, 2, ET], I32)
        slot = f.sb("slot", [P, SLOTS, 2, U], I32)
        got = f.sb("got", [P, SLOTS, 2, U, tw])
        terms = f.sb("terms", [P, 2, 2 * H, ET])
        keys = f.sb("keys", [HT, 2, P])
        prv = f.sb("prv", [HT, 2, P])
        nxt = f.sb("nxt", [HT, 2, P])
        pen = f.sb("pen", [HT, 2, 4, P])
        line = f.sb("line", [HT, 2, H, P])
        fwd = f.sb("fwd", [HT, 2, H, P])
        seg = f.sb("seg", [HT, 2, H, P])
        edge_keys = f.sb("edge_keys", [HT, 2, ET])
        own_keys = f.sb("own_keys", [HT, 2, 2])
        apart = f.sb("apart", [HT, 2, 2, 2 * ET])
        ends = f.sb("ends", [HT, H, 2 * ET])
        cand = f.sb("cand", [HT, H, 2 * ET])
        best = f.sb("best", [HT, 2, 2, H])
        most = f.sb("most", [P, H, ET])
        t1 = f.sb("t1", [P, H, ET])
        t2 = f.sb("t2", [P, H, ET])
        m = f.sb("m", [P, H, ET])
        ps_line = f.ps("ps_line", [P, 4, 512])
        ps_back = f.ps("ps_back", [P, 4, 512])
        picked, tick, copied, scaled = (f.sem(n) for n in ("picked", "tick", "copied", "scaled"))
        loaded, stage, turned, turned_back, sent, fetched, exps = (
            f.sem(n) for n in ("loaded", "stage", "turned", "turned_back", "sent", "fetched", "exps"))
        gathered = f.sems("gathered")
        block = f.block()
        marks = {}
        K = T["keys"]

        @block.gpsimd
        def _(pool):
            pool.sem_inc(copied, SLOTS)
            pool.wait_ge(scaled, 2)
            with pool.Fori(0, EDGE_GROUPS // SLOTS) as i:
                for s in range(SLOTS):
                    q = i * SLOTS + s
                    pool.wait_ge(copied, free(q))
                    pool.tensor_copy(slot[:, s], base[:, :, bass.ds(q * U, U)]).then_inc(picked, 1)
                    pool.wait_ge(picked, q + 1)
                    pool.sem_inc(tick, 1)
                    for k in range(2):
                        for u in range(U):
                            gather(pool, got[:, s, k, u, :], table, slot[:, s, k, u:u + 1]
                                   ).then_inc(gathered[s], 16)

        @block.vector
        def _(dve):
            for k, col in enumerate((SRC, DST)):
                dve.tensor_scalar(base[:, k, :], S.coli[:, col, :], float(scale), float(offset), ALU.mult,
                                  ALU.add).then_inc(scaled, 1)
            with dve.Fori(0, EDGE_GROUPS // SLOTS) as i:
                for s in range(SLOTS):
                    q = i * SLOTS + s
                    dve.wait_ge(gathered[s], (i + 1) * (16 * 2 * U))
                    for k in range(2):
                        t = dve.tensor_copy(terms[:, k, :, bass.ds(q * U, U)],
                                            got[:, s, k, :, 0:2 * H].rearrange("p u k -> p k u"))
                    t.then_inc(copied, 1)
            n = 0

            def step(*ins):
                nonlocal n
                for x in ins:
                    x.then_inc(stage, 1)
                n += len(ins)
                dve.wait_ge(stage, n)

            def differ(out, a, b):
                return [dve.tensor_tensor(out, a, b, ALU.not_equal)]

            dve.wait_ge(loaded, 16 * 5)
            step(*differ(pen[:, :, 0, :], keys[:], prv[:]), *differ(pen[:, :, 1, :], keys[:], nxt[:]),
                 *differ(pen[:, :, 2, :], keys[:], keys[:, :, 0:1].to_broadcast([HT, 2, P])),
                 *differ(pen[:, :, 3, :], keys[:], keys[:, :, P - 1:P].to_broadcast([HT, 2, P])),
                 dve.tensor_copy(own_keys[:, :, 0:1], keys[:, :, 0:1]),
                 dve.tensor_copy(own_keys[:, :, 1:2], keys[:, :, P - 1:P]))
            step(*[dve.tensor_scalar(apart[:, c, k, :], edge_keys[:].rearrange("p a t -> p (a t)"),
                                     own_keys[:, c, k:k + 1], NEG, ALU.not_equal, ALU.mult)
                   for c in range(2) for k in range(2)],
                 dve.tensor_scalar(pen[:], pen[:], NEG, None, ALU.mult))
            for c in range(2):
                for h in range(H):
                    dve.wait_ge(turned, c * H + h + 1)
                    dve.tensor_copy(line[:, c, h, :], ps_line[0:HT, (c * H + h) % 4, 0:P]).then_inc(stage, 1)
                    n += 1
            marks["lines"] = n
            dve.wait_ge(stage, n)
            step(*[dve.tensor_tensor_scan(fwd[:, c, h, :], pen[:, c, 0, :], line[:, c, h, :], NEG, ALU.add, ALU.max)
                   for c in range(2) for h in range(H)])
            step(*[dve.tensor_tensor_scan(seg[:, c, h, ::-1], pen[:, c, 1, ::-1], fwd[:, c, h, ::-1], NEG,
                                          ALU.add, ALU.max)
                   for c in range(2) for h in range(H)])
            marks["tiles"] = n
            dve.wait_ge(fetched, 16)
            for c in range(2):
                for k in range(2):
                    step(dve.tensor_tensor(cand[:], ends[:], apart[:, c, k, :].unsqueeze(1)
                                           .to_broadcast([HT, H, 2 * ET]), ALU.add))
                    step(dve.tensor_reduce(best[:, c, k, :], cand[:], AX_X, ALU.max))
            for k in range(2):
                step(*[dve.scalar_tensor_tensor(seg[:, c, h, :], pen[:, c, 2 + k, :], best[:, c, k, h:h + 1],
                                                seg[:, c, h, :], ALU.add, ALU.max)
                       for c in range(2) for h in range(H)])
            marks["segments"] = n
            for c in range(2):
                for h in range(H):
                    dve.wait_ge(turned_back, c * H + h + 1)
                    dve.tensor_copy(most[:, h, c * HT:(c + 1) * HT], ps_back[:, (c * H + h) % 4, 0:HT]
                                    ).then_inc(stage, 1)
                    n += 1
            dve.wait_ge(stage, n)

            def leaky(x, y):
                return dve.scalar_tensor_tensor(x, y, SLOPE, y, ALU.mult, ALU.max)

            src_s, dst_s, dst_d = terms[:, 0, 0:H, :], terms[:, 1, 0:H, :], terms[:, 1, H:2 * H, :]
            step(dve.tensor_tensor(most[:], most[:], dst_s, ALU.max))
            step(dve.tensor_tensor(most[:], most[:], dst_d, ALU.add), dve.tensor_tensor(t1[:], src_s, dst_d, ALU.add),
                 dve.tensor_tensor(t2[:], dst_s, dst_d, ALU.add))
            step(leaky(m[:], most[:]), leaky(t1[:], t1[:]), leaky(t2[:], t2[:]))
            step(dve.tensor_tensor(t1[:], t1[:], m[:], ALU.subtract), dve.tensor_tensor(t2[:], t2[:], m[:], ALU.subtract))
            marks["logits"] = n
            dve.wait_ge(exps, 2)

            def by_tile(x):
                return x[:, :, 0:H].rearrange("p t h -> p h t")

            step(dve.tensor_copy(by_tile(S.ws), t1[:]),
                 dve.tensor_tensor(by_tile(S.wd), t2[:], S.colf[:, SF, :].unsqueeze(1).to_broadcast([P, H, ET]),
                                   ALU.mult))
            step(dve.tensor_tensor(by_tile(S.wt), by_tile(S.ws), by_tile(S.wd), ALU.add))

        @block.tensor
        def _(pe):
            pe.wait_ge(copied, EDGE_GROUPS + SLOTS)
            for c in range(2):
                for h in range(H):
                    b = c * H + h
                    if b >= 4:
                        pe.wait_ge(stage, marks["lines"] - 2 * H + b - 3)
                    pe.transpose(ps_line[0:HT, b % 4, 0:P], terms[:, 0, h, c * HT:(c + 1) * HT], S.ident[:]
                                 ).then_inc(turned, 1)
            pe.wait_ge(stage, marks["segments"])
            for c in range(2):
                for h in range(H):
                    b = c * H + h
                    if b >= 4:
                        pe.wait_ge(stage, marks["segments"] + b - 3)
                    pe.transpose(ps_back[:, b % 4, 0:HT], seg[:, c, h, :], S.ident[0:HT, 0:HT]
                                 ).then_inc(turned_back, 1)

        @block.scalar
        def _(act):
            act.wait_ge(stage, marks["logits"])
            act.activation(t1[:], t1[:], ACT.Exp).then_inc(exps, 1)
            act.activation(t2[:], t2[:], ACT.Exp).then_inc(exps, 1)

        @block.sync
        def _(sp):
            for out, at in ((prv, 0), (keys, 1), (nxt, 2)):
                sp.dma_start(out[:], K[0, at:at + ET * P].rearrange("(c p e) -> p c e", p=HT, e=P)
                             ).then_inc(loaded, 16)
            with nc.allow_non_contiguous_dma(reason="first key of each tile"):
                sp.dma_start(edge_keys[:, 0, :], K[0:1, 1:1 + ET * P].rearrange("o (t e) -> o t e", e=P)[:, :, 0]
                             .to_broadcast([HT, ET])).then_inc(loaded, 16)
            sp.dma_start(edge_keys[:, 1, :], T["last"][0:1, 0:ET].to_broadcast([HT, ET])).then_inc(loaded, 16)
            sp.wait_ge(stage, marks["tiles"])
            dst = T["ends"][0:H, :].rearrange("h (k c p) -> k p c h", k=2, p=HT)
            with nc.allow_non_contiguous_dma(reason="one value per tile, head and end"):
                for k, e in ((0, 0), (1, P - 1)):
                    for c in range(2):
                        sp.dma_start(dst[k, :, c, :], seg[:, c, :, e]).then_inc(sent, 16)
            sp.wait_ge(sent, 64)
            sp.dma_start(ends[:], T["ends"][0:H, :].unsqueeze(0).to_broadcast([HT, H, 2 * ET])).then_inc(fetched, 16)


def gat_sum(nc, T, S, name, layer):
    first = layer == 1
    table = T["X1"] if first else T["H2"]
    out = T["RAW260"] if first else T["RAW129"]
    H = HEADS if first else 1
    w = out.shape[1]
    wt = table.shape[1]
    D = w - H
    with Phase(nc, name) as f:
        slot = f.sb("slot", [P, SLOTS, 2, U], I32)
        rows = f.sb("rows", [P, SLOTS, 2, U, wt])
        x_t = f.sb("x_t", [P, 2, U * P])
        v = f.sb("v", [P, SLOTS, U, w])
        part = f.sb("part", [P, SLOTS, U, D])
        krow = f.sb("krow", [P, SLOTS, U * P])
        same = f.sb("same", [P, SLOTS, U, P])
        sums = f.sb("sums", [P, SLOTS, U, w])
        ps_t = f.ps("ps_t", [P, 2, 512])
        ps_h = f.ps("ps_h", [P, 2, U, 256]) if first else None
        acc = f.ps("acc", [P, 2, 512])
        picked, tick, matched, summed, copied, turned, x_ready, hidden, weighted, parted, valued = (
            f.sem(n) for n in ("picked", "tick", "matched", "summed", "copied", "turned", "x_ready", "hidden",
                               "weighted", "parted", "valued"))
        gathered, keyed, stored = f.sems("gathered"), f.sems("keyed"), f.sems("stored")
        primed = prime_stores(f, stored, 1, S.ident_dram)
        block = f.block()
        iters = EDGE_GROUPS // SLOTS
        out_g = groups_of(out)
        rows_used = turned if first else valued

        @block.sync
        def _(sp):
            for m in (matched, turned, x_ready, hidden, weighted, parted, valued):
                sp.sem_inc(m, SLOTS)
            for m in (summed, copied):
                sp.sem_inc(m, 2 * SLOTS)
            with sp.Fori(0, iters) as i:
                for s in range(SLOTS):
                    q = i * SLOTS + s
                    sp.wait_ge(matched, free(q))
                    sp.dma_start(krow[:, s], T["keys"][0:1, bass.ds(q * (U * P) + 1, U * P)]
                                 .to_broadcast([P, U * P])).then_inc(keyed[s], 16)
            for s in range(SLOTS):
                sp.wait_ge(stored[s], 16 * (iters + 1))

        @block.gpsimd
        def _(pool):
            with pool.Fori(0, iters) as i:
                for s in range(SLOTS):
                    q = i * SLOTS + s
                    pool.wait_ge(rows_used, free(q))
                    for k, col in enumerate((SRC, DST)):
                        t = pool.tensor_copy(slot[:, s, k], S.coli[:, col, bass.ds(q * U, U)])
                    t.then_inc(picked, 1)
                    pool.wait_ge(picked, q + 1)
                    pool.sem_inc(tick, 1)
                    for k in range(2):
                        for u in range(U):
                            gather(pool, rows[:, s, k, u, :], table, slot[:, s, k, u:u + 1]
                                   ).then_inc(gathered[s], 16)

        @block.tensor
        def _(pe):
            with pe.Fori(0, iters) as i:
                for s in range(SLOTS):
                    q = i * SLOTS + s
                    if first:
                        pe.wait_ge(gathered[s], (i + 1) * (16 * 2 * U))
                        pe.wait_ge(x_ready, behind(q))
                        for k in range(2):
                            for u in range(U):
                                t = pe.transpose(ps_t[:, k, u * P:(u + 1) * P], rows[:, s, k, u, :], S.ident[:])
                        t.then_inc(turned, 1)
                        pe.wait_ge(x_ready, done(q))
                        pe.wait_ge(parted, behind(q))
                        for k in range(2):
                            for u in range(U):
                                t = pe.matmul(ps_h[:, k, u, :], x_t[:, k, u * P:(u + 1) * P], S.W1[:],
                                              start=True, stop=True)
                        t.then_inc(hidden, 1)
                for s in range(SLOTS):
                    q = i * SLOTS + s
                    pe.wait_ge(valued, done(q))
                    pe.wait_ge(matched, done(q))
                    for half in range(2):
                        pe.wait_ge(copied, q * 2 + (half + 2 * SLOTS))
                        for b in range(2):
                            u = 2 * half + b
                            t = pe.matmul(acc[:, b, 0:w], same[:, s, u, :], v[:, s, u, :], start=True, stop=True)
                        t.then_inc(summed, 1)

        @block.vector
        def _(dve):
            with dve.Fori(0, iters) as i:
                for s in range(SLOTS):
                    q = i * SLOTS + s
                    dve.wait_ge(keyed[s], (i + 1) * 16)
                    dve.wait_ge(summed, q * 2 + 2)
                    dve.tensor_tensor(same[:, s], krow[:, s].rearrange("p (u e) -> p u e", u=U),
                                      S.colf[:, KD, bass.ds(q * U, U)].unsqueeze(2).to_broadcast([P, U, P]),
                                      ALU.is_equal).then_inc(matched, 1)
                for s in range(SLOTS):
                    q = i * SLOTS + s
                    if first:
                        dve.wait_ge(hidden, done(q))
                    else:
                        dve.wait_ge(gathered[s], (i + 1) * (16 * 2 * U))

                    def values(k):
                        if first:
                            return ps_h[:, k].rearrange("p u (h c) -> p (u h) c", h=HEADS)
                        return rows[:, s, k, :, 0:C]

                    def heads(x):
                        return x.rearrange("p u (h c) -> p u h c", h=H)

                    for k, (dest, wgt, mark) in enumerate(((v[:, s, :, 0:D], S.ws, weighted),
                                                           (part[:, s], S.wd, parted))):
                        wcol = wgt[:, bass.ds(q * U, U), 0:H]
                        if first:
                            dve.tensor_tensor(heads(dest), heads(ps_h[:, k]),
                                              wcol.unsqueeze(3).to_broadcast([P, U, H, HID]), ALU.mult
                                              ).then_inc(mark, 1)
                        else:
                            dve.tensor_tensor(dest, rows[:, s, k, :, 0:C], wcol.to_broadcast([P, U, C]), ALU.mult
                                              ).then_inc(mark, 1)
                    dve.tensor_copy(v[:, s, :, D:w], S.wt[:, bass.ds(q * U, U), 0:H])
                    dve.wait_ge(weighted, done(q))
                    dve.wait_ge(parted, done(q))
                    dve.tensor_tensor(v[:, s, :, 0:D], v[:, s, :, 0:D], part[:, s], ALU.add).then_inc(valued, 1)

        @block.scalar
        def _(act):
            primed(act)
            with act.Fori(0, iters) as i:
                if first:
                    for s in range(SLOTS):
                        q = i * SLOTS + s
                        act.wait_ge(turned, done(q))
                        act.wait_ge(hidden, behind(q))
                        act.activation(x_t[:], ps_t[:], ACT.Copy).then_inc(x_ready, 1)
                for s in range(SLOTS):
                    q = i * SLOTS + s
                    act.wait_ge(stored[s], (i + 1) * 16)
                    for half in range(2):
                        act.wait_ge(summed, q * 2 + (half + 2 * SLOTS + 1))
                        act.activation(sums[:, s, 2 * half:2 * half + 2, :], acc[:, :, 0:w], ACT.Copy
                                       ).then_inc(copied, 1)
                    act.wait_ge(copied, q * 2 + (2 * SLOTS + 2))
                    act.dma_start(out_g[q], sums[:, s]).then_inc(stored[s], 16)


def gat_nodes(nc, T, S):
    with Phase(nc, "gatnodes") as f:
        r = Rows(f, S, dense=False, stores=U)
        rows = f.sb("rows", [P, SLOTS, U, C + 1])
        own = f.sb("own", [P, SLOTS, U, C])
        den = f.sb("den", [P, SLOTS, U, 1])
        inv = f.sb("inv", [P, SLOTS, U, 1])
        z = f.sb("z", [P, SLOTS, U, C])
        res = f.sb("res", [P, SLOTS, U, C])
        ln = LayerNorm(f)
        safe, inverted, owned = f.sem("safe"), f.sem("inverted"), f.sem("owned")
        block = f.block()

        @block.sync
        def _(sp):
            r.prime(sp, (safe, inverted, owned, *ln.sems))
            r.load(sp, [(rows, groups_of(T["RAW129"]))])
            r.finish(sp)

        @block.gpsimd
        def _(pool):
            r.pool_loop(pool, gathers=[(own, T["X1"], DST, owned)], scatters=[(res, T["X2"], SCD, NP_)])

        @block.vector
        def _(dve):
            ln.setup(dve)
            with dve.Fori(0, r.iters) as i:
                for s in range(SLOTS):
                    dve.wait_ge(r.ready, free(i * SLOTS + s))
                for s in range(SLOTS):
                    q = i * SLOTS + s
                    r.wait_loads(dve, i, s, 1)
                    dve.tensor_scalar(den[:, s], rows[:, s, :, C:C + 1], 1e-30, None, ALU.max).then_inc(safe, 1)
                for s in range(SLOTS):
                    q = i * SLOTS + s
                    dve.wait_ge(safe, done(q))
                    dve.reciprocal(inv[:, s], den[:, s]).then_inc(inverted, 1)
                for s in range(SLOTS):
                    q = i * SLOTS + s
                    dve.wait_ge(inverted, done(q))
                    dve.tensor_tensor(z[:, s], rows[:, s, :, 0:C], inv[:, s].to_broadcast([P, U, C]), ALU.mult
                                      ).then_inc(r.used, 1)
                for s in range(SLOTS):
                    q = i * SLOTS + s
                    r.wait_loads(dve, i, s, 0, 1)
                    dve.wait_ge(r.used, done(q))
                    dve.tensor_tensor(z[:, s], z[:, s], own[:, s], ALU.add).then_inc(owned, 1)
                for s in range(SLOTS):
                    q = i * SLOTS + s
                    dve.wait_ge(owned, done(q))
                    dve.tensor_tensor(z[:, s], z[:, s], bc_rows(S.b2[:]), ALU.add).then_inc(ln.z_ready, 1)
                ln.moments(dve, i, z, r.tick)
                ln.scale(dve, i, z, res, r.ready, r.out_free)

        @block.scalar
        def _(act):
            act.wait_ge(ln.eps_set, 1)
            with act.Fori(0, r.iters) as i:
                ln.deviation(act, i)



def gin_rows(nc, T, A, S, name, dense):
    with Phase(nc, name) as f:
        r = Rows(f, S, dense, stores=1 if dense else U)
        x = f.sb("x", [P, SLOTS, U, C])
        agg = None if dense else f.sb("agg", [P, SLOTS, U, C + 1])
        turned_t = f.sb("turned_t", [P, SLOTS, U * P])
        agg_t = None if dense else f.sb("agg_t", [P, SLOTS, U * P])
        pre = None if dense else f.sb("pre", [P, SLOTS, U, C])
        hid = None if dense else f.sb("hid", [P, SLOTS, U * P])
        add = None if dense else f.sb("add", [P, SLOTS, U, C])
        w = f.sb("w", [P, 3, C])
        rows = f.sb("rows", [P, 4, C])
        b1 = f.sb("b1", [P, 1])
        z = f.sb("z", [P, SLOTS, U, C])
        y = f.sb("y", [P, SLOTS, U, C])
        res = f.sb("res", [P, SLOTS, U, C])
        ps_t = f.ps("ps_t", [P, U * P])
        ps_o = f.ps("ps_o", [P, U * P])
        ps_g = f.ps("ps_g", [P, U * P])
        ps_p = f.ps("ps_p", [P, U * P])
        ps_1 = f.ps("ps_1", [P, U * P])
        ps_2 = f.ps("ps_2", [P, U * P])
        ln, ln2 = LayerNorm(f), LayerNorm(f, "2")
        turned, turned_out, own_h, normed, gained = (f.sem(n) for n in (
            "turned", "turned_out", "own_h", "normed", "gained"))
        f.beta_in = f.sem("beta_in")
        agg_turned, agg_out, pre_ready, counted, pre_turned, pre_out, layer1, relued, layer2, biased, added = (
            f.sem(n) for n in ("agg_turned", "agg_out", "pre_ready", "counted", "pre_turned", "pre_out", "layer1",
                               "relued", "layer2", "biased", "added"))
        block = f.block()

        @block.sync
        def _(sp):
            for out, src in ((w[:, 0, :], A["L2_Wpre"]), (w[:, 1, :], A["L2_W1"]), (w[:, 2, :], A["L2_W2"]),
                             (rows[:, 0, :], A["L2_bpre_rows"]), (rows[:, 1, :], A["L2_b2_rows"]),
                             (rows[:, 2, :], A["L2_gamma_rows"]), (rows[:, 3, :], A["L2_beta_rows"]),
                             (b1[:], A["L2_b1_col"])):
                sp.dma_start(out, src).then_inc(r.weights, 16)
            r.prime(sp, (turned, turned_out, own_h, normed, gained, agg_turned, agg_out, pre_ready, counted,
                         pre_turned, pre_out, layer1, relued, layer2, biased, added, *ln.sems, *ln2.sems))
            r.load(sp, [(x, groups_of(T["X2"]))] if dense else [(agg, groups_of(T["RAW129"]))])
            r.finish(sp)

        @block.gpsimd
        def _(pool):
            if dense:
                r.pool_loop(pool, stores=[(res, groups_of(T["X3"]))])
            else:
                r.pool_loop(pool, gathers=[(x, T["X2"], DST, ln2.z_ready)], scatters=[(res, T["X3"], SCD, NP_)])

        @block.tensor
        def _(pe):
            pe.wait_ge(r.weights, 16 * 8)
            with pe.Fori(0, r.iters) as i:
                if not dense:
                    for s in range(SLOTS):
                        q = i * SLOTS + s
                        r.wait_loads(pe, i, s, 1)
                        pe.wait_ge(agg_out, behind(q))
                        for u in range(U):
                            t = pe.transpose(ps_g[:, u * P:(u + 1) * P], agg[:, s, u, 0:C], S.ident[:])
                        t.then_inc(agg_turned, 1)
                        pe.wait_ge(agg_out, done(q))
                        pe.wait_ge(counted, behind(q))
                        for u in range(U):
                            t = pe.matmul(ps_p[:, u * P:(u + 1) * P], agg_t[:, s, u * P:(u + 1) * P], w[:, 0, :],
                                          start=True, stop=True)
                        t.then_inc(pre_ready, 1)
                for s in range(SLOTS):
                    q = i * SLOTS + s
                    r.wait_loads(pe, i, s, 1 if dense else 0, 0 if dense else 1)
                    pe.wait_ge(turned_out, behind(q))
                    for u in range(U):
                        t = pe.transpose(ps_t[:, u * P:(u + 1) * P], x[:, s, u, :], S.ident[:])
                    t.then_inc(turned, 1)
                if not dense:
                    for s in range(SLOTS):
                        q = i * SLOTS + s
                        pe.wait_ge(counted, done(q))
                        pe.wait_ge(pre_out, behind(q))
                        for u in range(U):
                            t = pe.transpose(ps_1[:, u * P:(u + 1) * P], pre[:, s, u, :], S.ident[:])
                        t.then_inc(pre_turned, 1)
                        pe.wait_ge(pre_out, done(q))
                        pe.wait_ge(relued, behind(q))
                        pe.matmul(ps_1[:], w[:, 1, :], agg_t[:, s], start=True, stop=True).then_inc(layer1, 1)
                        pe.wait_ge(relued, done(q))
                        pe.wait_ge(biased, behind(q))
                        for u in range(U):
                            t = pe.matmul(ps_2[:, u * P:(u + 1) * P], hid[:, s, u * P:(u + 1) * P], w[:, 2, :],
                                          start=True, stop=True)
                        t.then_inc(layer2, 1)
                for s in range(SLOTS):
                    q = i * SLOTS + s
                    pe.wait_ge(turned_out, done(q))
                    pe.wait_ge(ln.z_ready, behind(q))
                    for u in range(U):
                        t = pe.matmul(ps_o[:, u * P:(u + 1) * P], turned_t[:, s, u * P:(u + 1) * P], w[:, 0, :],
                                      start=True, stop=True)
                    t.then_inc(own_h, 1)

        @block.scalar
        def _(act):
            act.wait_ge(r.weights, 16 * 8)
            act.wait_ge(ln.eps_set, 1)
            act.wait_ge(ln2.eps_set, 1)
            with act.Fori(0, r.iters) as i:
                if not dense:
                    for s in range(SLOTS):
                        q = i * SLOTS + s
                        act.wait_ge(agg_turned, done(q))
                        act.activation(agg_t[:, s], ps_g[:], ACT.Copy).then_inc(agg_out, 1)
                for s in range(SLOTS):
                    q = i * SLOTS + s
                    act.wait_ge(turned, done(q))
                    act.activation(turned_t[:, s], ps_t[:], ACT.Copy).then_inc(turned_out, 1)
                if not dense:
                    for s in range(SLOTS):
                        q = i * SLOTS + s
                        act.wait_ge(pre_turned, done(q))
                        act.activation(agg_t[:, s], ps_1[:], ACT.Copy).then_inc(pre_out, 1)
                        act.wait_ge(layer1, done(q))
                        act.activation(hid[:, s], ps_1[:], ACT.Relu, bias=b1[:]).then_inc(relued, 1)
                ln.deviation(act, i)
                ln2.deviation(act, i)

        @block.vector
        def _(dve):
            ln.setup(dve)
            ln2.setup(dve)
            dve.wait_ge(r.weights, 16 * 8)
            with dve.Fori(0, r.iters) as i:
                for s in range(SLOTS):
                    dve.wait_ge(r.ready, free(i * SLOTS + s))
                if not dense:
                    for s in range(SLOTS):
                        q = i * SLOTS + s
                        dve.wait_ge(pre_ready, done(q))
                        for u in range(U):
                            t = dve.scalar_tensor_tensor(pre[:, s, u, :], rows[:, 0, :], agg[:, s, u, C:C + 1],
                                                         ps_p[:, u * P:(u + 1) * P], ALU.mult, ALU.add)
                        t.then_inc(counted, 1)
                        dve.wait_ge(counted, done(q))
                        dve.sem_inc(r.used, 1)
                    for s in range(SLOTS):
                        q = i * SLOTS + s
                        dve.wait_ge(layer2, done(q))
                        dve.tensor_tensor(add[:, s], ps_2[:].rearrange("p (u c) -> p u c", u=U),
                                          bc_rows(rows[:, 1, :]), ALU.add).then_inc(biased, 1)
                    for s in range(SLOTS):
                        q = i * SLOTS + s
                        dve.wait_ge(biased, done(q))
                        for u in range(U):
                            t = dve.scalar_tensor_tensor(add[:, s, u, :], add[:, s, u, :], 0.0, rows[:, 0, :],
                                                         ALU.max, ALU.add)
                        t.then_inc(added, 1)
                for s in range(SLOTS):
                    q = i * SLOTS + s
                    dve.wait_ge(own_h, done(q))
                    if not dense:
                        dve.wait_ge(added, done(q))
                    dve.tensor_tensor(z[:, s], ps_o[:].rearrange("p (u c) -> p u c", u=U),
                                      bc_rows(S.c2[:]) if dense else add[:, s], ALU.add).then_inc(ln.z_ready, 1)
                ln.moments(dve, i, z, r.tick)
                ln.scale(dve, i, z, y, normed, None)
                for s in range(SLOTS):
                    q = i * SLOTS + s
                    dve.wait_ge(normed, done(q))
                    dve.tensor_tensor(z[:, s], y[:, s], bc_rows(rows[:, 2, :]), ALU.mult).then_inc(gained, 1)
                for s in range(SLOTS):
                    q = i * SLOTS + s
                    dve.wait_ge(gained, done(q))
                    dve.tensor_tensor(y[:, s], z[:, s], bc_rows(rows[:, 3, :]), ALU.add).then_inc(f.beta_in, 1)
                for s in range(SLOTS):
                    q = i * SLOTS + s
                    dve.wait_ge(f.beta_in, q + 1)
                    dve.tensor_tensor(z[:, s], y[:, s], x[:, s], ALU.add).then_inc(ln2.z_ready, 1)
                    if dense:
                        dve.wait_ge(ln2.z_ready, done(q))
                        dve.sem_inc(r.used, 1)
                ln2.moments(dve, i, z, r.tick)
                ln2.scale(dve, i, z, res, r.ready, r.out_free)


class Softplus:

    def __init__(self, f, name):
        self.absx = f.sb(f"absx{name}", [P, SLOTS, U * P])
        self.lg = f.sb(f"lg{name}", [P, SLOTS, U * P])
        self.abs_ready, self.exp_ready, self.log_ready = (f.sem(f"{n}{name}") for n in (
            "abs_ready", "exp_ready", "log_ready"))
        self.sems = [self.abs_ready, self.exp_ready, self.log_ready]

    def scalar(self, act, i, x, x_ready, used, one, bias=None, single=True):
        for s in range(SLOTS):
            q = i * SLOTS + s
            act.wait_ge(x_ready, done(q))
            act.wait_ge(self.log_ready, free(q))
            if bias is None:
                act.activation(self.absx[:, s], x(s), ACT.Abs).then_inc(self.abs_ready, 1)
            else:
                act.activation(self.absx[:, s], x(s), ACT.Abs, bias=bias).then_inc(self.abs_ready, 1)
        for s in range(SLOTS):
            q = i * SLOTS + s
            act.wait_ge(self.abs_ready, done(q))
            act.activation(self.absx[:, s], self.absx[:, s], ACT.Exp, scale=-1.0).then_inc(self.exp_ready, 1)
        for s in range(SLOTS):
            q = i * SLOTS + s
            act.wait_ge(self.exp_ready, done(q))
            act.wait_ge(used, free(q))
            act.activation(self.lg[:, s], self.absx[:, s], ACT.Ln, bias=one).then_inc(self.log_ready, 1)


def messages(nc, T, A, S):
    with Phase(nc, "messages") as f:
        r = Rows(f, S, dense=True, stores=1, groups=EDGE_GROUPS)
        e = f.sb("e", [P, SLOTS, U, C])
        x = f.sb("x", [P, SLOTS, U, C])
        e_t = f.sb("e_t", [P, SLOTS, U * P])
        x_t = f.sb("x_t", [P, SLOTS, U * P])
        w = f.sb("w", [P, 3, C])
        rows = f.sb("rows", [P, 2, C])
        be1 = f.sb("be1", [P, 1])
        one = f.sb("one", [P, 1])
        pos = f.sb("pos", [P, SLOTS, U * P])
        act1 = f.sb("act1", [P, SLOTS, U * P])
        y = f.sb("y", [P, SLOTS, U, C])
        filt = f.sb("filt", [P, SLOTS, U, C])
        hn = f.sb("hn", [P, SLOTS, U, C])
        res = f.sb("res", [P, SLOTS, U, C])
        ps_e = f.ps("ps_e", [P, U * P])
        ps_x = f.ps("ps_x", [P, U * P])
        ps_1 = [f.ps(f"ps_1{s}", [P, U * P]) for s in range(SLOTS)]
        ps_2 = f.ps("ps_2", [P, U * P])
        ps_n = f.ps("ps_n", [P, U * P])
        sp1, sp2 = Softplus(f, "1"), Softplus(f, "2")
        x_used, e_out, x_out, layer1, clipped, act1_ready, layer2, y_ready, node, hn_ready, filt_ready, one_set = (
            f.sem(n) for n in ("x_used", "e_out", "x_out", "layer1", "clipped", "act1_ready", "layer2", "y_ready",
                               "node", "hn_ready", "filt_ready", "one_set"))
        block = f.block()

        @block.sync
        def _(sp):
            for out, src in ((w[:, 0, :], A["L3_We1T"]), (w[:, 1, :], A["L3_We2T"]), (w[:, 2, :], A["L3_WnT"]),
                             (rows[:, 0, :], A["L3_be2_rows"]), (rows[:, 1, :], A["L3_bn_rows"]),
                             (be1[:], A["L3_be1_col"])):
                sp.dma_start(out, src).then_inc(r.weights, 16)
            r.prime(sp, (x_used, e_out, x_out, layer1, clipped, act1_ready, layer2, y_ready, node, hn_ready,
                         filt_ready, *sp1.sems, *sp2.sems))
            r.load(sp, [(e, groups_of(A["edge_attr"]))])
            r.finish(sp)

        @block.gpsimd
        def _(pool):
            r.pool_loop(pool, gathers=[(x, T["X3"], SRCO, x_used)], stores=[(res, groups_of(T["M"]))])

        @block.tensor
        def _(pe):
            pe.wait_ge(r.weights, 16 * 6)
            with pe.Fori(0, r.iters) as i:
                for s in range(SLOTS):
                    q = i * SLOTS + s
                    r.wait_loads(pe, i, s, 1)
                    pe.wait_ge(e_out, behind(q))
                    for u in range(U):
                        t = pe.transpose(ps_e[:, u * P:(u + 1) * P], e[:, s, u, :], S.ident[:])
                    t.then_inc(r.used, 1)
                for s in range(SLOTS):
                    q = i * SLOTS + s
                    pe.wait_ge(e_out, done(q))
                    pe.wait_ge(clipped, free(q))
                    pe.wait_ge(sp1.abs_ready, free(q))
                    pe.matmul(ps_1[s][:], w[:, 0, :], e_t[:, s], start=True, stop=True).then_inc(layer1, 1)
                for s in range(SLOTS):
                    q = i * SLOTS + s
                    r.wait_loads(pe, i, s, 0, 1)
                    pe.wait_ge(x_out, behind(q))
                    for u in range(U):
                        t = pe.transpose(ps_x[:, u * P:(u + 1) * P], x[:, s, u, :], S.ident[:])
                    t.then_inc(x_used, 1)
                for s in range(SLOTS):
                    q = i * SLOTS + s
                    pe.wait_ge(x_out, done(q))
                    pe.wait_ge(hn_ready, behind(q))
                    for u in range(U):
                        t = pe.matmul(ps_n[:, u * P:(u + 1) * P], x_t[:, s, u * P:(u + 1) * P], w[:, 2, :],
                                      start=True, stop=True)
                    t.then_inc(node, 1)
                for s in range(SLOTS):
                    q = i * SLOTS + s
                    pe.wait_ge(act1_ready, done(q))
                    pe.wait_ge(y_ready, behind(q))
                    for u in range(U):
                        t = pe.matmul(ps_2[:, u * P:(u + 1) * P], act1[:, s, u * P:(u + 1) * P], w[:, 1, :],
                                      start=True, stop=True)
                    t.then_inc(layer2, 1)

        @block.scalar
        def _(act):
            act.wait_ge(r.weights, 16 * 6)
            act.wait_ge(one_set, 1)
            with act.Fori(0, r.iters) as i:
                for s in range(SLOTS):
                    q = i * SLOTS + s
                    act.wait_ge(r.used, done(q))
                    act.wait_ge(layer1, free(q))
                    act.activation(e_t[:, s], ps_e[:], ACT.Copy).then_inc(e_out, 1)
                for s in range(SLOTS):
                    q = i * SLOTS + s
                    act.wait_ge(x_used, done(q))
                    act.wait_ge(node, free(q))
                    act.activation(x_t[:, s], ps_x[:], ACT.Copy).then_inc(x_out, 1)
                sp1.scalar(act, i, lambda s: ps_1[s][:], clipped, act1_ready, one[:], bias=be1[:])
                sp2.scalar(act, i, lambda s: y[:, s].rearrange("p u c -> p (u c)"), y_ready, filt_ready, one[:])

        @block.vector
        def _(dve):
            dve.memset(one[:], 1.0).then_inc(one_set, 1)
            dve.wait_ge(r.weights, 16 * 6)
            with dve.Fori(0, r.iters) as i:
                for s in range(SLOTS):
                    dve.wait_ge(r.ready, free(i * SLOTS + s))
                for s in range(SLOTS):
                    q = i * SLOTS + s
                    dve.wait_ge(layer1, done(q))
                    dve.tensor_scalar(pos[:, s], ps_1[s][:], be1[:], 0.0, ALU.add, ALU.max).then_inc(clipped, 1)
                for s in range(SLOTS):
                    q = i * SLOTS + s
                    dve.wait_ge(node, done(q))
                    dve.tensor_tensor(hn[:, s], ps_n[:].rearrange("p (u c) -> p u c", u=U), bc_rows(rows[:, 1, :]),
                                      ALU.add).then_inc(hn_ready, 1)
                for s in range(SLOTS):
                    q = i * SLOTS + s
                    dve.wait_ge(sp1.log_ready, done(q))
                    dve.wait_ge(clipped, done(q))
                    dve.wait_ge(layer2, free(q))
                    dve.scalar_tensor_tensor(act1[:, s], sp1.lg[:, s], -LOG2, pos[:, s], ALU.add, ALU.add
                                             ).then_inc(act1_ready, 1)
                for s in range(SLOTS):
                    q = i * SLOTS + s
                    dve.wait_ge(layer2, done(q))
                    dve.wait_ge(sp2.abs_ready, free(q))
                    dve.tensor_tensor(y[:, s], ps_2[:].rearrange("p (u c) -> p u c", u=U), bc_rows(rows[:, 0, :]),
                                      ALU.add).then_inc(y_ready, 1)
                for s in range(SLOTS):
                    q = i * SLOTS + s
                    dve.wait_ge(sp2.log_ready, done(q))
                    dve.scalar_tensor_tensor(filt[:, s].rearrange("p u c -> p (u c)"),
                                             y[:, s].rearrange("p u c -> p (u c)"), 0.0, sp2.lg[:, s],
                                             ALU.max, ALU.add).then_inc(filt_ready, 1)
                for s in range(SLOTS):
                    q = i * SLOTS + s
                    dve.wait_ge(filt_ready, done(q))
                    dve.wait_ge(hn_ready, done(q))
                    r.out_free(dve, i, s)
                    dve.scalar_tensor_tensor(res[:, s].rearrange("p u c -> p (u c)"),
                                             filt[:, s].rearrange("p u c -> p (u c)"), -LOG2,
                                             hn[:, s].rearrange("p u c -> p (u c)"), ALU.add, ALU.mult
                                             ).then_inc(r.ready, 1)


def schnet_rows(nc, T, A, S, out):
    with Phase(nc, "schnet") as f:
        r = Rows(f, S, dense=False, stores=U)
        agg = f.sb("agg", [P, SLOTS, U, C])
        own = f.sb("own", [P, SLOTS, U, C])
        agg_t = f.sb("agg_t", [P, SLOTS, U * P])
        w = f.sb("w", [P, 2, C])
        brow = f.sb("brow", [P, C])
        b1 = f.sb("b1", [P, 1])
        one = f.sb("one", [P, 1])
        pos = f.sb("pos", [P, SLOTS, U * P])
        hid = f.sb("hid", [P, SLOTS, U * P])
        z = f.sb("z", [P, SLOTS, U, C])
        res = f.sb("res", [P, SLOTS, U, C])
        ps_t = f.ps("ps_t", [P, U * P])
        ps_1 = [f.ps(f"ps_1{s}", [P, U * P]) for s in range(SLOTS)]
        ps_2 = f.ps("ps_2", [P, U * P])
        sp1 = Softplus(f, "1")
        ln = LayerNorm(f)
        agg_out, layer1, clipped, hid_ready, layer2, owned, one_set = (f.sem(n) for n in (
            "agg_out", "layer1", "clipped", "hid_ready", "layer2", "owned", "one_set"))
        block = f.block()

        @block.sync
        def _(sp):
            for dst, src in ((w[:, 0, :], A["L3_Wfc1T"]), (w[:, 1, :], A["L3_Wfc2T"]),
                             (brow[:], A["L3_bfc2_rows"]), (b1[:], A["L3_bfc1_col"])):
                sp.dma_start(dst, src).then_inc(r.weights, 16)
            r.prime(sp, (agg_out, layer1, clipped, hid_ready, layer2, owned, *sp1.sems, *ln.sems))
            r.load(sp, [(agg, groups_of(T["RAW128"]))])
            r.finish(sp)

        @block.gpsimd
        def _(pool):
            r.pool_loop(pool, gathers=[(own, T["X3"], DST, owned)], scatters=[(res, out, SCD, NP_)])

        @block.tensor
        def _(pe):
            pe.wait_ge(r.weights, 16 * 4)
            with pe.Fori(0, r.iters) as i:
                for s in range(SLOTS):
                    q = i * SLOTS + s
                    r.wait_loads(pe, i, s, 1)
                    pe.wait_ge(agg_out, behind(q))
                    for u in range(U):
                        t = pe.transpose(ps_t[:, u * P:(u + 1) * P], agg[:, s, u, :], S.ident[:])
                    t.then_inc(r.used, 1)
                for s in range(SLOTS):
                    q = i * SLOTS + s
                    pe.wait_ge(agg_out, done(q))
                    pe.wait_ge(clipped, free(q))
                    pe.wait_ge(sp1.abs_ready, free(q))
                    pe.matmul(ps_1[s][:], w[:, 0, :], agg_t[:, s], start=True, stop=True).then_inc(layer1, 1)
                for s in range(SLOTS):
                    q = i * SLOTS + s
                    pe.wait_ge(hid_ready, done(q))
                    pe.wait_ge(owned, behind(q))
                    for u in range(U):
                        t = pe.matmul(ps_2[:, u * P:(u + 1) * P], hid[:, s, u * P:(u + 1) * P], w[:, 1, :],
                                      start=True, stop=True)
                    t.then_inc(layer2, 1)

        @block.scalar
        def _(act):
            act.wait_ge(r.weights, 16 * 4)
            act.wait_ge(one_set, 1)
            act.wait_ge(ln.eps_set, 1)
            with act.Fori(0, r.iters) as i:
                for s in range(SLOTS):
                    q = i * SLOTS + s
                    act.wait_ge(r.used, done(q))
                    act.wait_ge(layer1, free(q))
                    act.activation(agg_t[:, s], ps_t[:], ACT.Copy).then_inc(agg_out, 1)
                sp1.scalar(act, i, lambda s: ps_1[s][:], clipped, hid_ready, one[:], bias=b1[:])
                ln.deviation(act, i)

        @block.vector
        def _(dve):
            ln.setup(dve)
            dve.memset(one[:], 1.0).then_inc(one_set, 1)
            dve.wait_ge(r.weights, 16 * 4)
            with dve.Fori(0, r.iters) as i:
                for s in range(SLOTS):
                    dve.wait_ge(r.ready, free(i * SLOTS + s))
                for s in range(SLOTS):
                    q = i * SLOTS + s
                    dve.wait_ge(layer1, done(q))
                    dve.tensor_scalar(pos[:, s], ps_1[s][:], b1[:], 0.0, ALU.add, ALU.max).then_inc(clipped, 1)
                for s in range(SLOTS):
                    q = i * SLOTS + s
                    dve.wait_ge(sp1.log_ready, done(q))
                    dve.wait_ge(clipped, done(q))
                    dve.wait_ge(layer2, free(q))
                    dve.scalar_tensor_tensor(hid[:, s], sp1.lg[:, s], -LOG2, pos[:, s], ALU.add, ALU.add
                                             ).then_inc(hid_ready, 1)
                for s in range(SLOTS):
                    q = i * SLOTS + s
                    dve.wait_ge(layer2, done(q))
                    r.wait_loads(dve, i, s, 0, 1)
                    dve.tensor_tensor(z[:, s], ps_2[:].rearrange("p (u c) -> p u c", u=U), own[:, s], ALU.add
                                      ).then_inc(owned, 1)
                for s in range(SLOTS):
                    q = i * SLOTS + s
                    dve.wait_ge(owned, done(q))
                    dve.tensor_tensor(z[:, s], z[:, s], bc_rows(brow[:]), ALU.add).then_inc(ln.z_ready, 1)
                ln.moments(dve, i, z, r.tick)
                ln.scale(dve, i, z, res, r.ready, r.out_free)



SCRATCH = {"sorted": (P, 3 * SORT_F), "keys": (2, SORT_N + 2), "last": (2, 2 * P), "ends": (HEADS, 2 * EDGE_TILES),
           "E": (N_HYPER, C), "X1": (NP_, C), "AA": (NP_, 2 * HEADS), "H2": (NP_, H2W),
           "X2": (NP_, C), "X3": (NP_, C), "M": (EP, C),
           "RAW129": (EP, C + 1), "RAW128": (EP, C), "RAW260": (EP, HC + HEADS)}


def build(nc, A, out, upto=None):
    T = {n: nc.dram_tensor(n, s, F32, kind="Internal").ap() for n, s in SCRATCH.items()}
    raw = T["RAW129"]
    with ExitStack() as ctx:
        S = Tables(nc, ctx, A["ident"])
        sort_phase(nc, T, A)
        index_phase(nc, T, A, S)
        if upto == "index":
            return T
        weights_phase(nc, A, S)
        hw_phase(nc, T, A, S)
        plain_norm(nc, S, "x1", [A["x"]], S.b0[:], T["X1"])
        sum_pass(nc, T, S, "e1", 0, A["x"], SRC, C + 1, raw, "ones")
        fix_pass(nc, S, "e1fix", 0, raw, C + 1)
        hyper_rows(nc, T, S, "e1rows", raw, T["E"], affine=False)
        sum_pass(nc, T, S, "n1", 1, T["E"], HYP, C + 1, raw, "hw")
        fix_pass(nc, S, "n1fix", 1, raw, C + 1)
        node_rows(nc, T, A, S, "n1rows", raw, 1)
        batch_norm(nc, A, S)
        if upto == "bn":
            return T
        sum_pass(nc, T, S, "e2", 0, T["X1"], SRC, C + 1, raw, "ones")
        fix_pass(nc, S, "e2fix", 0, raw, C + 1)
        hyper_rows(nc, T, S, "e2rows", raw, T["E"], affine=True)
        sum_pass(nc, T, S, "n2", 1, T["E"], HYP, C + 1, raw, "hw")
        fix_pass(nc, S, "n2fix", 1, raw, C + 1)
        node_rows(nc, T, A, S, "n2rows", raw, 2)
        if upto == "x1":
            return T
        gat_rows(nc, T, S, "gat1dense", dense=True)
        attention_phase(nc, T, S, "att1", HEADS, T["AA"], 1, 0)
        gat_sum(nc, T, S, "gat1sum", 1)
        fix_pass(nc, S, "gat1fix", 0, T["RAW260"], HC + HEADS)
        gat_rows(nc, T, S, "gat1rows", dense=False)
        if upto == "h2":
            return T
        attention_phase(nc, T, S, "att2", 1, T["H2"].rearrange("n (k c) -> (n k) c", c=4), H2W // 4, C // 4)
        gat_sum(nc, T, S, "gat2sum", 2)
        fix_pass(nc, S, "gat2fix", 0, raw, C + 1)
        plain_norm(nc, S, "x2", [T["X1"], T["H2"]], S.b2[:], T["X2"])
        gat_nodes(nc, T, S)
        if upto == "x2":
            return T
        sum_pass(nc, T, S, "gin", 0, T["X2"], SRC, C + 1, raw, "ones")
        fix_pass(nc, S, "ginfix", 0, raw, C + 1)
        gin_rows(nc, T, A, S, "gindense", dense=True)
        gin_rows(nc, T, A, S, "ginrows", dense=False)
        if upto == "x3":
            return T
        messages(nc, T, A, S)
        sum_pass(nc, T, S, "sch", 0, T["M"], PERM, C, T["RAW128"])
        fix_pass(nc, S, "schfix", 0, T["RAW128"], C)
        plain_norm(nc, S, "x4", [T["X3"]], S.c3[:], out)
        schnet_rows(nc, T, A, S, out)
    return T


def lay_out(inputs):
    import numpy as np

    a = {k: np.asarray(v) for k, v in inputs.items()}

    def padded(x, rows, fill=0):
        out = np.full((rows, *x.shape[1:]), fill, x.dtype)
        out[:len(x)] = x
        return out

    def rows(x):
        return np.ascontiguousarray(np.broadcast_to(x.reshape(1, -1), (P, x.size)))

    def turned(x):
        return np.ascontiguousarray(x.T)

    src, dst = a["src"].astype(np.int32), a["dst"].astype(np.int32)
    src_p, dst_p = padded(src, SORT_N, N_NODES), padded(dst, SORT_N, N_NODES)
    out = dict(constants())
    out.update(
        x=padded(a["x"], NP_), edge_attr=padded(a["edge_attr_128"], EP),
        src=src_p.reshape(P, SORT_F), dst=dst_p.reshape(P, SORT_F),
        src_cols=turned(src_p[:EP].reshape(EDGE_TILES, P)),
        hw=np.ascontiguousarray(a["L0_gnn_hyperedge_weight"].reshape(-1, 1)),
        L0_W1T=turned(a["L0_gnn_W1"]), L0_W2T=turned(a["L0_gnn_W2"]),
        L0_b1_rows=rows(a["L0_gnn_b1"]), L0_gamma_rows=rows(a["L0_gnn_gamma"]),
        L0_beta_rows=rows(a["L0_gnn_beta"]), L0_b2_rows=rows(a["L0_gnn_b2"]),
        L1_W1=a["L1_gnn_W1"], L1_W2=np.ascontiguousarray(a["L1_gnn_W2"].reshape(2, P, C).transpose(1, 0, 2)),
        L1_b1_cols=turned(a["L1_gnn_b1"].reshape(2, P)),
        L1_as1=rows(a["L1_gnn_att_src1"]), L1_ad1=rows(a["L1_gnn_att_dst1"]),
        L1_as2=rows(a["L1_gnn_att_src2"]), L1_ad2=rows(a["L1_gnn_att_dst2"]), L1_b2_rows=rows(a["L1_gnn_b2"]),
        L2_Wpre=a["L2_gnn_W_pre"], L2_W1=a["L2_gnn_W1"], L2_W2=a["L2_gnn_W2"],
        L2_b1_col=np.ascontiguousarray(a["L2_gnn_b1"].reshape(-1, 1)),
        L2_b2_rows=rows(a["L2_gnn_b2"]), L2_bpre_rows=rows(a["L2_gnn_b_pre"]),
        L2_gamma_rows=rows(a["L2_gnn_gamma"]), L2_beta_rows=rows(a["L2_gnn_beta"]),
        L3_WnT=turned(a["L3_gnn_W_node"]), L3_bn_rows=rows(a["L3_gnn_b_node"]),
        L3_We1T=turned(a["L3_gnn_W_e1"]), L3_be1_col=np.ascontiguousarray(a["L3_gnn_b_e1"].reshape(-1, 1)),
        L3_We2T=turned(a["L3_gnn_W_e2"]), L3_be2_rows=rows(a["L3_gnn_b_e2"]),
        L3_Wfc1T=turned(a["L3_gnn_W_fc1"]), L3_bfc1_col=np.ascontiguousarray(a["L3_gnn_b_fc1"].reshape(-1, 1)),
        L3_Wfc2T=turned(a["L3_gnn_W_fc2"]), L3_bfc2_rows=rows(a["L3_gnn_b_fc2"]),
    )
    return out


def kernel(**inputs):
    import numpy as np
    import concourse.bacc as bacc
    from concourse.bass_utils import run_bass_kernel_spmd

    nc = bacc.Bacc("TRN2", target_bir_lowering=False, num_devices=1)
    arrays = {f"in_{n}": x for n, x in lay_out(inputs).items()}
    A = {n[3:]: nc.dram_tensor(n, x.shape, mybir.dt.from_np(x.dtype), kind="ExternalInput").ap()
         for n, x in arrays.items()}
    out = nc.dram_tensor("out", (NP_, C), F32, kind="ExternalOutput").ap()
    build(nc, A, out)
    ran = run_bass_kernel_spmd(nc, [arrays], core_ids=[0])
    return np.asarray(ran.results[0]["out"])[:N_NODES]
```

```python
from contextlib import ExitStack

import concourse.bass as bass
from concourse import mybir

F32 = mybir.dt.float32
I32 = mybir.dt.int32
ALU = mybir.AluOpType
ACT = mybir.ActivationFunctionType
AX_X = mybir.AxisListType.X

P = 128
N_NODES = 50000
N_HYPER = 10000
C = 128
HEADS = 4
HID = 64
HC = HEADS * HID
TILES_PER_GROUP = U = 4
SLOTS = 4
NP_ = 53248
NODE_GROUPS = NP_ // (P * U)
EDGE_TILES = 208
EDGE_GROUPS = EDGE_TILES // U
EP = EDGE_TILES * P
SORT_F = 256
SORT_N = P * SORT_F
HALF_T = EDGE_TILES // 2
H2W = 132
SKIP = 1000000.0
NEG = -1.0e30
SLOPE = 0.2
EPS = 1e-5
LOG2 = 0.6931471805599453
SPLIT = 17664
ENC_NEG = float(0x8000 + SPLIT)
ENC_ADD = float(0x80 - SPLIT)


def done(q):
    return q + 1 + SLOTS


def behind(q):
    return q + SLOTS


def two_behind(q):
    return q + SLOTS - 1


def free(q):
    return q + 1


class Phase:

    def __init__(self, nc, name):
        self.nc, self.name, self.ctx, self.own_sems = nc, name, ExitStack(), []

    def __enter__(self):
        self.ctx.__enter__()
        return self

    def __exit__(self, *a):
        self.ctx.__exit__(*a)
        self.nc.clear_and_free_semaphores(self.own_sems)
        self.nc.all_engine_barrier()

    def sb(self, name, shape, dt=F32):
        return self.ctx.enter_context(self.nc.sbuf_tensor(f"{self.name}_{name}", shape, dt))

    def ps(self, name, shape):
        return self.ctx.enter_context(self.nc.psum_tensor(f"{self.name}_{name}", shape, F32))

    def sem(self, name):
        self.own_sems.append(self.nc.alloc_semaphore(f"{self.name}_{name}"))
        return self.own_sems[-1]

    def sems(self, name, n=SLOTS):
        return [self.sem(f"{name}{i}") for i in range(n)]

    def block(self):
        return self.ctx.enter_context(self.nc.Block())


def groups_of(table, g0=0):
    return table.rearrange("(g u p) w -> g p u w", u=U, p=P)


def prime_stores(f, stored, n, ident, name="spare"):
    spare = f.sb(name, [1, SLOTS, 16])

    def issue(eng):
        for s in range(SLOTS):
            eng.dma_start(spare[:, s, :], ident[0:1, 0:16]).then_inc(stored[s], 16 * n)
    return issue


def gather(pool, out, table, index):
    return pool.indirect_dma_start(out, None, table, bass.IndirectOffsetOnAxis(ap=index, axis=0))


def scatter(pool, table, index, rows, values):
    return pool.indirect_dma_start(table, bass.IndirectOffsetOnAxis(ap=index, axis=0), values, None,
                                   bounds_check=rows - 1, oob_is_err=False)


def sort_phase(nc, T, A):
    with Phase(nc, "sort") as f:
        raw = f.sb("raw", [P, 3, SORT_F], I32)
        keyf = f.sb("keyf", [P, 2, SORT_F])
        offs = f.sb("offs", [P, 2, SORT_F])
        top = f.sb("top", [P, 2, SORT_F], I32)
        words = f.sb("words", [P, 2, 3 * SORT_F])
        signs = f.sb("signs", [P, 8, SORT_F])
        signs_t = f.sb("signs_t", [P, 7, P])
        ident = f.sb("ident", [P, P])
        turned = f.ps("turned", [P, 2, 512])
        loaded, stage, turn, out = f.sem("loaded"), f.sem("stage"), f.sem("turn"), f.sem("out")
        block = f.block()
        turns = []

        @block.sync
        def _(sp):
            sp.dma_start(raw[:, 0, :], A["dst"]).then_inc(loaded, 16)
            sp.dma_start(raw[:, 1, :], A["src"]).then_inc(loaded, 16)
            sp.dma_start(raw[:, 2, :], A["edge_no"]).then_inc(loaded, 16)
            sp.dma_start(signs[:], A["sort_signs"]).then_inc(loaded, 16)
            sp.dma_start(signs_t[:], A["sort_signs_t"]).then_inc(loaded, 16)
            sp.dma_start(ident[:], A["ident"]).then_inc(loaded, 16)

        @block.vector
        def _(dve):
            n = 0

            def step(*ins):
                nonlocal n
                for x in ins:
                    x.then_inc(stage, 1)
                n += len(ins)
                dve.wait_ge(stage, n)

            dve.wait_ge(loaded, 96)
            step(dve.tensor_copy(keyf[:], raw[:, 0:2, :]))
            step(dve.tensor_scalar(offs[:], keyf[:], float(SPLIT), ENC_NEG, ALU.is_lt, ALU.mult))
            step(dve.scalar_tensor_tensor(top[:], keyf[:], ENC_ADD, offs[:], ALU.add, ALU.add))
            w0 = words[:, 0, :].bitcast(I32).rearrange("p (a f) -> p a f", a=3)
            step(*[dve.scalar_tensor_tensor(w0[:, a, :], top[:, k, :], 16, raw[:, pay, :],
                                            ALU.logical_shift_left, ALU.bitwise_or)
                   for a, k, pay in ((0, 0, 2), (1, 0, 1), (2, 1, 0))])
            cur = 0

            def compare(d):
                nonlocal cur
                a = words[:, cur, :].rearrange("p (g t d) -> p g t d", t=2, d=d)
                b = words[:, 1 - cur, :].rearrange("p (g t d) -> p g t d", t=2, d=d)
                step(dve.tensor_tensor(b[:, :, 0, :], a[:, :, 0, :], a[:, :, 1, :], ALU.min),
                     dve.tensor_tensor(b[:, :, 1, :], a[:, :, 0, :], a[:, :, 1, :], ALU.max))
                cur = 1 - cur

            turn_no = 0

            def turn_over(mask):
                nonlocal turn_no, cur
                turns.append((cur, n))
                turn_no += 1
                dve.wait_ge(turn, turn_no)
                new = words[:, 1 - cur, :]
                if mask is None:
                    step(dve.tensor_copy(new[:, 0:512], turned[:, 0, :]),
                         dve.tensor_copy(new[:, 512:768], turned[:, 1, 0:256]))
                else:
                    m = mask.unsqueeze(1)
                    step(dve.tensor_tensor(new[:, 0:512].rearrange("p (a q) -> p a q", q=P),
                                           turned[:, 0, :].rearrange("p (a q) -> p a q", q=P),
                                           m.to_broadcast([P, 4, P]), ALU.mult),
                         dve.tensor_tensor(new[:, 512:768].rearrange("p (a q) -> p a q", q=P),
                                           turned[:, 1, 0:256].rearrange("p (a q) -> p a q", q=P),
                                           m.to_broadcast([P, 2, P]), ALU.mult))
                cur = 1 - cur

            for level in range(1, 9):
                a = words[:, cur, :].rearrange("p (a f) -> p a f", a=3)
                b = words[:, 1 - cur, :].rearrange("p (a f) -> p a f", a=3)
                step(dve.tensor_tensor(b, a, signs[:, level - 1, :].unsqueeze(1).to_broadcast([P, 3, SORT_F]),
                                       ALU.mult))
                cur = 1 - cur
                for m in reversed(range(level)):
                    compare(1 << m)
            for level in range(9, 16):
                turn_over(signs_t[:, level - 9, :])
                for m in reversed(range(level - 8)):
                    compare(1 << m)
                turn_over(None)
                for m in reversed(range(8)):
                    compare(1 << m)
            f.final, f.final_n = cur, n

        @block.tensor
        def _(pe):
            for buf, n in turns:
                pe.wait_ge(stage, n)
                for b in range(6):
                    t = pe.transpose(turned[:, b // 4, (b % 4) * P:(b % 4 + 1) * P],
                                     words[:, buf, b * P:(b + 1) * P], ident[:])
                t.then_inc(turn, 1)

        @block.scalar
        def _(act):
            act.wait_ge(stage, f.final_n)
            act.dma_start(T["sorted"], words[:, f.final, :]).then_inc(out, 16)
            act.wait_ge(out, 16)


def constants():
    import numpy as np
    j = np.arange(SORT_N).reshape(P, SORT_F)

    def sgn(k):
        return np.where((j >> k) & 1, -1.0, 1.0) if k else np.ones(j.shape)

    full = [sgn(k) * sgn(k - 1) if k > 1 else sgn(1) for k in range(1, 16)]
    signs = np.stack(full[:8], 1).astype(np.float32)
    signs_t = np.broadcast_to(np.stack([m[:, 0] for m in full[8:]])[None], (P, 7, P)).astype(np.float32)
    return {
        "edge_no": j.astype(np.int32),
        "sort_signs": signs,
        "sort_signs_t": np.ascontiguousarray(signs_t),
        "ident": np.eye(P, dtype=np.float32),
        "is_last": (j % P == P - 1).astype(np.float32),
        "later": (np.arange(EDGE_TILES).reshape(2, HALF_T).T[:, :, None] > np.arange(EDGE_TILES)).astype(np.float32),
    }



KD, SF, KS, SM = range(4)
SRC, SCD, SCE, PERM, DST, HYP, SCS, NOD, SRCO = range(9)


class Tables:

    def __init__(self, nc, ctx, ident_dram):
        self.ident_dram = ident_dram

        def sb(name, shape, dt=F32):
            return ctx.enter_context(nc.sbuf_tensor(name, shape, dt))

        self.colf = sb("colf", [P, 4, EDGE_TILES])
        self.coli = sb("coli", [P, 9, EDGE_TILES], I32)
        self.joins = sb("joins", [HALF_T, 2, 2, EDGE_TILES])
        self.ident = sb("identity", [P, P])
        self.hw = sb("hw_col", [P, EDGE_TILES])
        self.ws = sb("w_src", [P, EDGE_TILES, HEADS])
        self.wd = sb("w_self", [P, EDGE_TILES, HEADS])
        self.wt = sb("w_total", [P, EDGE_TILES, HEADS])
        self.affine = sb("affine", [P, 2, C])
        self.affine_sums = sb("affine_sums", [P, 2, U * C])
        self.W1 = sb("W1", [P, HC])
        self.WA = sb("WA", [P, 2 * HEADS])
        self.W2x = sb("W2x", [P, 2, H2W])
        self.b1col = sb("b1col", [P, 2])
        self.b0 = sb("b0", [P, C])
        self.b2 = sb("b2", [P, C])
        self.c2 = sb("c2", [P, C])
        self.c3 = sb("c3", [P, C])


def index_phase(nc, T, A, S):
    with Phase(nc, "index") as f:
        words = f.sb("words", [P, 3, SORT_F], I32)
        bits = f.sb("bits", [P, 3, 2, SORT_F], I32)
        key = f.sb("key", [P, 3, SORT_F])
        off = f.sb("off", [P, 3, SORT_F])
        prv = f.sb("prv", [P, 2, SORT_F])
        nxt = f.sb("nxt", [P, 2, SORT_F])
        new = f.sb("new", [P, 2, SORT_F])
        rep = f.sb("rep", [P, 2, SORT_F])
        tmp = f.sb("tmp", [P, 2, SORT_F])
        is_last = f.sb("is_last", [P, SORT_F])
        arr = f.sb("arr", [P, 12, SORT_F])
        guard = f.sb("guard", [1, 2])
        zeros = f.sb("zeros", [80, 2000])
        later = f.sb("later", [HALF_T, 2, EDGE_TILES])
        last_row = f.sb("last_row", [HALF_T, 2, EDGE_TILES])
        first_col = f.sb("first_col", [HALF_T, 2, 2])
        eq = f.sb("eq", [HALF_T, 2, 2, EDGE_TILES])
        psT = f.ps("turned", [P, 4, 512])
        filled, loaded, stage, kept, back, tile_keys, turned = (f.sem(n) for n in (
            "filled", "loaded", "stage", "kept", "back", "tile_keys", "turned"))
        block = f.block()
        marks = {}

        @block.vector
        def _(dve):
            n = 0

            def step(*ins):
                nonlocal n
                for x in ins:
                    x.then_inc(stage, 1)
                n += len(ins)
                dve.wait_ge(stage, n)

            step(dve.memset(guard[:], -1.0), dve.memset(zeros[:], 0.0))
            marks["guard"] = n
            dve.wait_ge(loaded, 16 * 5)
            step(dve.tensor_scalar(bits[:, :, 0, :], words[:], 16, None, ALU.logical_shift_right),
                 dve.tensor_scalar(bits[:, :, 1, :], words[:], 0xFFFF, None, ALU.bitwise_and))
            step(dve.tensor_scalar(off[:], bits[:, :, 0, :], 32768.0, ENC_NEG, ALU.is_ge, ALU.mult))
            step(dve.scalar_tensor_tensor(key[:], bits[:, :, 0, :], -ENC_ADD, off[:], ALU.add, ALU.subtract))
            marks["key"] = n
            dve.wait_ge(back, 16 * 4)
            kk = key[:, 1:3, :]
            step(dve.tensor_tensor(new[:], kk, prv[:], ALU.not_equal),
                 dve.tensor_tensor(rep[:], kk, nxt[:], ALU.not_equal))
            step(dve.tensor_tensor(rep[:], rep[:], is_last[:].unsqueeze(1).to_broadcast([P, 2, SORT_F]), ALU.max))
            def tiles(x, o):
                return x[:, o, :].rearrange("p (h e) -> p h e", h=2)
            step(*[dve.tensor_tensor(tiles(tmp, o), tiles(key, o + 1),
                                     tiles(prv, o)[:, :, 0:1].to_broadcast([P, 2, P]), ALU.not_equal)
                   for o in range(2)])
            step(dve.tensor_tensor(rep[:], rep[:], tmp[:], ALU.mult))
            step(dve.tensor_copy(arr[:, 0, :], key[:, 1, :]),
                 dve.tensor_copy(arr[:, 1, :], new[:, 0, :]),
                 dve.tensor_copy(arr[:, 2, :], key[:, 2, :]),
                 dve.scalar_tensor_tensor(arr[:, 3, :], key[:, 2, :], float(N_NODES), rep[:, 1, :],
                                          ALU.is_lt, ALU.mult),
                 dve.tensor_copy(arr[:, 4, :], bits[:, 1, 1, :]),
                 dve.scalar_tensor_tensor(arr[:, 5, :], key[:, 1, :], -SKIP, rep[:, 0, :], ALU.add, ALU.mult),
                 dve.scalar_tensor_tensor(tmp[:, 0, :], key[:, 1, :], float(N_HYPER), rep[:, 0, :],
                                          ALU.is_lt, ALU.mult),
                 dve.tensor_copy(arr[:, 7, :], bits[:, 0, 1, :]),
                 dve.tensor_copy(arr[:, 8, :], key[:, 1, :]),
                 dve.tensor_scalar(arr[:, 9, :], bits[:, 2, 1, :], float(N_HYPER - 1), None, ALU.min),
                 dve.scalar_tensor_tensor(arr[:, 10, :], key[:, 2, :], -SKIP, rep[:, 1, :], ALU.add, ALU.mult),
                 dve.tensor_copy(arr[:, 11, :], key[:, 2, :]))
            step(dve.scalar_tensor_tensor(arr[:, 6, :], key[:, 1, :], -SKIP, tmp[:, 0, :], ALU.add, ALU.mult))
            step(*[dve.tensor_scalar(arr[:, a, :], arr[:, a, :], SKIP, None, ALU.add) for a in (5, 6, 10)])
            marks["arr"] = n
            dve.wait_ge(tile_keys, 16 * 4)
            for o in range(2):
                step(*[dve.tensor_scalar(eq[:, o, c, :], last_row[:, o, :], first_col[:, o, c:c + 1], None,
                                         ALU.is_equal) for c in range(2)])
            step(*[dve.tensor_tensor(S.joins[:, o, :, :], eq[:, o, :, :], later[:], ALU.mult)
                   for o in range(2)])
            for a in range(12):
                dve.wait_ge(turned, a + 1)
                col = S.colf[:, a, :] if a < 4 else S.coli[:, a - 4, :]
                dve.tensor_copy(col.rearrange("e (p h) -> e h p", h=2),
                                psT[:, a % 4, 0:2 * P].rearrange("e (h p) -> e h p", h=2)[:, :, 0:HALF_T]
                                ).then_inc(stage, 1)
            marks["columns"] = n

        @block.tensor
        def _(pe):
            pe.wait_ge(stage, marks["arr"])
            for a in range(12):
                if a >= 4:
                    pe.wait_ge(stage, marks["columns"] + a - 3)
                for h in range(2):
                    t = pe.transpose(psT[:, a % 4, h * P:(h + 1) * P], arr[:, a, h * P:(h + 1) * P], S.ident[:])
                t.then_inc(turned, 1)

        @block.sync
        def _(sp):
            sp.dma_start(words[:], T["sorted"].bitcast(I32).rearrange("p (a f) -> p a f", a=3)).then_inc(loaded, 16)
            sp.dma_start(is_last[:], A["is_last"]).then_inc(loaded, 16)
            sp.dma_start(later[:], A["later"]).then_inc(loaded, 16)
            sp.dma_start(S.coli[:, SRCO, :], A["src_cols"]).then_inc(loaded, 16)
            sp.dma_start(S.ident[:], A["ident"]).then_inc(loaded, 16)
            sp.wait_ge(stage, marks["guard"])
            e_rows = T["E"].rearrange("(p r) c -> p (r c)", p=80)
            for k in range(N_HYPER * C // (80 * 2000)):
                sp.dma_start(e_rows[:, k * 2000:(k + 1) * 2000], zeros[:]).then_inc(filled, 16)
            for o in range(2):
                sp.dma_start(T["keys"][o:o + 1, 0:1], guard[:, 0:1]).then_inc(kept, 16)
                sp.dma_start(T["keys"][o:o + 1, SORT_N + 1:SORT_N + 2], guard[:, 1:2]).then_inc(kept, 16)
            sp.wait_ge(stage, marks["key"])
            for o in range(2):
                sp.dma_start(T["keys"][o, 1:SORT_N + 1].rearrange("(p f) -> p f", p=P),
                             key[:, o + 1, :]).then_inc(kept, 16)
                with nc.allow_non_contiguous_dma(reason="two keys per partition"):
                    for h in range(2):
                        sp.dma_start(T["last"][o].rearrange("(p h) -> p h", h=2)[:, h:h + 1],
                                     key[:, o + 1, h * P + P - 1:h * P + P]).then_inc(kept, 16)
            sp.wait_ge(kept, 16 * 10)
            sp.wait_ge(filled, N_HYPER * C // (80 * 2000) * 16)
            for o in range(2):
                sp.dma_start(prv[:, o, :], T["keys"][o, 0:SORT_N].rearrange("(p f) -> p f", p=P)
                             ).then_inc(back, 16)
                sp.dma_start(nxt[:, o, :], T["keys"][o, 2:SORT_N + 2].rearrange("(p f) -> p f", p=P)
                             ).then_inc(back, 16)
            for o in range(2):
                sp.dma_start(last_row[:, o, :], T["last"][o:o + 1, 0:EDGE_TILES].to_broadcast([HALF_T, EDGE_TILES])
                             ).then_inc(tile_keys, 16)
                with nc.allow_non_contiguous_dma(reason="first key of each tile"):
                    sp.dma_start(first_col[:, o, :],
                                 T["keys"][o, 1:1 + EDGE_TILES * P].rearrange("(c p e) -> p c e", p=HALF_T, e=P)
                                 [:, :, 0]).then_inc(tile_keys, 16)


def hw_phase(nc, T, A, S):
    with Phase(nc, "hw") as f:
        slot = f.sb("slot", [P, SLOTS, U], I32)
        got = f.sb("got", [P, SLOTS, U])
        picked, copied, tick = f.sem("picked"), f.sem("copied"), f.sem("tick")
        gathered = f.sems("gathered")
        block = f.block()

        @block.gpsimd
        def _(pool):
            pool.sem_inc(copied, SLOTS)
            with pool.Fori(0, EDGE_GROUPS // SLOTS) as i:
                for s in range(SLOTS):
                    q = i * SLOTS + s
                    pool.wait_ge(copied, free(q))
                    pool.tensor_copy(slot[:, s], S.coli[:, HYP, bass.ds(q * U, U)]).then_inc(picked, 1)
                    pool.wait_ge(picked, q + 1)
                    pool.sem_inc(tick, 1)
                    for u in range(U):
                        gather(pool, got[:, s, u:u + 1], A["hw"], slot[:, s, u:u + 1]).then_inc(gathered[s], 16)

        @block.vector
        def _(dve):
            with dve.Fori(0, EDGE_GROUPS // SLOTS) as i:
                for s in range(SLOTS):
                    q = i * SLOTS + s
                    dve.wait_ge(gathered[s], (i + 1) * (16 * U))
                    dve.tensor_copy(S.hw[:, bass.ds(q * U, U)], got[:, s]).then_inc(copied, 1)



class SegmentSum:

    def __init__(self, f, T, S, order, table, idx, w, out, extra=None):
        self.T, self.S, self.order, self.table, self.idx, self.w, self.extra = T, S, order, table, idx, w, extra
        self.wt = table.shape[1]
        self.iters = EDGE_GROUPS // SLOTS
        self.out_g = groups_of(out)
        self.slot = f.sb("sum_slot", [P, SLOTS, U], I32)
        self.v = f.sb("sum_v", [P, SLOTS, U, w])
        self.krow = f.sb("sum_krow", [P, SLOTS, U * P])
        self.same = f.sb("sum_same", [P, SLOTS, U, P])
        self.sums = f.sb("sum_sums", [P, SLOTS, U, w])
        self.acc = [f.ps(f"sum_acc{s}", [P, U, 256]) for s in range(2)]
        self.picked, self.tick, self.ones_set = f.sem("sum_picked"), f.sem("sum_tick"), f.sem("sum_ones_set")
        self.matched, self.summed, self.copied = f.sem("sum_matched"), f.sem("sum_summed"), f.sem("sum_copied")
        self.gathered, self.keyed, self.stored = (f.sems("sum_gathered"), f.sems("sum_keyed"),
                                                  f.sems("sum_stored"))
        self.prime_stores = prime_stores(f, self.stored, 1, S.ident_dram, "sum_spare")

    def sync_start(self, sp):
        for m in (self.matched, self.summed, self.copied):
            sp.sem_inc(m, SLOTS)

    def sync_steps(self, sp):
        def key_rows(i, s):
            q = i * SLOTS + s
            sp.wait_ge(self.matched, free(q))
            sp.dma_start(self.krow[:, s], self.T["keys"][self.order:self.order + 1, bass.ds(q * (U * P) + 1, U * P)]
                         .to_broadcast([P, U * P])).then_inc(self.keyed[s], 16)
        return [(4, key_rows)]

    def sync_end(self, sp):
        for s in range(SLOTS):
            sp.wait_ge(self.stored[s], 16 * (self.iters + 1))

    def pool_loop(self, pool):
        with pool.Fori(0, self.iters) as i:
            for s in range(SLOTS):
                q = i * SLOTS + s
                pool.wait_ge(self.summed, free(q))
                pool.tensor_copy(self.slot[:, s], self.S.coli[:, self.idx, bass.ds(q * U, U)]
                                 ).then_inc(self.picked, 1)
                pool.wait_ge(self.picked, q + 1)
                pool.sem_inc(self.tick, 1)
                for u in range(U):
                    gather(pool, self.v[:, s, u, 0:self.wt], self.table, self.slot[:, s, u:u + 1]
                           ).then_inc(self.gathered[s], 16)

    def vector_start(self, dve):
        if self.extra == "ones":
            dve.memset(self.v[:, :, :, self.wt:self.wt + 1], 1.0).then_inc(self.ones_set, 1)

    def vector_steps(self, dve):
        key = (KD, KS)[self.order]

        def match(i, s):
            q = i * SLOTS + s
            dve.wait_ge(self.keyed[s], (i + 1) * 16)
            dve.wait_ge(self.summed, free(q))
            if self.extra == "hw":
                dve.tensor_copy(self.v[:, s, :, self.wt], self.S.hw[:, bass.ds(q * U, U)])
            dve.tensor_tensor(self.same[:, s], self.krow[:, s].rearrange("p (u e) -> p u e", u=U),
                              self.S.colf[:, key, bass.ds(q * U, U)].unsqueeze(2).to_broadcast([P, U, P]),
                              ALU.is_equal).then_inc(self.matched, 1)
        return [(1, match)]

    def tensor_start(self, pe):
        if self.extra == "ones":
            pe.wait_ge(self.ones_set, 1)

    def tensor_steps(self, pe):
        def add_up(i, s):
            q = i * SLOTS + s
            pe.wait_ge(self.matched, done(q))
            pe.wait_ge(self.gathered[s], (i + 1) * (16 * U))
            pe.wait_ge(self.copied, two_behind(q))
            for u in range(U):
                m = pe.matmul(self.acc[s % 2][:, u, 0:self.w], self.same[:, s, u, :], self.v[:, s, u, :],
                              start=True, stop=True)
            m.then_inc(self.summed, 1)
        return [(0, add_up)]

    def scalar_steps(self, act):
        def take_sums(i, s):
            q = i * SLOTS + s
            act.wait_ge(self.summed, done(q))
            act.wait_ge(self.stored[s], (i + 1) * 16)
            act.activation(self.sums[:, s], self.acc[s % 2][:, :, 0:self.w], ACT.Copy).then_inc(self.copied, 1)
            act.wait_ge(self.copied, done(q))
            act.dma_start(self.out_g[q], self.sums[:, s]).then_inc(self.stored[s], 16)
        return [(0, take_sums)]


def steps_of(work, engine, eng):
    return {"sync": work.sync_steps, "vector": work.vector_steps, "tensor": work.tensor_steps,
            "scalar": work.scalar_steps}[engine](eng)


def sum_pass(nc, T, S, name, *of, norm=None):
    with Phase(nc, name) as f:
        sums = SegmentSum(f, T, S, *of)
        norm = norm(f) if norm else None
        block = f.block()

        @block.sync
        def _(sp):
            sums.sync_start(sp)
            if norm:
                norm.sync_start(sp)
            pipelined(sp, sums.iters, sums.sync_steps(sp), norm.sync_steps(sp) if norm else ())
            sums.sync_end(sp)
            if norm:
                norm.r.finish(sp)

        @block.gpsimd
        def _(pool):
            sums.pool_loop(pool)

        @block.vector
        def _(dve):
            sums.vector_start(dve)
            if norm:
                norm.ln.setup(dve)
            pipelined(dve, sums.iters, sums.vector_steps(dve), norm.vector_steps(dve) if norm else ())

        @block.tensor
        def _(pe):
            sums.tensor_start(pe)
            pipelined(pe, sums.iters, sums.tensor_steps(pe))

        @block.scalar
        def _(act):
            sums.prime_stores(act)
            if norm:
                norm.scalar_start(act)
            pipelined(act, sums.iters, sums.scalar_steps(act), norm.scalar_steps(act) if norm else ())


def fix_pass(nc, S, name, order, out, w):
    with Phase(nc, name) as f:
        first = f.sb("first", [HALF_T, 2, w])
        last = f.sb("last", [HALF_T, 2, w])
        full = f.sb("full", [HALF_T, 2, w])
        acc = f.ps("acc", [P, 2, 512])
        loaded, carried, added, stored = (f.sem(n) for n in ("loaded", "carried", "added", "stored"))
        block = f.block()
        rows = out.rearrange("(c p e) w -> p c e w", p=HALF_T, e=P)

        @block.sync
        def _(sp):
            sp.dma_start(first[:], rows[:, :, 0, :]).then_inc(loaded, 16)
            sp.dma_start(last[:], rows[:, :, P - 1, :]).then_inc(loaded, 16)
            sp.wait_ge(added, 1)
            sp.dma_start(rows[:, :, P - 1, :], full[:]).then_inc(stored, 16)
            sp.wait_ge(stored, 16)

        @block.tensor
        def _(pe):
            pe.wait_ge(loaded, 32)
            for c in range(2):
                for later in range(2):
                    m = pe.matmul(acc[0:HALF_T, c, 0:w], S.joins[:, order, later, c * HALF_T:(c + 1) * HALF_T],
                                  first[:, later, :], start=(later == 0), stop=(later == 1))
            m.then_inc(carried, 1)

        @block.vector
        def _(dve):
            dve.wait_ge(carried, 1)
            dve.tensor_tensor(full[:], last[:], acc[0:HALF_T, :, 0:w], ALU.add).then_inc(added, 1)



def bc_rows(row, n=U):
    return row.unsqueeze(1).to_broadcast([P, n, C])


def pipelined(eng, iters, steps, twice=()):
    lead = max([n for n, _ in steps] + [-(-n // 2) for n, _ in twice])
    last = iters * SLOTS

    def at(q):
        for n, step in steps:
            if 0 <= q + n < last:
                step((q + n) // SLOTS, (q + n) % SLOTS)
        for k in range(2):
            for n, step in twice:
                g = 2 * q + k + n
                if 0 <= g < 2 * last:
                    step(g // SLOTS, g % SLOTS)

    for q in range(-lead, 0):
        at(q)
    whole = iters - -(-lead // SLOTS)
    with eng.Fori(0, whole) as i:
        for s in range(SLOTS):
            for n, step in steps:
                step(i + (s + n) // SLOTS, (s + n) % SLOTS)
            for k in range(2):
                for n, step in twice:
                    g = 2 * s + k + n
                    step(i * 2 + g // SLOTS, g % SLOTS)
    for q in range(whole * SLOTS, last):
        at(q)


class Rows:

    def __init__(self, f, S, dense, stores, groups=None, name=""):
        self.f, self.S, self.dense = f, S, dense
        self.iters = (groups or (NODE_GROUPS if dense else EDGE_GROUPS)) // SLOTS
        self.loaded = f.sems(f"{name}loaded")
        self.gathered = f.sems(f"{name}gathered")
        self.stored = f.sems(f"{name}stored")
        self.used = f.sem(f"{name}used")
        self.ready = f.sem(f"{name}ready")
        self.picked, self.picked_out, self.tick = (f.sem(f"{name}{n}") for n in ("picked", "picked_out", "tick"))
        self.weights = f.sem(f"{name}weights")
        self.stores = stores
        self.prime_stores = prime_stores(f, self.stored, stores, S.ident_dram, f"{name}spare")
        self.slot = f.sb(f"{name}slot", [P, SLOTS, U], I32)
        self.slot_out = f.sb(f"{name}slot_out", [P, SLOTS, U], I32)

    def prime(self, sp, sems):
        for m in (self.used, self.ready, *sems):
            sp.sem_inc(m, SLOTS)

    def load(self, sp, pairs):
        load = self.load_step(sp, pairs)
        with sp.Fori(0, self.iters) as i:
            for s in range(SLOTS):
                load(i, s)

    def load_step(self, sp, pairs):
        def load(i, s):
            q = i * SLOTS + s
            sp.wait_ge(self.used, free(q))
            for buf, table in pairs:
                sp.dma_start(buf[:, s], table[q]).then_inc(self.loaded[s], 16)
        return load

    def finish(self, sp):
        for s in range(SLOTS):
            sp.wait_ge(self.stored[s], 16 * self.stores * (self.iters + 1))

    def gather_group(self, pool, q, s, buf, table, idx, buf_used):
        pool.wait_ge(buf_used, free(q))
        pool.tensor_copy(self.slot[:, s], self.S.coli[:, idx, bass.ds(q * U, U)]).then_inc(self.picked, 1)
        pool.wait_ge(self.picked, q + 1)
        pool.sem_inc(self.tick, 1)
        for u in range(U):
            gather(pool, buf[:, s, u, :], table, self.slot[:, s, u:u + 1]).then_inc(self.gathered[s], 16)

    def scatter_group(self, pool, i, s, buf, table, idx, rows):
        q = i * SLOTS + s
        pool.wait_ge(self.stored[s], (i + 1) * (16 * U))
        pool.tensor_copy(self.slot_out[:, s], self.S.coli[:, idx, bass.ds(q * U, U)]).then_inc(self.picked_out, 1)
        pool.wait_ge(self.picked_out, q + 1)
        pool.sem_inc(self.tick, 1)
        pool.wait_ge(self.ready, done(q))
        pool.sem_inc(self.tick, 1)
        for u in range(U):
            scatter(pool, table, self.slot_out[:, s, u:u + 1], rows, buf[:, s, u, :]).then_inc(self.stored[s], 16)

    def pool_loop(self, pool, gathers=None, scatters=None, ahead=0):
        pipelined(pool, self.iters, [
            *([(0, lambda i, s: self.scatter_group(pool, i, s, *scatters))] if scatters else []),
            *([(ahead, lambda i, s: self.gather_group(pool, i * SLOTS + s, s, *gathers))] if gathers else []),
        ])

    def store(self, eng, i, s, *pairs):
        q = i * SLOTS + s
        eng.wait_ge(self.ready, done(q))
        for buf, table in pairs:
            eng.dma_start(table[q], buf[:, s]).then_inc(self.stored[s], 16)

    def wait_loads(self, eng, i, s, plain, gathers=0):
        if plain:
            eng.wait_ge(self.loaded[s], (i + 1) * (16 * plain))
        if gathers:
            eng.wait_ge(self.gathered[s], (i + 1) * (16 * U * gathers))

    def out_free(self, eng, i, s):
        eng.wait_ge(self.stored[s], (i + 1) * (16 * self.stores))


class LayerNorm:

    def __init__(self, f, name=""):
        self.stats = f.sb(f"stats{name}", [P, SLOTS, U, 6])
        self.mv = f.sb(f"mv{name}", [P, SLOTS, U, 2])
        self.std = f.sb(f"std{name}", [P, SLOTS, U])
        self.rstd = f.sb(f"rstd{name}", [P, SLOTS, U])
        self.shift = f.sb(f"shift{name}", [P, SLOTS, U])
        self.eps = f.sb(f"eps{name}", [P, 1])
        self.z_ready, self.stats_ready, self.mv_ready, self.std_ready, self.rstd_ready, self.shift_ready = (
            f.sem(f"{n}{name}") for n in ("z_ready", "stats_ready", "mv_ready", "std_ready", "rstd_ready",
                                          "shift_ready"))
        self.eps_set = f.sem(f"eps_set{name}")
        self.sems = [self.z_ready, self.stats_ready, self.mv_ready, self.std_ready, self.rstd_ready,
                     self.shift_ready]

    def setup(self, dve):
        dve.memset(self.eps[:], EPS).then_inc(self.eps_set, 1)

    def moments(self, dve, i, s, z, tick):
        q = i * SLOTS + s
        dve.wait_ge(self.z_ready, done(q))
        for u in range(U):
            b = dve.bn_stats(self.stats[:, s, u, :], z[:, s, u, :])
        b.then_inc(self.stats_ready, 1)
        dve.wait_ge(self.stats_ready, done(q))
        dve.sem_inc(tick, 1)
        for u in range(U):
            b = dve.bn_aggr(self.mv[:, s, u, :], self.stats[:, s, u, :])
        b.then_inc(self.mv_ready, 1)

    def deviation(self, act, i, s):
        q = i * SLOTS + s
        act.wait_ge(self.mv_ready, done(q))
        act.activation(self.std[:, s], self.mv[:, s, :, 1], ACT.Sqrt, bias=self.eps[:]).then_inc(self.std_ready, 1)

    def factors(self, dve, i, s):
        q = i * SLOTS + s
        dve.wait_ge(self.std_ready, done(q))
        dve.reciprocal(self.rstd[:, s], self.std[:, s]).then_inc(self.rstd_ready, 1)
        dve.wait_ge(self.rstd_ready, done(q))
        dve.scalar_tensor_tensor(self.shift[:, s], self.mv[:, s, :, 0], -1.0, self.rstd[:, s],
                                 ALU.mult, ALU.mult).then_inc(self.shift_ready, 1)

    def scale(self, act, i, s, z, out, ready, r=None, table=None):
        q = i * SLOTS + s
        if r:
            r.out_free(act, i, s)
        act.wait_ge(self.shift_ready, done(q))
        for u in range(U):
            b = act.activation(out[:, s, u, :], z[:, s, u, :], ACT.Identity, bias=self.shift[:, s, u:u + 1],
                               scale=self.rstd[:, s, u:u + 1])
        b.then_inc(ready, 1)
        if table is not None:
            r.store(act, i, s, (out, table))


def hyper_rows(nc, T, S, name, raw, out, affine):
    with Phase(nc, name) as f:
        r = Rows(f, S, dense=False, stores=U)
        rows = f.sb("rows", [P, SLOTS, U, C + 1])
        inv = f.sb("inv", [P, SLOTS, U, 1])
        mean = f.sb("mean", [P, SLOTS, U, C])
        inverted, scaled, shifted = f.sem("inverted"), f.sem("scaled"), f.sem("shifted")
        block = f.block()

        @block.sync
        def _(sp):
            r.prime(sp, (inverted, scaled, shifted))
            r.load(sp, [(rows, groups_of(raw))])
            r.finish(sp)

        @block.gpsimd
        def _(pool):
            r.prime_stores(pool)
            r.pool_loop(pool, scatters=(mean, out, SCE, N_HYPER))

        @block.vector
        def _(dve):
            def invert(i, s):
                q = i * SLOTS + s
                dve.wait_ge(r.ready, free(q))
                r.wait_loads(dve, i, s, 1)
                dve.reciprocal(inv[:, s], rows[:, s, :, C:C + 1]).then_inc(inverted, 1)

            def divide(i, s):
                q = i * SLOTS + s
                dve.wait_ge(inverted, done(q))
                r.out_free(dve, i, s)
                m = dve.tensor_tensor(mean[:, s], rows[:, s, :, 0:C], inv[:, s].to_broadcast([P, U, C]),
                                      ALU.mult)
                m.then_inc(r.used, 1)
                if affine:
                    dve.wait_ge(r.used, done(q))
                    dve.tensor_tensor(mean[:, s], mean[:, s], bc_rows(S.affine[:, 0, :]), ALU.mult
                                      ).then_inc(scaled, 1)
                    dve.wait_ge(scaled, done(q))
                    dve.tensor_tensor(mean[:, s], mean[:, s], bc_rows(S.affine[:, 1, :]), ALU.add
                                      ).then_inc(shifted, 1)
                    dve.wait_ge(shifted, done(q))
                dve.sem_inc(r.ready, 1) if affine else dve.wait_ge(r.used, done(q))
                if not affine:
                    dve.sem_inc(r.ready, 1)

            pipelined(dve, r.iters, [
                (0, divide),
                (1, invert),
            ])


def node_rows(nc, T, A, S, name, raw, layer):
    with Phase(nc, name) as f:
        r = Rows(f, S, dense=False, stores=U)
        rows = f.sb("rows", [P, SLOTS, U, C + 1])
        own = f.sb("own", [P, SLOTS, U, C])
        pos = f.sb("pos", [P, SLOTS, U, 1])
        safe = f.sb("safe", [P, SLOTS, U, 1])
        inv = f.sb("inv", [P, SLOTS, U, 1])
        mean = f.sb("mean", [P, SLOTS, U, C])
        mean_t = f.sb("mean_t", [P, SLOTS, U * P])
        w = f.sb("w", [P, C])
        bias = f.sb("bias", [P, C])
        z = f.sb("z", [P, SLOTS, U, C])
        res = f.sb("res", [P, SLOTS, U, C])
        flagged = f.sb("flagged", [P, SLOTS, U, C])
        squares = f.sb("squares", [P, SLOTS, U, C])
        ones = f.sb("ones", [P, P])
        zeros = f.sb("zeros", [P, U * C])
        ps_t = [f.ps(f"ps_t{s}", [P, 512]) for s in range(2)]
        ps_o = [f.ps(f"ps_o{s}", [P, 512]) for s in range(2)]
        ps_sum = f.ps("ps_sum", [P, 512])
        ps_sq = f.ps("ps_sq", [P, 512])
        masked, inverted, scaled, turned, turned_out, product = (f.sem(n) for n in (
            "masked", "inverted", "scaled", "turned", "turned_out", "product"))
        flag_set, squared, counted, ones_set, summed = (f.sem(n) for n in (
            "flag_set", "squared", "counted", "ones_set", "summed"))
        ln = LayerNorm(f) if layer == 2 else None
        block = f.block()

        @block.sync
        def _(sp):
            sp.dma_start(w[:], A[f"L0_W{layer}T"]).then_inc(r.weights, 16)
            sp.dma_start(bias[:], A["L0_b2_rows"]).then_inc(r.weights, 16)
            sp.wait_ge(r.weights, 32)
            r.prime(sp, (masked, inverted, scaled, turned, turned_out, product, flag_set, squared, counted,
                         *(ln.sems if ln else ())))
            r.load(sp, [(rows, groups_of(raw))])
            r.finish(sp)

        @block.gpsimd
        def _(pool):
            r.prime_stores(pool)
            if layer == 1:
                r.pool_loop(pool, scatters=(res, T["X1"], SCS, NP_))
            else:
                r.pool_loop(pool, gathers=(own, A["x"], NOD, flag_set), scatters=(res, T["X1"], SCS, NP_),
                            ahead=5)

        @block.vector
        def _(dve):
            dve.memset(ones[:], 1.0).then_inc(ones_set, 1)
            dve.memset(zeros[:], 0.0).then_inc(ones_set, 1)
            if ln:
                ln.setup(dve)
            dve.wait_ge(r.weights, 32)
            def mask(i, s):
                q = i * SLOTS + s
                dve.wait_ge(r.used, free(q))
                r.wait_loads(dve, i, s, 1)
                dve.tensor_scalar(pos[:, s], rows[:, s, :, C:C + 1], 0.0, None, ALU.is_gt)
                dve.tensor_scalar(safe[:, s], rows[:, s, :, C:C + 1], 1.1754944e-38, None, ALU.max
                                  ).then_inc(masked, 1)

            def invert(i, s):
                q = i * SLOTS + s
                dve.wait_ge(masked, done(q))
                dve.reciprocal(inv[:, s], safe[:, s]).then_inc(inverted, 1)

            def gate(i, s):
                q = i * SLOTS + s
                dve.wait_ge(inverted, done(q))
                dve.tensor_tensor(safe[:, s], inv[:, s], pos[:, s], ALU.mult).then_inc(scaled, 1)

            def divide(i, s):
                q = i * SLOTS + s
                dve.wait_ge(scaled, done(q))
                dve.wait_ge(turned, free(q))
                dve.tensor_tensor(mean[:, s], rows[:, s, :, 0:C], safe[:, s].to_broadcast([P, U, C]),
                                  ALU.mult).then_inc(r.used, 1)

            def take_product(i, s):
                q = i * SLOTS + s
                if layer == 1:
                    dve.wait_ge(product, done(q))
                    r.out_free(dve, i, s)
                    dve.tensor_copy(res[:, s], ps_o[s % 2][:].rearrange("p (u c) -> p u c", u=U)
                                    ).then_inc(r.ready, 1)
                    dve.wait_ge(counted, free(q))
                    dve.tensor_tensor(flagged[:, s], ps_o[s % 2][:].rearrange("p (u c) -> p u c", u=U),
                                      S.colf[:, SM, bass.ds(q * U, U)].unsqueeze(2).to_broadcast([P, U, C]),
                                      ALU.mult).then_inc(flag_set, 1)
                else:
                    dve.wait_ge(product, done(q))
                    r.wait_loads(dve, i, s, 0, 1)
                    dve.wait_ge(r.ready, free(q))
                    dve.tensor_tensor(z[:, s], ps_o[s % 2][:].rearrange("p (u c) -> p u c", u=U), own[:, s],
                                      ALU.add).then_inc(flag_set, 1)
                    dve.wait_ge(flag_set, done(q))
                    dve.tensor_tensor(z[:, s], z[:, s], bc_rows(bias[:]), ALU.add).then_inc(ln.z_ready, 1)

            def moments(i, s):
                ln.moments(dve, i, s, z, r.tick)

            def factors(i, s):
                ln.factors(dve, i, s)

            pipelined(dve, r.iters, [
                *([(0, factors)] if ln else []),
                (2, take_product),
                *([(2, moments)] if ln else []),
                (4, mask),
                (4, invert),
                (4, gate),
                (4, divide),
            ])

        @block.tensor
        def _(pe):
            pe.wait_ge(r.weights, 32)
            pe.wait_ge(ones_set, 2)
            if layer == 1:
                for p in (ps_sum, ps_sq):
                    pe.matmul(p[:], ones[:], zeros[:], start=True, stop=False, skip_group_check=True)
            def turn(i, s):
                q = i * SLOTS + s
                pe.wait_ge(r.used, done(q))
                pe.wait_ge(turned_out, two_behind(q))
                for u in range(U):
                    t = pe.transpose(ps_t[s % 2][:, u * P:(u + 1) * P], mean[:, s, u, :], S.ident[:])
                t.then_inc(turned, 1)

            def multiply(i, s):
                q = i * SLOTS + s
                pe.wait_ge(turned_out, done(q))
                pe.wait_ge(flag_set, two_behind(q))
                for u in range(U):
                    t = pe.matmul(ps_o[s % 2][:, u * C:(u + 1) * C], mean_t[:, s, u * P:(u + 1) * P], w[:],
                                  start=True, stop=True)
                t.then_inc(product, 1)

            def count(i, s):
                q = i * SLOTS + s
                pe.wait_ge(squared, done(q))
                pe.matmul(ps_sum[:], ones[:], flagged[:, s].rearrange("p u c -> p (u c)"),
                          start=False, stop=False, skip_group_check=True)
                pe.matmul(ps_sq[:], ones[:], squares[:, s].rearrange("p u c -> p (u c)"),
                          start=False, stop=False, skip_group_check=True).then_inc(counted, 1)

            pipelined(pe, r.iters, [
                *([(0, count)] if layer == 1 else []),
                (2, multiply),
                (3, turn),
            ])

        @block.scalar
        def _(act):
            if ln:
                act.wait_ge(ln.eps_set, 1)
            def take_turned(i, s):
                q = i * SLOTS + s
                act.wait_ge(turned, done(q))
                act.wait_ge(product, free(q))
                act.activation(mean_t[:, s], ps_t[s % 2][:], ACT.Copy).then_inc(turned_out, 1)

            def square(i, s):
                q = i * SLOTS + s
                act.wait_ge(flag_set, done(q))
                act.wait_ge(counted, free(q))
                act.activation(squares[:, s], flagged[:, s], ACT.Square).then_inc(squared, 1)

            def deviation(i, s):
                ln.deviation(act, i, s)

            def scale(i, s):
                ln.scale(act, i, s, z, res, r.ready, r)

            pipelined(act, r.iters, [
                *([(0, scale)] if not (layer == 1) else []),
                *([(1, square)] if layer == 1 else []),
                *([(1, deviation)] if not (layer == 1) else []),
                (3, take_turned),
            ])
            if layer == 1:
                act.wait_ge(counted, r.iters * SLOTS + SLOTS)
                act.activation(S.affine_sums[:, 0, :], ps_sum[:], ACT.Copy).then_inc(summed, 1)
                act.activation(S.affine_sums[:, 1, :], ps_sq[:], ACT.Copy).then_inc(summed, 1)


def batch_norm(nc, A, S):
    with Phase(nc, "bn") as f:
        rows = f.sb("rows", [P, 3, C])
        tot = f.sb("tot", [P, 2, C])
        mean = f.sb("mean", [P, 2, C])
        sq = f.sb("sq", [P, C])
        var = f.sb("var", [P, C])
        std = f.sb("std", [P, C])
        inv = f.sb("inv", [P, C])
        mu = f.sb("mu", [P, C])
        eps = f.sb("eps", [P, 1])
        loaded, stage, rooted = f.sem("loaded"), f.sem("stage"), f.sem("rooted")
        block = f.block()
        marks = {}

        @block.sync
        def _(sp):
            for k, n in enumerate(("L0_b1_rows", "L0_gamma_rows", "L0_beta_rows")):
                sp.dma_start(rows[:, k, :], A[n]).then_inc(loaded, 16)

        @block.vector
        def _(dve):
            n = 0

            def step(x):
                nonlocal n
                x.then_inc(stage, 1)
                n += 1
                dve.wait_ge(stage, n)

            step(dve.memset(eps[:], EPS))
            step(dve.tensor_reduce(tot[:], S.affine_sums[:].rearrange("p k (u c) -> p k c u", u=U), AX_X, ALU.add))
            step(dve.tensor_scalar(mean[:], tot[:], 1.0 / N_NODES, None, ALU.mult))
            step(dve.tensor_tensor(sq[:], mean[:, 0, :], mean[:, 0, :], ALU.mult))
            step(dve.tensor_tensor(var[:], mean[:, 1, :], sq[:], ALU.subtract))
            step(dve.tensor_scalar(var[:], var[:], 0.0, None, ALU.max))
            marks["var"] = n
            dve.wait_ge(rooted, 1)
            dve.wait_ge(loaded, 48)
            step(dve.reciprocal(inv[:], std[:]))
            step(dve.tensor_tensor(S.affine[:, 0, :], rows[:, 1, :], inv[:], ALU.mult))
            step(dve.tensor_tensor(mu[:], mean[:, 0, :], rows[:, 0, :], ALU.add))
            step(dve.tensor_tensor(mu[:], rows[:, 0, :], mu[:], ALU.subtract))
            step(dve.tensor_tensor(mu[:], mu[:], S.affine[:, 0, :], ALU.mult))
            step(dve.tensor_tensor(S.affine[:, 1, :], mu[:], rows[:, 2, :], ALU.add))

        @block.scalar
        def _(act):
            act.wait_ge(stage, marks["var"])
            act.activation(std[:], var[:], ACT.Sqrt, bias=eps[:]).then_inc(rooted, 1)


class NodeNorm:

    def __init__(self, f, S, adds, bias, out):
        self.adds, self.bias, self.out = adds, bias, out
        self.r = Rows(f, S, dense=True, stores=1, name="norm_")
        self.bufs = [f.sb(f"norm_in{k}", [P, SLOTS, U, t.shape[1]]) for k, t in enumerate(adds)]
        self.z = f.sb("norm_z", [P, SLOTS, U, C])
        self.res = f.sb("norm_res", [P, SLOTS, U, C])
        self.ln = LayerNorm(f, "norm_")
        self.added = f.sem("norm_added")

    def sync_start(self, sp):
        self.r.prime(sp, (self.added, *self.ln.sems))

    def sync_steps(self, sp):
        return [(6, self.r.load_step(sp, [(b, groups_of(t)) for b, t in zip(self.bufs, self.adds)]))]

    def vector_steps(self, dve):
        r, ln, z, bufs = self.r, self.ln, self.z, self.bufs

        def add(i, s):
            q = i * SLOTS + s
            dve.wait_ge(r.ready, free(q))
            r.wait_loads(dve, i, s, len(bufs))
            dve.tensor_tensor(z[:, s], bufs[0][:, s, :, 0:C], bc_rows(self.bias), ALU.add
                              ).then_inc(self.added if len(bufs) == 2 else ln.z_ready, 1)
            if len(bufs) == 2:
                dve.wait_ge(self.added, done(q))
                dve.tensor_tensor(z[:, s], z[:, s], bufs[1][:, s, :, 0:C], ALU.add).then_inc(ln.z_ready, 1)
            dve.wait_ge(ln.z_ready, done(q))
            dve.sem_inc(r.used, 1)

        return [(0, lambda i, s: ln.factors(dve, i, s)), (2, add), (2, lambda i, s: ln.moments(dve, i, s, z, r.tick))]

    def scalar_start(self, act):
        act.wait_ge(self.ln.eps_set, 1)
        self.r.prime_stores(act)

    def scalar_steps(self, act):
        r, ln = self.r, self.ln
        return [(0, lambda i, s: ln.scale(act, i, s, self.z, self.res, r.ready, r, groups_of(self.out))),
                (1, lambda i, s: ln.deviation(act, i, s))]


def weights_phase(nc, A, S):
    with Phase(nc, "weights") as f:
        att1 = f.sb("att1", [P, 2, HC])
        att2 = f.sb("att2", [P, 2, C])
        prod1 = f.sb("prod1", [P, 2, HC])
        prod2 = f.sb("prod2", [P, 2, 2, C])
        cols = f.sb("cols", [P, 2])
        w = f.sb("w", [P, 2, C])
        rows = f.sb("rows", [P, 3, C])
        hid = f.sb("hid", [P, 2])
        absx = f.sb("absx", [P, 1])
        ex = f.sb("ex", [P, 1])
        lg = f.sb("lg", [P, 1])
        spread = f.sb("spread", [P, 2, P])
        one = f.sb("one", [P, 1])
        acc = f.ps("acc", [P, 2, C])
        loaded, stage, logs, multiplied = f.sem("loaded"), f.sem("stage"), f.sem("logs"), f.sem("multiplied")
        block = f.block()
        marks = {}

        @block.sync
        def _(sp):
            for out, src in ((S.W1[:], A["L1_W1"]), (S.W2x[:, :, 0:C], A["L1_W2"]), (S.b1col[:], A["L1_b1_cols"]),
                             (att1[:, 0, :], A["L1_as1"]), (att1[:, 1, :], A["L1_ad1"]),
                             (att2[:, 0, :], A["L1_as2"]), (att2[:, 1, :], A["L1_ad2"]),
                             (cols[:, 0:1], A["L2_b1_col"]), (cols[:, 1:2], A["L3_bfc1_col"]),
                             (w[:, 0, :], A["L2_W2"]), (w[:, 1, :], A["L3_Wfc2T"]),
                             (rows[:, 0, :], A["L2_b2_rows"]), (rows[:, 1, :], A["L2_bpre_rows"]),
                             (rows[:, 2, :], A["L3_bfc2_rows"]), (S.b0[:], A["L0_b2_rows"]),
                             (S.b2[:], A["L1_b2_rows"])):
                sp.dma_start(out, src).then_inc(loaded, 16)

        @block.vector
        def _(dve):
            n = 0

            def step(*ins):
                nonlocal n
                for x in ins:
                    x.then_inc(stage, 1)
                n += len(ins)
                dve.wait_ge(stage, n)

            dve.wait_ge(loaded, 16 * 16)
            step(dve.memset(one[:], 1.0), dve.memset(S.W2x[:, :, C + 2:H2W], 0.0))
            marks["one"] = n
            step(*[dve.tensor_tensor(prod1[:, k, :], S.W1[:], att1[:, k, :], ALU.mult) for k in range(2)],
                 *[dve.tensor_tensor(prod2[:, k, :, :], S.W2x[:, :, 0:C],
                                     att2[:, k, :].unsqueeze(1).to_broadcast([P, 2, C]), ALU.mult)
                   for k in range(2)])
            step(*[dve.tensor_reduce(S.WA[:, k * HEADS:(k + 1) * HEADS],
                                     prod1[:, k, :].rearrange("p (h c) -> p h c", h=HEADS), AX_X, ALU.add)
                   for k in range(2)],
                 *[dve.tensor_reduce(S.W2x[:, :, C + k:C + k + 1], prod2[:, k, :, :], AX_X, ALU.add)
                   for k in range(2)])
            step(dve.tensor_scalar(hid[:], cols[:], 0.0, None, ALU.max))
            dve.wait_ge(logs, 3)
            step(dve.scalar_tensor_tensor(hid[:, 1:2], lg[:], -LOG2, hid[:, 1:2], ALU.add, ALU.add))
            step(dve.tensor_copy(spread[:], hid[:].unsqueeze(2).to_broadcast([P, 2, P])))
            marks["spread"] = n
            dve.wait_ge(multiplied, 1)
            step(dve.tensor_tensor(S.c2[:], acc[:, 0, :], rows[:, 0, :], ALU.add),
                 dve.tensor_tensor(S.c3[:], acc[:, 1, :], rows[:, 2, :], ALU.add))
            step(dve.tensor_scalar(S.c2[:], S.c2[:], 0.0, None, ALU.max))
            step(dve.tensor_tensor(S.c2[:], S.c2[:], rows[:, 1, :], ALU.add))

        @block.scalar
        def _(act):
            act.wait_ge(stage, marks["one"])
            act.activation(absx[:], cols[:, 1:2], ACT.Abs).then_inc(logs, 1)
            act.wait_ge(logs, 1)
            act.activation(ex[:], absx[:], ACT.Exp, scale=-1.0).then_inc(logs, 1)
            act.wait_ge(logs, 2)
            act.activation(lg[:], ex[:], ACT.Ln, bias=one[:]).then_inc(logs, 1)

        @block.tensor
        def _(pe):
            pe.wait_ge(stage, marks["spread"])
            for k in range(2):
                m = pe.matmul(acc[:, k, :], spread[:, k, :], w[:, k, :], start=True, stop=True)
            m.then_inc(multiplied, 1)



def gat_rows(nc, T, S, name, dense):
    with Phase(nc, name) as f:
        r = Rows(f, S, dense, stores=2 if dense else U)
        w_in = C if dense else HC + HEADS
        rows = f.sb("rows", [P, SLOTS, U, w_in])
        x_t = f.sb("x_t", [P, SLOTS, U * P])
        inv = f.sb("inv", [P, SLOTS, U, HEADS])
        den = f.sb("den", [P, SLOTS, U, HEADS])
        mean = f.sb("mean", [P, SLOTS, U, HC])
        aa = f.sb("aa", [P, SLOTS, U, 2 * HEADS])
        pos = f.sb("pos", [P, SLOTS, 2, U * P])
        neg = f.sb("neg", [P, SLOTS, 2, U * P])
        elu = f.sb("elu", [P, SLOTS, 2, U * P])
        res = f.sb("res", [P, SLOTS, U, H2W])
        ps_t = f.ps("ps_t", [P, U * P])
        ps_a = f.ps("ps_a", [P, 512])
        ps_h = [f.ps(f"ps_h{s}", [P, 2, U * P]) for s in range(2)]
        ps_o = f.ps("ps_o", [P, U, 256])
        x_ready, hidden, aa_out, relued, clipped, exped, elu_ready, product, safe, inverted, normed = (
            f.sem(n) for n in ("x_ready", "hidden", "aa_out", "relued", "clipped", "exped", "elu_ready",
                               "product", "safe", "inverted", "normed"))
        block = f.block()

        @block.sync
        def _(sp):
            r.prime(sp, (x_ready, hidden, aa_out, relued, clipped, exped, elu_ready, product, safe, inverted,
                         normed))
            r.load(sp, [(rows, groups_of(T["X1"] if dense else T["RAW260"]))])
            r.finish(sp)

        @block.gpsimd
        def _(pool):
            if not dense:
                r.prime_stores(pool)
                r.pool_loop(pool, scatters=(res, T["H2"], SCD, NP_))

        @block.tensor
        def _(pe):
            def turn(i, s):
                q = i * SLOTS + s
                if dense:
                    r.wait_loads(pe, i, s, 1)
                    pe.wait_ge(x_ready, behind(q))
                    for u in range(U):
                        t = pe.transpose(ps_t[:, u * P:(u + 1) * P], rows[:, s, u, :], S.ident[:])
                    t.then_inc(r.used, 1)

            def hidden_layer(i, s):
                q = i * SLOTS + s
                pe.wait_ge(relued, two_behind(q))
                pe.wait_ge(clipped, two_behind(q))
                if dense:
                    pe.wait_ge(aa_out, behind(q))
                    pe.wait_ge(x_ready, done(q))
                    for u in range(U):
                        pe.matmul(ps_a[:, u * 8:(u + 1) * 8], x_t[:, s, u * P:(u + 1) * P], S.WA[:],
                                  start=True, stop=True)
                    for c in range(2):
                        t = pe.matmul(ps_h[s % 2][:, c, :], S.W1[:, c * P:(c + 1) * P], x_t[:, s], start=True, stop=True)
                else:
                    pe.wait_ge(normed, done(q))
                    for c in range(2):
                        for u in range(U):
                            t = pe.transpose(ps_h[s % 2][:, c, u * P:(u + 1) * P],
                                             mean[:, s, u, c * P:(c + 1) * P], S.ident[:])
                t.then_inc(hidden, 1)

            def multiply(i, s):
                q = i * SLOTS + s
                pe.wait_ge(elu_ready, done(q))
                pe.wait_ge(r.ready, behind(q))
                for u in range(U):
                    for c in range(2):
                        t = pe.matmul(ps_o[:, u, 0:H2W], elu[:, s, c, u * P:(u + 1) * P], S.W2x[:, c, :],
                                      start=(c == 0), stop=(c == 1))
                t.then_inc(product, 1)

            pipelined(pe, r.iters, [
                (0, multiply),
                (3, hidden_layer),
                (4, turn),
            ])

        @block.vector
        def _(dve):
            def guard(i, s):
                q = i * SLOTS + s
                dve.wait_ge(normed, free(q))
                r.wait_loads(dve, i, s, 1)
                dve.tensor_scalar(den[:, s], rows[:, s, :, HC:HC + HEADS], 1e-30, None, ALU.max
                                  ).then_inc(safe, 1)

            def invert(i, s):
                q = i * SLOTS + s
                dve.wait_ge(safe, done(q))
                dve.reciprocal(inv[:, s], den[:, s]).then_inc(inverted, 1)

            def divide(i, s):
                q = i * SLOTS + s
                dve.wait_ge(inverted, done(q))
                dve.wait_ge(hidden, free(q))
                for u in range(U):
                    t = dve.tensor_tensor(mean[:, s, u, :].rearrange("p (h c) -> p h c", h=HEADS),
                                          rows[:, s, u, 0:HC].rearrange("p (h c) -> p h c", h=HEADS),
                                          inv[:, s, u, :].unsqueeze(2).to_broadcast([P, HEADS, HID]),
                                          ALU.mult)
                t.then_inc(normed, 1)
                dve.wait_ge(normed, done(q))
                dve.sem_inc(r.used, 1)

            def clip(i, s):
                q = i * SLOTS + s
                dve.wait_ge(hidden, done(q))
                if dense:
                    r.out_free(dve, i, s)
                    dve.tensor_copy(aa[:, s].rearrange("p u k -> p (u k)"), ps_a[:, 0:U * 8]).then_inc(aa_out, 1)
                dve.wait_ge(exped, free(q))
                for c in range(2):
                    t = dve.tensor_scalar(neg[:, s, c, :], ps_h[s % 2][:, c, :], S.b1col[:, c:c + 1], 0.0,
                                          ALU.add, ALU.min)
                t.then_inc(clipped, 1)

            def add(i, s):
                q = i * SLOTS + s
                dve.wait_ge(exped, done(q))
                dve.wait_ge(product, free(q))
                dve.scalar_tensor_tensor(elu[:, s].rearrange("p c r -> p (c r)"),
                                         neg[:, s].rearrange("p c r -> p (c r)"), -1.0,
                                         pos[:, s].rearrange("p c r -> p (c r)"), ALU.add, ALU.add
                                         ).then_inc(elu_ready, 1)

            pipelined(dve, r.iters, [
                (1, add),
                (3, clip),
                *([(4, guard)] if not dense else []),
                *([(4, invert)] if not dense else []),
                *([(4, divide)] if not dense else []),
            ])

        @block.scalar
        def _(act):
            if dense:
                r.prime_stores(act)
            def take_turned(i, s):
                q = i * SLOTS + s
                act.wait_ge(r.used, done(q))
                act.wait_ge(hidden, free(q))
                act.activation(x_t[:, s], ps_t[:], ACT.Copy).then_inc(x_ready, 1)

            def positive(i, s):
                q = i * SLOTS + s
                act.wait_ge(clipped, done(q))
                act.wait_ge(elu_ready, free(q))
                for c in range(2):
                    t = act.activation(pos[:, s, c, :], ps_h[s % 2][:, c, :], ACT.Relu, bias=S.b1col[:, c:c + 1])
                t.then_inc(relued, 1)

            def exponent(i, s):
                q = i * SLOTS + s
                act.wait_ge(clipped, done(q))
                act.wait_ge(elu_ready, free(q))
                act.activation(neg[:, s].rearrange("p c r -> p (c r)"),
                               neg[:, s].rearrange("p c r -> p (c r)"), ACT.Exp).then_inc(exped, 1)

            def take_product(i, s):
                q = i * SLOTS + s
                act.wait_ge(product, done(q))
                r.out_free(act, i, s)
                act.activation(res[:, s], ps_o[:, :, 0:H2W], ACT.Copy).then_inc(r.ready, 1)
                if dense:
                    act.wait_ge(aa_out, done(q))
                    r.store(act, i, s, (res, groups_of(T["H2"])), (aa, groups_of(T["AA"])))

            pipelined(act, r.iters, [
                (0, take_product),
                (2, positive),
                (2, exponent),
                *([(4, take_turned)] if dense else []),
            ])


def attention_phase(nc, T, S, name, H, table, scale, offset, norm=None):
    ET, HT = EDGE_TILES, HALF_T
    tw = table.shape[1]
    with Phase(nc, name) as f:
        base = f.sb("base", [P, 2, ET], I32)
        slot = f.sb("slot", [P, SLOTS, 2, U], I32)
        got = f.sb("got", [P, SLOTS, 2, U, tw])
        terms = f.sb("terms", [P, 2, 2 * H, ET])
        keys = f.sb("keys", [HT, 2, P])
        prv = f.sb("prv", [HT, 2, P])
        nxt = f.sb("nxt", [HT, 2, P])
        pen = f.sb("pen", [HT, 2, 4, P])
        line = f.sb("line", [HT, 2, H, P])
        fwd = f.sb("fwd", [HT, 2, H, P])
        seg = f.sb("seg", [HT, 2, H, P])
        edge_keys = f.sb("edge_keys", [HT, 2, ET])
        own_keys = f.sb("own_keys", [HT, 2, 2])
        apart = f.sb("apart", [HT, 2, 2, 2 * ET])
        ends = f.sb("ends", [HT, H, 2 * ET])
        cand = f.sb("cand", [HT, H, 2 * ET])
        best = f.sb("best", [HT, 2, 2, H])
        most = f.sb("most", [P, H, ET])
        t1 = f.sb("t1", [P, H, ET])
        t2 = f.sb("t2", [P, H, ET])
        m = f.sb("m", [P, H, ET])
        ps_line = f.ps("ps_line", [P, 4, 512])
        ps_back = f.ps("ps_back", [P, 4, 512])
        picked, tick, copied, scaled = (f.sem(n) for n in ("picked", "tick", "copied", "scaled"))
        loaded, stage, turned, turned_back, sent, fetched, exps = (
            f.sem(n) for n in ("loaded", "stage", "turned", "turned_back", "sent", "fetched", "exps"))
        gathered = f.sems("gathered")
        norm = norm(f) if norm else None
        block = f.block()
        iters = EDGE_GROUPS // SLOTS
        marks = {}
        K = T["keys"]

        @block.gpsimd
        def _(pool):
            pool.sem_inc(copied, SLOTS)
            pool.wait_ge(scaled, 2)
            with pool.Fori(0, EDGE_GROUPS // SLOTS) as i:
                for s in range(SLOTS):
                    q = i * SLOTS + s
                    pool.wait_ge(copied, free(q))
                    pool.tensor_copy(slot[:, s], base[:, :, bass.ds(q * U, U)]).then_inc(picked, 1)
                    pool.wait_ge(picked, q + 1)
                    pool.sem_inc(tick, 1)
                    for k in range(2):
                        for u in range(U):
                            gather(pool, got[:, s, k, u, :], table, slot[:, s, k, u:u + 1]
                                   ).then_inc(gathered[s], 16)

        @block.vector
        def _(dve):
            for k, col in enumerate((SRC, DST)):
                dve.tensor_scalar(base[:, k, :], S.coli[:, col, :], float(scale), float(offset), ALU.mult,
                                  ALU.add).then_inc(scaled, 1)
            if norm:
                norm.ln.setup(dve)

            def take_terms(i, s):
                dve.wait_ge(gathered[s], (i + 1) * (16 * 2 * U))
                for k in range(2):
                    t = dve.tensor_copy(terms[:, k, :, bass.ds((i * SLOTS + s) * U, U)],
                                        got[:, s, k, :, 0:2 * H].rearrange("p u k -> p k u"))
                t.then_inc(copied, 1)

            pipelined(dve, iters, [(0, take_terms)], norm.vector_steps(dve) if norm else ())
            n = 0

            def step(*ins):
                nonlocal n
                for x in ins:
                    x.then_inc(stage, 1)
                n += len(ins)
                dve.wait_ge(stage, n)

            def differ(out, a, b):
                return [dve.tensor_tensor(out, a, b, ALU.not_equal)]

            dve.wait_ge(loaded, 16 * 5)
            step(*differ(pen[:, :, 0, :], keys[:], prv[:]), *differ(pen[:, :, 1, :], keys[:], nxt[:]),
                 *differ(pen[:, :, 2, :], keys[:], keys[:, :, 0:1].to_broadcast([HT, 2, P])),
                 *differ(pen[:, :, 3, :], keys[:], keys[:, :, P - 1:P].to_broadcast([HT, 2, P])),
                 dve.tensor_copy(own_keys[:, :, 0:1], keys[:, :, 0:1]),
                 dve.tensor_copy(own_keys[:, :, 1:2], keys[:, :, P - 1:P]))
            step(*[dve.tensor_scalar(apart[:, c, k, :], edge_keys[:].rearrange("p a t -> p (a t)"),
                                     own_keys[:, c, k:k + 1], NEG, ALU.not_equal, ALU.mult)
                   for c in range(2) for k in range(2)],
                 dve.tensor_scalar(pen[:], pen[:], NEG, None, ALU.mult))
            for c in range(2):
                for h in range(H):
                    dve.wait_ge(turned, c * H + h + 1)
                    dve.tensor_copy(line[:, c, h, :], ps_line[0:HT, (c * H + h) % 4, 0:P]).then_inc(stage, 1)
                    n += 1
            marks["lines"] = n
            dve.wait_ge(stage, n)
            step(*[dve.tensor_tensor_scan(fwd[:, c, h, :], pen[:, c, 0, :], line[:, c, h, :], NEG, ALU.add, ALU.max)
                   for c in range(2) for h in range(H)])
            step(*[dve.tensor_tensor_scan(seg[:, c, h, ::-1], pen[:, c, 1, ::-1], fwd[:, c, h, ::-1], NEG,
                                          ALU.add, ALU.max)
                   for c in range(2) for h in range(H)])
            marks["tiles"] = n
            dve.wait_ge(fetched, 16)
            for c in range(2):
                for k in range(2):
                    step(dve.tensor_tensor(cand[:], ends[:], apart[:, c, k, :].unsqueeze(1)
                                           .to_broadcast([HT, H, 2 * ET]), ALU.add))
                    step(dve.tensor_reduce(best[:, c, k, :], cand[:], AX_X, ALU.max))
            for k in range(2):
                step(*[dve.scalar_tensor_tensor(seg[:, c, h, :], pen[:, c, 2 + k, :], best[:, c, k, h:h + 1],
                                                seg[:, c, h, :], ALU.add, ALU.max)
                       for c in range(2) for h in range(H)])
            marks["segments"] = n
            for c in range(2):
                for h in range(H):
                    dve.wait_ge(turned_back, c * H + h + 1)
                    dve.tensor_copy(most[:, h, c * HT:(c + 1) * HT], ps_back[:, (c * H + h) % 4, 0:HT]
                                    ).then_inc(stage, 1)
                    n += 1
            dve.wait_ge(stage, n)

            def leaky(x, y):
                return dve.scalar_tensor_tensor(x, y, SLOPE, y, ALU.mult, ALU.max)

            src_s, dst_s, dst_d = terms[:, 0, 0:H, :], terms[:, 1, 0:H, :], terms[:, 1, H:2 * H, :]
            step(dve.tensor_tensor(most[:], most[:], dst_s, ALU.max))
            step(dve.tensor_tensor(most[:], most[:], dst_d, ALU.add), dve.tensor_tensor(t1[:], src_s, dst_d, ALU.add),
                 dve.tensor_tensor(t2[:], dst_s, dst_d, ALU.add))
            step(leaky(m[:], most[:]), leaky(t1[:], t1[:]), leaky(t2[:], t2[:]))
            step(dve.tensor_tensor(t1[:], t1[:], m[:], ALU.subtract), dve.tensor_tensor(t2[:], t2[:], m[:], ALU.subtract))
            marks["logits"] = n
            dve.wait_ge(exps, 2)

            def by_tile(x):
                return x[:, :, 0:H].rearrange("p t h -> p h t")

            step(dve.tensor_copy(by_tile(S.ws), t1[:]),
                 dve.tensor_tensor(by_tile(S.wd), t2[:], S.colf[:, SF, :].unsqueeze(1).to_broadcast([P, H, ET]),
                                   ALU.mult))
            step(dve.tensor_tensor(by_tile(S.wt), by_tile(S.ws), by_tile(S.wd), ALU.add))

        @block.tensor
        def _(pe):
            pe.wait_ge(copied, EDGE_GROUPS + SLOTS)
            for c in range(2):
                for h in range(H):
                    b = c * H + h
                    if b >= 4:
                        pe.wait_ge(stage, marks["lines"] - 2 * H + b - 3)
                    pe.transpose(ps_line[0:HT, b % 4, 0:P], terms[:, 0, h, c * HT:(c + 1) * HT], S.ident[:]
                                 ).then_inc(turned, 1)
            pe.wait_ge(stage, marks["segments"])
            for c in range(2):
                for h in range(H):
                    b = c * H + h
                    if b >= 4:
                        pe.wait_ge(stage, marks["segments"] + b - 3)
                    pe.transpose(ps_back[:, b % 4, 0:HT], seg[:, c, h, :], S.ident[0:HT, 0:HT]
                                 ).then_inc(turned_back, 1)

        @block.scalar
        def _(act):
            if norm:
                norm.scalar_start(act)
                pipelined(act, iters, [], norm.scalar_steps(act))
            act.wait_ge(stage, marks["logits"])
            act.activation(t1[:], t1[:], ACT.Exp).then_inc(exps, 1)
            act.activation(t2[:], t2[:], ACT.Exp).then_inc(exps, 1)

        @block.sync
        def _(sp):
            for out, at in ((prv, 0), (keys, 1), (nxt, 2)):
                sp.dma_start(out[:], K[0, at:at + ET * P].rearrange("(c p e) -> p c e", p=HT, e=P)
                             ).then_inc(loaded, 16)
            with nc.allow_non_contiguous_dma(reason="first key of each tile"):
                sp.dma_start(edge_keys[:, 0, :], K[0:1, 1:1 + ET * P].rearrange("o (t e) -> o t e", e=P)[:, :, 0]
                             .to_broadcast([HT, ET])).then_inc(loaded, 16)
            sp.dma_start(edge_keys[:, 1, :], T["last"][0:1, 0:ET].to_broadcast([HT, ET])).then_inc(loaded, 16)
            if norm:
                norm.sync_start(sp)
                pipelined(sp, iters, [], norm.sync_steps(sp))
            sp.wait_ge(stage, marks["tiles"])
            dst = T["ends"][0:H, :].rearrange("h (k c p) -> k p c h", k=2, p=HT)
            with nc.allow_non_contiguous_dma(reason="one value per tile, head and end"):
                for k, e in ((0, 0), (1, P - 1)):
                    for c in range(2):
                        sp.dma_start(dst[k, :, c, :], seg[:, c, :, e]).then_inc(sent, 16)
            sp.wait_ge(sent, 64)
            sp.dma_start(ends[:], T["ends"][0:H, :].unsqueeze(0).to_broadcast([HT, H, 2 * ET])).then_inc(fetched, 16)
            if norm:
                norm.r.finish(sp)


def gat_sum(nc, T, S, name, layer):
    first = layer == 1
    table = T["X1"] if first else T["H2"]
    out = T["RAW260"] if first else T["RAW129"]
    H = HEADS if first else 1
    w = out.shape[1]
    wt = table.shape[1]
    D = w - H
    with Phase(nc, name) as f:
        slot = f.sb("slot", [P, SLOTS, 2, U], I32)
        rows = f.sb("rows", [P, SLOTS, 2, U, wt])
        x_t = f.sb("x_t", [P, 2, U * P])
        v = f.sb("v", [P, SLOTS, U, w])
        part = f.sb("part", [P, SLOTS, U, D])
        krow = f.sb("krow", [P, SLOTS, U * P])
        same = f.sb("same", [P, SLOTS, U, P])
        sums = f.sb("sums", [P, SLOTS, U, w])
        ps_t = f.ps("ps_t", [P, 2, 512])
        ps_h = f.ps("ps_h", [P, 2, U, 256]) if first else None
        acc = f.ps("acc", [P, 2, 512])
        picked, tick, matched, summed, copied, turned, x_ready, hidden, weighted, parted, valued = (
            f.sem(n) for n in ("picked", "tick", "matched", "summed", "copied", "turned", "x_ready", "hidden",
                               "weighted", "parted", "valued"))
        gathered, keyed, stored = f.sems("gathered"), f.sems("keyed"), f.sems("stored")
        primed = prime_stores(f, stored, 1, S.ident_dram)
        block = f.block()
        iters = EDGE_GROUPS // SLOTS
        out_g = groups_of(out)
        rows_used = turned if first else valued

        @block.sync
        def _(sp):
            for m in (matched, turned, x_ready, hidden, weighted, parted, valued):
                sp.sem_inc(m, SLOTS)
            for m in (summed, copied):
                sp.sem_inc(m, 2 * SLOTS)
            with sp.Fori(0, iters) as i:
                for s in range(SLOTS):
                    q = i * SLOTS + s
                    sp.wait_ge(matched, free(q))
                    sp.dma_start(krow[:, s], T["keys"][0:1, bass.ds(q * (U * P) + 1, U * P)]
                                 .to_broadcast([P, U * P])).then_inc(keyed[s], 16)
            for s in range(SLOTS):
                sp.wait_ge(stored[s], 16 * (iters + 1))

        @block.gpsimd
        def _(pool):
            with pool.Fori(0, iters) as i:
                for s in range(SLOTS):
                    q = i * SLOTS + s
                    pool.wait_ge(rows_used, free(q))
                    for k, col in enumerate((SRC, DST)):
                        t = pool.tensor_copy(slot[:, s, k], S.coli[:, col, bass.ds(q * U, U)])
                    t.then_inc(picked, 1)
                    pool.wait_ge(picked, q + 1)
                    pool.sem_inc(tick, 1)
                    for k in range(2):
                        for u in range(U):
                            gather(pool, rows[:, s, k, u, :], table, slot[:, s, k, u:u + 1]
                                   ).then_inc(gathered[s], 16)

        @block.tensor
        def _(pe):
            with pe.Fori(0, iters) as i:
                for s in range(SLOTS):
                    q = i * SLOTS + s
                    if first:
                        pe.wait_ge(gathered[s], (i + 1) * (16 * 2 * U))
                        pe.wait_ge(x_ready, behind(q))
                        for k in range(2):
                            for u in range(U):
                                t = pe.transpose(ps_t[:, k, u * P:(u + 1) * P], rows[:, s, k, u, :], S.ident[:])
                        t.then_inc(turned, 1)
                        pe.wait_ge(x_ready, done(q))
                        pe.wait_ge(parted, behind(q))
                        for k in range(2):
                            for u in range(U):
                                t = pe.matmul(ps_h[:, k, u, :], x_t[:, k, u * P:(u + 1) * P], S.W1[:],
                                              start=True, stop=True)
                        t.then_inc(hidden, 1)
                for s in range(SLOTS):
                    q = i * SLOTS + s
                    pe.wait_ge(valued, done(q))
                    pe.wait_ge(matched, done(q))
                    for half in range(2):
                        pe.wait_ge(copied, q * 2 + (half + 2 * SLOTS))
                        for b in range(2):
                            u = 2 * half + b
                            t = pe.matmul(acc[:, b, 0:w], same[:, s, u, :], v[:, s, u, :], start=True, stop=True)
                        t.then_inc(summed, 1)

        @block.vector
        def _(dve):
            with dve.Fori(0, iters) as i:
                for s in range(SLOTS):
                    q = i * SLOTS + s
                    dve.wait_ge(keyed[s], (i + 1) * 16)
                    dve.wait_ge(summed, q * 2 + 2)
                    dve.tensor_tensor(same[:, s], krow[:, s].rearrange("p (u e) -> p u e", u=U),
                                      S.colf[:, KD, bass.ds(q * U, U)].unsqueeze(2).to_broadcast([P, U, P]),
                                      ALU.is_equal).then_inc(matched, 1)
                for s in range(SLOTS):
                    q = i * SLOTS + s
                    if first:
                        dve.wait_ge(hidden, done(q))
                    else:
                        dve.wait_ge(gathered[s], (i + 1) * (16 * 2 * U))

                    def values(k):
                        if first:
                            return ps_h[:, k].rearrange("p u (h c) -> p (u h) c", h=HEADS)
                        return rows[:, s, k, :, 0:C]

                    def heads(x):
                        return x.rearrange("p u (h c) -> p u h c", h=H)

                    for k, (dest, wgt, mark) in enumerate(((v[:, s, :, 0:D], S.ws, weighted),
                                                           (part[:, s], S.wd, parted))):
                        wcol = wgt[:, bass.ds(q * U, U), 0:H]
                        if first:
                            dve.tensor_tensor(heads(dest), heads(ps_h[:, k]),
                                              wcol.unsqueeze(3).to_broadcast([P, U, H, HID]), ALU.mult
                                              ).then_inc(mark, 1)
                        else:
                            dve.tensor_tensor(dest, rows[:, s, k, :, 0:C], wcol.to_broadcast([P, U, C]), ALU.mult
                                              ).then_inc(mark, 1)
                    dve.tensor_copy(v[:, s, :, D:w], S.wt[:, bass.ds(q * U, U), 0:H])
                    dve.wait_ge(weighted, done(q))
                    dve.wait_ge(parted, done(q))
                    dve.tensor_tensor(v[:, s, :, 0:D], v[:, s, :, 0:D], part[:, s], ALU.add).then_inc(valued, 1)

        @block.scalar
        def _(act):
            primed(act)
            with act.Fori(0, iters) as i:
                if first:
                    for s in range(SLOTS):
                        q = i * SLOTS + s
                        act.wait_ge(turned, done(q))
                        act.wait_ge(hidden, behind(q))
                        act.activation(x_t[:], ps_t[:], ACT.Copy).then_inc(x_ready, 1)
                for s in range(SLOTS):
                    q = i * SLOTS + s
                    act.wait_ge(stored[s], (i + 1) * 16)
                    for half in range(2):
                        act.wait_ge(summed, q * 2 + (half + 2 * SLOTS + 1))
                        act.activation(sums[:, s, 2 * half:2 * half + 2, :], acc[:, :, 0:w], ACT.Copy
                                       ).then_inc(copied, 1)
                    act.wait_ge(copied, q * 2 + (2 * SLOTS + 2))
                    act.dma_start(out_g[q], sums[:, s]).then_inc(stored[s], 16)


def gat_nodes(nc, T, S):
    with Phase(nc, "gatnodes") as f:
        r = Rows(f, S, dense=False, stores=U)
        rows = f.sb("rows", [P, SLOTS, U, C + 1])
        own = f.sb("own", [P, SLOTS, U, C])
        den = f.sb("den", [P, SLOTS, U, 1])
        inv = f.sb("inv", [P, SLOTS, U, 1])
        z = f.sb("z", [P, SLOTS, U, C])
        res = f.sb("res", [P, SLOTS, U, C])
        ln = LayerNorm(f)
        safe, inverted, owned = f.sem("safe"), f.sem("inverted"), f.sem("owned")
        block = f.block()

        @block.sync
        def _(sp):
            r.prime(sp, (safe, inverted, owned, *ln.sems))
            r.load(sp, [(rows, groups_of(T["RAW129"]))])
            r.finish(sp)

        @block.gpsimd
        def _(pool):
            r.prime_stores(pool)
            r.pool_loop(pool, gathers=(own, T["X1"], DST, owned), scatters=(res, T["X2"], SCD, NP_),
                        ahead=5)

        @block.vector
        def _(dve):
            ln.setup(dve)
            def guard(i, s):
                q = i * SLOTS + s
                dve.wait_ge(r.ready, free(q))
                r.wait_loads(dve, i, s, 1)
                dve.tensor_scalar(den[:, s], rows[:, s, :, C:C + 1], 1e-30, None, ALU.max).then_inc(safe, 1)

            def invert(i, s):
                q = i * SLOTS + s
                dve.wait_ge(safe, done(q))
                dve.reciprocal(inv[:, s], den[:, s]).then_inc(inverted, 1)

            def divide(i, s):
                q = i * SLOTS + s
                dve.wait_ge(inverted, done(q))
                dve.tensor_tensor(z[:, s], rows[:, s, :, 0:C], inv[:, s].to_broadcast([P, U, C]), ALU.mult
                                  ).then_inc(r.used, 1)

            def add_own(i, s):
                q = i * SLOTS + s
                r.wait_loads(dve, i, s, 0, 1)
                dve.wait_ge(r.used, done(q))
                dve.tensor_tensor(z[:, s], z[:, s], own[:, s], ALU.add).then_inc(owned, 1)

            def add_bias(i, s):
                q = i * SLOTS + s
                dve.wait_ge(owned, done(q))
                dve.tensor_tensor(z[:, s], z[:, s], bc_rows(S.b2[:]), ALU.add).then_inc(ln.z_ready, 1)

            def moments(i, s):
                ln.moments(dve, i, s, z, r.tick)

            def factors(i, s):
                ln.factors(dve, i, s)

            pipelined(dve, r.iters, [
                (0, factors),
                (2, guard),
                (2, invert),
                (2, divide),
                (2, add_own),
                (2, add_bias),
                (2, moments),
            ])

        @block.scalar
        def _(act):
            act.wait_ge(ln.eps_set, 1)
            def deviation(i, s):
                ln.deviation(act, i, s)

            def scale(i, s):
                ln.scale(act, i, s, z, res, r.ready, r)

            pipelined(act, r.iters, [
                (0, scale),
                (1, deviation),
            ])



def gin_rows(nc, T, A, S, name, dense, beside=None):
    with Phase(nc, name) as f:
        r = Rows(f, S, dense, stores=1 if dense else U)
        x = f.sb("x", [P, SLOTS, U, C])
        agg = None if dense else f.sb("agg", [P, SLOTS, U, C + 1])
        turned_t = f.sb("turned_t", [P, SLOTS, U * P])
        agg_t = None if dense else f.sb("agg_t", [P, SLOTS, U * P])
        pre_t = None if dense else f.sb("pre_t", [P, SLOTS, U * P])
        pre = None if dense else f.sb("pre", [P, SLOTS, U, C])
        hid = None if dense else f.sb("hid", [P, SLOTS, U * P])
        add = None if dense else f.sb("add", [P, SLOTS, U, C])
        w = f.sb("w", [P, 3, C])
        rows = f.sb("rows", [P, 4, C])
        b1 = f.sb("b1", [P, 1])
        z = f.sb("z", [P, SLOTS, U, C])
        y = f.sb("y", [P, SLOTS, U, C])
        shifted = f.sb("shifted", [P, SLOTS, U, C])
        z2 = f.sb("z2", [P, SLOTS, U, C])
        res = f.sb("res", [P, SLOTS, U, C])
        ps_t = f.ps("ps_t", [P, U * P])
        ps_o = [f.ps(f"ps_o{s}", [P, U * P]) for s in range(2)]
        ps_g = None if dense else f.ps("ps_g", [P, U * P])
        ps_p = None if dense else f.ps("ps_p", [P, U * P])
        ps_r = None if dense else f.ps("ps_r", [P, U * P])
        ps_1 = None if dense else f.ps("ps_1", [P, U * P])
        ps_2 = None if dense else f.ps("ps_2", [P, U * P])
        ln, ln2 = LayerNorm(f), LayerNorm(f, "2")
        turned, turned_out, own_h, normed, gained = (f.sem(n) for n in (
            "turned", "turned_out", "own_h", "normed", "gained"))
        shifted_x = f.sem("shifted_x")
        agg_turned, agg_out, pre_ready, counted, pre_turned, pre_out, layer1, relued, layer2, biased, added = (
            f.sem(n) for n in ("agg_turned", "agg_out", "pre_ready", "counted", "pre_turned", "pre_out", "layer1",
                               "relued", "layer2", "biased", "added"))
        sums = beside(f) if beside else None
        block = f.block()

        def run(eng, engine, steps):
            if sums:
                pipelined(eng, sums.iters, steps_of(sums, engine, eng), steps)
            else:
                pipelined(eng, r.iters, steps)

        @block.sync
        def _(sp):
            for out, src in ((w[:, 0, :], A["L2_Wpre"]), (w[:, 1, :], A["L2_W1"]), (w[:, 2, :], A["L2_W2"]),
                             (rows[:, 0, :], A["L2_bpre_rows"]), (rows[:, 1, :], A["L2_b2_rows"]),
                             (rows[:, 2, :], A["L2_gamma_rows"]), (rows[:, 3, :], A["L2_beta_rows"]),
                             (b1[:], A["L2_b1_col"])):
                sp.dma_start(out, src).then_inc(r.weights, 16)
            r.prime(sp, (shifted_x, turned, turned_out, own_h, normed, gained, agg_turned, agg_out, pre_ready, counted,
                         pre_turned, pre_out, layer1, relued, layer2, biased, added, *ln.sems, *ln2.sems))
            if sums:
                sums.sync_start(sp)
            run(sp, "sync", [(10 if dense else 0, r.load_step(
                sp, [(x, groups_of(T["X2"]))] if dense else [(agg, groups_of(T["RAW129"]))]))])
            r.finish(sp)
            if sums:
                sums.sync_end(sp)

        @block.gpsimd
        def _(pool):
            if sums:
                sums.pool_loop(pool)
            if not dense:
                r.prime_stores(pool)
                r.pool_loop(pool, gathers=(x, T["X2"], DST, shifted_x), scatters=(res, T["X3"], SCD, NP_),
                            ahead=9)

        @block.tensor
        def _(pe):
            pe.wait_ge(r.weights, 16 * 8)
            if sums:
                sums.tensor_start(pe)

            def aggregate(i, s):
                q = i * SLOTS + s
                r.wait_loads(pe, i, s, 1)
                pe.wait_ge(agg_out, behind(q))
                for u in range(U):
                    t = pe.transpose(ps_g[:, u * P:(u + 1) * P], agg[:, s, u, 0:C], S.ident[:])
                t.then_inc(agg_turned, 1)

            def pre_layer(i, s):
                q = i * SLOTS + s
                pe.wait_ge(agg_out, done(q))
                pe.wait_ge(counted, behind(q))
                for u in range(U):
                    t = pe.matmul(ps_p[:, u * P:(u + 1) * P], agg_t[:, s, u * P:(u + 1) * P], w[:, 0, :],
                                  start=True, stop=True)
                t.then_inc(pre_ready, 1)

            def turn(i, s):
                q = i * SLOTS + s
                r.wait_loads(pe, i, s, 1 if dense else 0, 0 if dense else 1)
                pe.wait_ge(turned_out, behind(q))
                for u in range(U):
                    t = pe.transpose(ps_t[:, u * P:(u + 1) * P], x[:, s, u, :], S.ident[:])
                t.then_inc(turned, 1)

            def turn_pre(i, s):
                q = i * SLOTS + s
                pe.wait_ge(counted, done(q))
                pe.wait_ge(pre_out, behind(q))
                for u in range(U):
                    t = pe.transpose(ps_r[:, u * P:(u + 1) * P], pre[:, s, u, :], S.ident[:])
                t.then_inc(pre_turned, 1)

            def layer_1(i, s):
                q = i * SLOTS + s
                pe.wait_ge(pre_out, done(q))
                pe.wait_ge(relued, behind(q))
                pe.matmul(ps_1[:], w[:, 1, :], pre_t[:, s], start=True, stop=True).then_inc(layer1, 1)

            def layer_2(i, s):
                q = i * SLOTS + s
                pe.wait_ge(relued, done(q))
                pe.wait_ge(biased, behind(q))
                for u in range(U):
                    t = pe.matmul(ps_2[:, u * P:(u + 1) * P], hid[:, s, u * P:(u + 1) * P], w[:, 2, :],
                                  start=True, stop=True)
                t.then_inc(layer2, 1)

            def own(i, s):
                q = i * SLOTS + s
                pe.wait_ge(turned_out, done(q))
                pe.wait_ge(ln.z_ready, two_behind(q))
                for u in range(U):
                    t = pe.matmul(ps_o[s % 2][:, u * P:(u + 1) * P], turned_t[:, s, u * P:(u + 1) * P], w[:, 0, :],
                                  start=True, stop=True)
                t.then_inc(own_h, 1)

            run(pe, "tensor", [
                (5, own),
                *([(5, layer_2), (6, layer_1)] if not dense else []),
                (6, turn),
                *([(7, turn_pre), (8, pre_layer), (9, aggregate)] if not dense else []),
            ])

        @block.scalar
        def _(act):
            act.wait_ge(r.weights, 16 * 8)
            act.wait_ge(ln.eps_set, 1)
            act.wait_ge(ln2.eps_set, 1)
            if dense:
                r.prime_stores(act)
            if sums:
                sums.prime_stores(act)

            def take_agg(i, s):
                q = i * SLOTS + s
                act.wait_ge(agg_turned, done(q))
                act.wait_ge(pre_ready, free(q))
                act.activation(agg_t[:, s], ps_g[:], ACT.Copy).then_inc(agg_out, 1)

            def take_turned(i, s):
                q = i * SLOTS + s
                act.wait_ge(turned, done(q))
                act.wait_ge(own_h, free(q))
                act.activation(turned_t[:, s], ps_t[:], ACT.Copy).then_inc(turned_out, 1)

            def take_pre(i, s):
                q = i * SLOTS + s
                act.wait_ge(pre_turned, done(q))
                act.wait_ge(layer1, free(q))
                act.activation(pre_t[:, s], ps_r[:], ACT.Copy).then_inc(pre_out, 1)

            def take_hidden(i, s):
                q = i * SLOTS + s
                act.wait_ge(layer1, done(q))
                act.wait_ge(layer2, free(q))
                act.activation(hid[:, s], ps_1[:], ACT.Relu, bias=b1[:]).then_inc(relued, 1)

            def deviation(i, s):
                ln.deviation(act, i, s)

            def scale(i, s):
                ln.scale(act, i, s, z, y, normed)

            def deviation2(i, s):
                ln2.deviation(act, i, s)

            def scale2(i, s):
                ln2.scale(act, i, s, z2, res, r.ready, r, groups_of(T["X3"]) if dense else None)

            run(act, "scalar", [
                (0, scale2),
                (1, deviation2),
                (3, scale),
                (4, deviation),
                *([(6, take_hidden)] if not dense else []),
                (6, take_turned),
                *([(7, take_pre), (9, take_agg)] if not dense else []),
            ])

        @block.vector
        def _(dve):
            ln.setup(dve)
            ln2.setup(dve)
            if sums:
                sums.vector_start(dve)
            dve.wait_ge(r.weights, 16 * 8)
            def add_counted(i, s):
                q = i * SLOTS + s
                dve.wait_ge(pre_turned, free(q))
                dve.wait_ge(pre_ready, done(q))
                for u in range(U):
                    t = dve.scalar_tensor_tensor(pre[:, s, u, :], rows[:, 0, :], agg[:, s, u, C:C + 1],
                                                 ps_p[:, u * P:(u + 1) * P], ALU.mult, ALU.add)
                t.then_inc(counted, 1)
                dve.wait_ge(counted, done(q))
                dve.sem_inc(r.used, 1)

            def add_b2(i, s):
                q = i * SLOTS + s
                dve.wait_ge(layer2, done(q))
                dve.wait_ge(ln.z_ready, free(q))
                dve.tensor_tensor(add[:, s], ps_2[:].rearrange("p (u c) -> p u c", u=U),
                                  bc_rows(rows[:, 1, :]), ALU.add).then_inc(biased, 1)

            def relu(i, s):
                q = i * SLOTS + s
                dve.wait_ge(biased, done(q))
                for u in range(U):
                    t = dve.scalar_tensor_tensor(add[:, s, u, :], add[:, s, u, :], 0.0, rows[:, 0, :],
                                                 ALU.max, ALU.add)
                t.then_inc(added, 1)

            def add_hidden(i, s):
                q = i * SLOTS + s
                dve.wait_ge(own_h, done(q))
                dve.wait_ge(normed, free(q))
                if not dense:
                    dve.wait_ge(added, done(q))
                dve.tensor_tensor(z[:, s], ps_o[s % 2][:].rearrange("p (u c) -> p u c", u=U),
                                  bc_rows(S.c2[:]) if dense else add[:, s], ALU.add).then_inc(ln.z_ready, 1)

            def moments(i, s):
                ln.moments(dve, i, s, z, r.tick)

            def factors(i, s):
                ln.factors(dve, i, s)

            def gain(i, s):
                q = i * SLOTS + s
                dve.wait_ge(normed, done(q))
                dve.wait_ge(r.ready, free(q))
                dve.tensor_tensor(z2[:, s], y[:, s], bc_rows(rows[:, 2, :]), ALU.mult).then_inc(gained, 1)

            def shift(i, s):
                q = i * SLOTS + s
                dve.wait_ge(turned, done(q))
                r.wait_loads(dve, i, s, 1 if dense else 0, 0 if dense else 1)
                dve.wait_ge(ln2.z_ready, free(q))
                dve.tensor_tensor(shifted[:, s], x[:, s], bc_rows(rows[:, 3, :]), ALU.add
                                  ).then_inc(r.used if dense else shifted_x, 1)

            def add_own(i, s):
                q = i * SLOTS + s
                dve.wait_ge(gained, done(q))
                dve.wait_ge(r.used if dense else shifted_x, done(q))
                dve.tensor_tensor(z2[:, s], z2[:, s], shifted[:, s], ALU.add).then_inc(ln2.z_ready, 1)

            def moments2(i, s):
                ln2.moments(dve, i, s, z2, r.tick)

            def factors2(i, s):
                ln2.factors(dve, i, s)

            run(dve, "vector", [
                (0, factors2),
                (2, gain),
                (2, add_own),
                (2, moments2),
                (3, factors),
                *([(5, add_b2)] if not dense else []),
                *([(5, relu)] if not dense else []),
                (5, add_hidden),
                (5, moments),
                (6, shift),
                *([(8, add_counted)] if not dense else []),
            ])


class Softplus:

    def __init__(self, f, name):
        self.absx = f.sb(f"absx{name}", [P, SLOTS, U * P])
        self.lg = f.sb(f"lg{name}", [P, SLOTS, U * P])
        self.abs_ready, self.exp_ready, self.log_ready = (f.sem(f"{n}{name}") for n in (
            "abs_ready", "exp_ready", "log_ready"))
        self.sems = [self.abs_ready, self.exp_ready, self.log_ready]

    def magnitude(self, act, i, s, x, x_ready, bias=0.0):
        q = i * SLOTS + s
        act.wait_ge(x_ready, done(q))
        act.wait_ge(self.log_ready, free(q))
        act.activation(self.absx[:, s], x, ACT.Abs, bias=bias).then_inc(self.abs_ready, 1)

    def exponential(self, act, i, s):
        q = i * SLOTS + s
        act.wait_ge(self.abs_ready, done(q))
        act.activation(self.absx[:, s], self.absx[:, s], ACT.Exp, scale=-1.0).then_inc(self.exp_ready, 1)

    def logarithm(self, act, i, s, used, one):
        q = i * SLOTS + s
        act.wait_ge(self.exp_ready, done(q))
        act.wait_ge(used, free(q))
        act.activation(self.lg[:, s], self.absx[:, s], ACT.Ln, bias=one).then_inc(self.log_ready, 1)


def messages(nc, T, A, S):
    with Phase(nc, "messages") as f:
        r = Rows(f, S, dense=True, stores=1, groups=EDGE_GROUPS)
        e = f.sb("e", [P, SLOTS, U, C])
        x = f.sb("x", [P, SLOTS, U, C])
        e_t = f.sb("e_t", [P, SLOTS, U * P])
        x_t = f.sb("x_t", [P, SLOTS, U * P])
        w = f.sb("w", [P, 3, C])
        rows = f.sb("rows", [P, 2, C])
        be1 = f.sb("be1", [P, 1])
        one = f.sb("one", [P, 1])
        pos = f.sb("pos", [P, SLOTS, U * P])
        act1 = f.sb("act1", [P, SLOTS, U * P])
        y = f.sb("y", [P, SLOTS, U, C])
        filt = f.sb("filt", [P, SLOTS, U, C])
        hn = f.sb("hn", [P, SLOTS, U, C])
        res = f.sb("res", [P, SLOTS, U, C])
        ps_e = f.ps("ps_e", [P, U * P])
        ps_x = f.ps("ps_x", [P, U * P])
        ps_1 = [f.ps(f"ps_1{s}", [P, U * P]) for s in range(2)]
        ps_2 = [f.ps(f"ps_2{s}", [P, U * P]) for s in range(2)]
        ps_n = f.ps("ps_n", [P, U * P])
        sp1, sp2 = Softplus(f, "1"), Softplus(f, "2")
        x_used, e_out, x_out, layer1, clipped, act1_ready, layer2, y_ready, node, hn_ready, filt_ready, one_set = (
            f.sem(n) for n in ("x_used", "e_out", "x_out", "layer1", "clipped", "act1_ready", "layer2", "y_ready",
                               "node", "hn_ready", "filt_ready", "one_set"))
        block = f.block()

        @block.sync
        def _(sp):
            for out, src in ((w[:, 0, :], A["L3_We1T"]), (w[:, 1, :], A["L3_We2T"]), (w[:, 2, :], A["L3_WnT"]),
                             (rows[:, 0, :], A["L3_be2_rows"]), (rows[:, 1, :], A["L3_bn_rows"]),
                             (be1[:], A["L3_be1_col"])):
                sp.dma_start(out, src).then_inc(r.weights, 16)
            r.prime(sp, (x_used, e_out, x_out, layer1, clipped, act1_ready, layer2, y_ready, node, hn_ready,
                         filt_ready, *sp1.sems, *sp2.sems))
            r.load(sp, [(e, groups_of(A["edge_attr"]))])
            r.finish(sp)

        @block.gpsimd
        def _(pool):
            r.pool_loop(pool, gathers=(x, T["X3"], SRCO, x_used))

        @block.tensor
        def _(pe):
            pe.wait_ge(r.weights, 16 * 6)
            def turn_e(i, s):
                q = i * SLOTS + s
                r.wait_loads(pe, i, s, 1)
                pe.wait_ge(e_out, behind(q))
                for u in range(U):
                    t = pe.transpose(ps_e[:, u * P:(u + 1) * P], e[:, s, u, :], S.ident[:])
                t.then_inc(r.used, 1)

            def turn_x(i, s):
                q = i * SLOTS + s
                r.wait_loads(pe, i, s, 0, 1)
                pe.wait_ge(x_out, behind(q))
                for u in range(U):
                    t = pe.transpose(ps_x[:, u * P:(u + 1) * P], x[:, s, u, :], S.ident[:])
                t.then_inc(x_used, 1)

            def layer_1(i, s):
                q = i * SLOTS + s
                pe.wait_ge(e_out, done(q))
                pe.wait_ge(clipped, two_behind(q))
                pe.wait_ge(sp1.abs_ready, two_behind(q))
                pe.matmul(ps_1[s % 2][:], w[:, 0, :], e_t[:, s], start=True, stop=True).then_inc(layer1, 1)

            def node_layer(i, s):
                q = i * SLOTS + s
                pe.wait_ge(x_out, done(q))
                pe.wait_ge(hn_ready, behind(q))
                for u in range(U):
                    t = pe.matmul(ps_n[:, u * P:(u + 1) * P], x_t[:, s, u * P:(u + 1) * P], w[:, 2, :],
                                  start=True, stop=True)
                t.then_inc(node, 1)

            def layer_2(i, s):
                q = i * SLOTS + s
                pe.wait_ge(act1_ready, done(q))
                pe.wait_ge(y_ready, two_behind(q))
                for u in range(U):
                    t = pe.matmul(ps_2[s % 2][:, u * P:(u + 1) * P], act1[:, s, u * P:(u + 1) * P], w[:, 1, :],
                                  start=True, stop=True)
                t.then_inc(layer2, 1)

            pipelined(pe, r.iters, [
                (3, layer_2),
                (5, node_layer),
                (6, layer_1),
                (7, turn_e),
                (7, turn_x),
            ])

        @block.scalar
        def _(act):
            act.wait_ge(r.weights, 16 * 6)
            act.wait_ge(one_set, 1)
            r.prime_stores(act)
            def take_e(i, s):
                q = i * SLOTS + s
                act.wait_ge(r.used, done(q))
                act.wait_ge(layer1, free(q))
                act.activation(e_t[:, s], ps_e[:], ACT.Copy).then_inc(e_out, 1)

            def take_x(i, s):
                q = i * SLOTS + s
                act.wait_ge(x_used, done(q))
                act.wait_ge(node, free(q))
                act.activation(x_t[:, s], ps_x[:], ACT.Copy).then_inc(x_out, 1)

            def abs_1(i, s):
                sp1.magnitude(act, i, s, ps_1[s % 2][:], clipped, bias=be1[:])

            def abs_2(i, s):
                sp2.magnitude(act, i, s, y[:, s].rearrange("p u c -> p (u c)"), y_ready)

            def store(i, s):
                r.store(act, i, s, (res, groups_of(T["M"])))

            pipelined(act, r.iters, [
                (0, store),
                (2, abs_2),
                (5, abs_1),
                (2, lambda i, s: sp2.exponential(act, i, s)),
                (5, lambda i, s: sp1.exponential(act, i, s)),
                (2, lambda i, s: sp2.logarithm(act, i, s, filt_ready, one[:])),
                (5, lambda i, s: sp1.logarithm(act, i, s, act1_ready, one[:])),
                (7, take_e),
                (7, take_x),
            ])

        @block.vector
        def _(dve):
            dve.memset(one[:], 1.0).then_inc(one_set, 1)
            dve.wait_ge(r.weights, 16 * 6)
            def clip(i, s):
                q = i * SLOTS + s
                dve.wait_ge(act1_ready, free(q))
                dve.wait_ge(layer1, done(q))
                dve.tensor_scalar(pos[:, s], ps_1[s % 2][:], be1[:], 0.0, ALU.add, ALU.max).then_inc(clipped, 1)

            def node_bias(i, s):
                q = i * SLOTS + s
                dve.wait_ge(node, done(q))
                dve.wait_ge(r.ready, free(q))
                dve.tensor_tensor(hn[:, s], ps_n[:].rearrange("p (u c) -> p u c", u=U), bc_rows(rows[:, 1, :]),
                                  ALU.add).then_inc(hn_ready, 1)

            def activate(i, s):
                q = i * SLOTS + s
                dve.wait_ge(sp1.log_ready, done(q))
                dve.wait_ge(clipped, done(q))
                dve.wait_ge(layer2, free(q))
                dve.scalar_tensor_tensor(act1[:, s], sp1.lg[:, s], -LOG2, pos[:, s], ALU.add, ALU.add
                                         ).then_inc(act1_ready, 1)

            def bias2(i, s):
                q = i * SLOTS + s
                dve.wait_ge(layer2, done(q))
                dve.wait_ge(sp2.abs_ready, free(q))
                dve.wait_ge(filt_ready, free(q))
                dve.tensor_tensor(y[:, s], ps_2[s % 2][:].rearrange("p (u c) -> p u c", u=U), bc_rows(rows[:, 0, :]),
                                  ALU.add).then_inc(y_ready, 1)

            def filter(i, s):
                q = i * SLOTS + s
                dve.wait_ge(sp2.log_ready, done(q))
                dve.wait_ge(r.ready, free(q))
                dve.scalar_tensor_tensor(filt[:, s].rearrange("p u c -> p (u c)"),
                                         y[:, s].rearrange("p u c -> p (u c)"), 0.0, sp2.lg[:, s],
                                         ALU.max, ALU.add).then_inc(filt_ready, 1)

            def message(i, s):
                q = i * SLOTS + s
                dve.wait_ge(filt_ready, done(q))
                dve.wait_ge(hn_ready, done(q))
                r.out_free(dve, i, s)
                dve.scalar_tensor_tensor(res[:, s].rearrange("p u c -> p (u c)"),
                                         filt[:, s].rearrange("p u c -> p (u c)"), -LOG2,
                                         hn[:, s].rearrange("p u c -> p (u c)"), ALU.add, ALU.mult
                                         ).then_inc(r.ready, 1)

            pipelined(dve, r.iters, [
                (1, filter),
                (1, message),
                (3, bias2),
                (4, activate),
                (5, node_bias),
                (6, clip),
            ])


def schnet_rows(nc, T, A, S, out):
    with Phase(nc, "schnet") as f:
        r = Rows(f, S, dense=False, stores=U)
        agg = f.sb("agg", [P, SLOTS, U, C])
        own = f.sb("own", [P, SLOTS, U, C])
        agg_t = f.sb("agg_t", [P, SLOTS, U * P])
        w = f.sb("w", [P, 2, C])
        brow = f.sb("brow", [P, C])
        b1 = f.sb("b1", [P, 1])
        one = f.sb("one", [P, 1])
        pos = f.sb("pos", [P, SLOTS, U * P])
        hid = f.sb("hid", [P, SLOTS, U * P])
        z = f.sb("z", [P, SLOTS, U, C])
        res = f.sb("res", [P, SLOTS, U, C])
        ps_t = f.ps("ps_t", [P, U * P])
        ps_1 = [f.ps(f"ps_1{s}", [P, U * P]) for s in range(2)]
        ps_2 = [f.ps(f"ps_2{s}", [P, U * P]) for s in range(2)]
        sp1 = Softplus(f, "1")
        ln = LayerNorm(f)
        agg_out, layer1, clipped, hid_ready, layer2, owned, one_set = (f.sem(n) for n in (
            "agg_out", "layer1", "clipped", "hid_ready", "layer2", "owned", "one_set"))
        block = f.block()

        @block.sync
        def _(sp):
            for dst, src in ((w[:, 0, :], A["L3_Wfc1T"]), (w[:, 1, :], A["L3_Wfc2T"]),
                             (brow[:], A["L3_bfc2_rows"]), (b1[:], A["L3_bfc1_col"])):
                sp.dma_start(dst, src).then_inc(r.weights, 16)
            r.prime(sp, (agg_out, layer1, clipped, hid_ready, layer2, owned, *sp1.sems, *ln.sems))
            r.load(sp, [(agg, groups_of(T["RAW128"]))])
            r.finish(sp)

        @block.gpsimd
        def _(pool):
            r.prime_stores(pool)
            r.pool_loop(pool, gathers=(own, T["X3"], DST, owned), scatters=(res, out, SCD, NP_), ahead=5)

        @block.tensor
        def _(pe):
            pe.wait_ge(r.weights, 16 * 4)
            def turn(i, s):
                q = i * SLOTS + s
                r.wait_loads(pe, i, s, 1)
                pe.wait_ge(agg_out, behind(q))
                for u in range(U):
                    t = pe.transpose(ps_t[:, u * P:(u + 1) * P], agg[:, s, u, :], S.ident[:])
                t.then_inc(r.used, 1)

            def layer_1(i, s):
                q = i * SLOTS + s
                pe.wait_ge(agg_out, done(q))
                pe.wait_ge(clipped, two_behind(q))
                pe.wait_ge(sp1.abs_ready, two_behind(q))
                pe.matmul(ps_1[s % 2][:], w[:, 0, :], agg_t[:, s], start=True, stop=True).then_inc(layer1, 1)

            def layer_2(i, s):
                q = i * SLOTS + s
                pe.wait_ge(hid_ready, done(q))
                pe.wait_ge(owned, two_behind(q))
                for u in range(U):
                    t = pe.matmul(ps_2[s % 2][:, u * P:(u + 1) * P], hid[:, s, u * P:(u + 1) * P], w[:, 1, :],
                                  start=True, stop=True)
                t.then_inc(layer2, 1)

            pipelined(pe, r.iters, [
                (2, layer_2),
                (5, layer_1),
                (6, turn),
            ])

        @block.scalar
        def _(act):
            act.wait_ge(r.weights, 16 * 4)
            act.wait_ge(one_set, 1)
            act.wait_ge(ln.eps_set, 1)
            def take_agg(i, s):
                q = i * SLOTS + s
                act.wait_ge(r.used, done(q))
                act.wait_ge(layer1, free(q))
                act.activation(agg_t[:, s], ps_t[:], ACT.Copy).then_inc(agg_out, 1)

            def log(i, s):
                sp1.magnitude(act, i, s, ps_1[s % 2][:], clipped, bias=b1[:])
                sp1.exponential(act, i, s)
                sp1.logarithm(act, i, s, hid_ready, one[:])

            def deviation(i, s):
                ln.deviation(act, i, s)

            def scale(i, s):
                ln.scale(act, i, s, z, res, r.ready, r)

            pipelined(act, r.iters, [
                (0, scale),
                (1, deviation),
                (4, log),
                (6, take_agg),
            ])

        @block.vector
        def _(dve):
            ln.setup(dve)
            dve.memset(one[:], 1.0).then_inc(one_set, 1)
            dve.wait_ge(r.weights, 16 * 4)
            def clip(i, s):
                q = i * SLOTS + s
                dve.wait_ge(hid_ready, free(q))
                dve.wait_ge(layer1, done(q))
                dve.tensor_scalar(pos[:, s], ps_1[s % 2][:], b1[:], 0.0, ALU.add, ALU.max).then_inc(clipped, 1)

            def activate(i, s):
                q = i * SLOTS + s
                dve.wait_ge(sp1.log_ready, done(q))
                dve.wait_ge(clipped, done(q))
                dve.wait_ge(layer2, free(q))
                dve.scalar_tensor_tensor(hid[:, s], sp1.lg[:, s], -LOG2, pos[:, s], ALU.add, ALU.add
                                         ).then_inc(hid_ready, 1)

            def add_own(i, s):
                q = i * SLOTS + s
                dve.wait_ge(layer2, done(q))
                r.wait_loads(dve, i, s, 0, 1)
                dve.wait_ge(r.ready, free(q))
                dve.tensor_tensor(z[:, s], ps_2[s % 2][:].rearrange("p (u c) -> p u c", u=U), own[:, s], ALU.add
                                  ).then_inc(owned, 1)

            def add_bias(i, s):
                q = i * SLOTS + s
                dve.wait_ge(owned, done(q))
                dve.tensor_tensor(z[:, s], z[:, s], bc_rows(brow[:]), ALU.add).then_inc(ln.z_ready, 1)

            def moments(i, s):
                ln.moments(dve, i, s, z, r.tick)

            def factors(i, s):
                ln.factors(dve, i, s)

            pipelined(dve, r.iters, [
                (0, factors),
                (2, add_own),
                (2, add_bias),
                (2, moments),
                (3, activate),
                (5, clip),
            ])



SCRATCH = {"sorted": (P, 3 * SORT_F), "keys": (2, SORT_N + 2), "last": (2, 2 * P), "ends": (HEADS, 2 * EDGE_TILES),
           "E": (N_HYPER, C), "X1": (NP_, C), "AA": (NP_, 2 * HEADS), "H2": (NP_, H2W),
           "X2": (NP_, C), "X3": (NP_, C), "M": (EP, C),
           "RAW129": (EP, C + 1), "RAW128": (EP, C), "RAW260": (EP, HC + HEADS)}


def build(nc, A, out, upto=None):
    T = {n: nc.dram_tensor(n, s, F32, kind="Internal").ap() for n, s in SCRATCH.items()}
    raw = T["RAW129"]
    with ExitStack() as ctx:
        S = Tables(nc, ctx, A["ident"])
        sort_phase(nc, T, A)
        index_phase(nc, T, A, S)
        if upto == "index":
            return T
        weights_phase(nc, A, S)
        hw_phase(nc, T, A, S)
        sum_pass(nc, T, S, "e1", 0, A["x"], SRC, C + 1, raw, "ones",
                 norm=lambda f: NodeNorm(f, S, [A["x"]], S.b0[:], T["X1"]))
        fix_pass(nc, S, "e1fix", 0, raw, C + 1)
        hyper_rows(nc, T, S, "e1rows", raw, T["E"], affine=False)
        sum_pass(nc, T, S, "n1", 1, T["E"], HYP, C + 1, raw, "hw")
        fix_pass(nc, S, "n1fix", 1, raw, C + 1)
        node_rows(nc, T, A, S, "n1rows", raw, 1)
        batch_norm(nc, A, S)
        if upto == "bn":
            return T
        sum_pass(nc, T, S, "e2", 0, T["X1"], SRC, C + 1, raw, "ones")
        fix_pass(nc, S, "e2fix", 0, raw, C + 1)
        hyper_rows(nc, T, S, "e2rows", raw, T["E"], affine=True)
        sum_pass(nc, T, S, "n2", 1, T["E"], HYP, C + 1, raw, "hw")
        fix_pass(nc, S, "n2fix", 1, raw, C + 1)
        node_rows(nc, T, A, S, "n2rows", raw, 2)
        if upto == "x1":
            return T
        gat_rows(nc, T, S, "gat1dense", dense=True)
        attention_phase(nc, T, S, "att1", HEADS, T["AA"], 1, 0)
        gat_sum(nc, T, S, "gat1sum", 1)
        fix_pass(nc, S, "gat1fix", 0, T["RAW260"], HC + HEADS)
        gat_rows(nc, T, S, "gat1rows", dense=False)
        if upto == "h2":
            return T
        attention_phase(nc, T, S, "att2", 1, T["H2"].rearrange("n (k c) -> (n k) c", c=4), H2W // 4, C // 4,
                        norm=lambda f: NodeNorm(f, S, [T["X1"], T["H2"]], S.b2[:], T["X2"]))
        gat_sum(nc, T, S, "gat2sum", 2)
        fix_pass(nc, S, "gat2fix", 0, raw, C + 1)
        gat_nodes(nc, T, S)
        if upto == "x2":
            return T
        gin_rows(nc, T, A, S, "gindense", dense=True,
                 beside=lambda f: SegmentSum(f, T, S, 0, T["X2"], SRC, C + 1, raw, "ones"))
        fix_pass(nc, S, "ginfix", 0, raw, C + 1)
        gin_rows(nc, T, A, S, "ginrows", dense=False)
        if upto == "x3":
            return T
        messages(nc, T, A, S)
        sum_pass(nc, T, S, "sch", 0, T["M"], PERM, C, T["RAW128"],
                 norm=lambda f: NodeNorm(f, S, [T["X3"]], S.c3[:], out))
        fix_pass(nc, S, "schfix", 0, T["RAW128"], C)
        schnet_rows(nc, T, A, S, out)
    return T


def lay_out(inputs):
    import numpy as np

    a = {k: np.asarray(v) for k, v in inputs.items()}

    def padded(x, rows, fill=0):
        out = np.full((rows, *x.shape[1:]), fill, x.dtype)
        out[:len(x)] = x
        return out

    def rows(x):
        return np.ascontiguousarray(np.broadcast_to(x.reshape(1, -1), (P, x.size)))

    def turned(x):
        return np.ascontiguousarray(x.T)

    src, dst = a["src"].astype(np.int32), a["dst"].astype(np.int32)
    src_p, dst_p = padded(src, SORT_N, N_NODES), padded(dst, SORT_N, N_NODES)
    out = dict(constants())
    out.update(
        x=padded(a["x"], NP_), edge_attr=padded(a["edge_attr_128"], EP),
        src=src_p.reshape(P, SORT_F), dst=dst_p.reshape(P, SORT_F),
        src_cols=turned(src_p[:EP].reshape(EDGE_TILES, P)),
        hw=np.ascontiguousarray(a["L0_gnn_hyperedge_weight"].reshape(-1, 1)),
        L0_W1T=turned(a["L0_gnn_W1"]), L0_W2T=turned(a["L0_gnn_W2"]),
        L0_b1_rows=rows(a["L0_gnn_b1"]), L0_gamma_rows=rows(a["L0_gnn_gamma"]),
        L0_beta_rows=rows(a["L0_gnn_beta"]), L0_b2_rows=rows(a["L0_gnn_b2"]),
        L1_W1=a["L1_gnn_W1"], L1_W2=np.ascontiguousarray(a["L1_gnn_W2"].reshape(2, P, C).transpose(1, 0, 2)),
        L1_b1_cols=turned(a["L1_gnn_b1"].reshape(2, P)),
        L1_as1=rows(a["L1_gnn_att_src1"]), L1_ad1=rows(a["L1_gnn_att_dst1"]),
        L1_as2=rows(a["L1_gnn_att_src2"]), L1_ad2=rows(a["L1_gnn_att_dst2"]), L1_b2_rows=rows(a["L1_gnn_b2"]),
        L2_Wpre=a["L2_gnn_W_pre"], L2_W1=a["L2_gnn_W1"], L2_W2=a["L2_gnn_W2"],
        L2_b1_col=np.ascontiguousarray(a["L2_gnn_b1"].reshape(-1, 1)),
        L2_b2_rows=rows(a["L2_gnn_b2"]), L2_bpre_rows=rows(a["L2_gnn_b_pre"]),
        L2_gamma_rows=rows(a["L2_gnn_gamma"]), L2_beta_rows=rows(a["L2_gnn_beta"]),
        L3_WnT=turned(a["L3_gnn_W_node"]), L3_bn_rows=rows(a["L3_gnn_b_node"]),
        L3_We1T=turned(a["L3_gnn_W_e1"]), L3_be1_col=np.ascontiguousarray(a["L3_gnn_b_e1"].reshape(-1, 1)),
        L3_We2T=turned(a["L3_gnn_W_e2"]), L3_be2_rows=rows(a["L3_gnn_b_e2"]),
        L3_Wfc1T=turned(a["L3_gnn_W_fc1"]), L3_bfc1_col=np.ascontiguousarray(a["L3_gnn_b_fc1"].reshape(-1, 1)),
        L3_Wfc2T=turned(a["L3_gnn_W_fc2"]), L3_bfc2_rows=rows(a["L3_gnn_b_fc2"]),
    )
    return out


def kernel(**inputs):
    import numpy as np
    import concourse.bacc as bacc
    from concourse.bass_utils import run_bass_kernel_spmd

    nc = bacc.Bacc("TRN2", target_bir_lowering=False, num_devices=1)
    arrays = {f"in_{n}": x for n, x in lay_out(inputs).items()}
    A = {n[3:]: nc.dram_tensor(n, x.shape, mybir.dt.from_np(x.dtype), kind="ExternalInput").ap()
         for n, x in arrays.items()}
    out = nc.dram_tensor("out", (NP_, C), F32, kind="ExternalOutput").ap()
    build(nc, A, out)
    ran = run_bass_kernel_spmd(nc, [arrays], core_ids=[0])
    return np.asarray(ran.results[0]["out"])[:N_NODES]
```

```python
from contextlib import ExitStack

import concourse.bass as bass
from concourse import mybir

F32 = mybir.dt.float32
I32 = mybir.dt.int32
ALU = mybir.AluOpType
ACT = mybir.ActivationFunctionType
AX_X = mybir.AxisListType.X

P = 128
N_NODES = 50000
N_HYPER = 10000
C = 128
HEADS = 4
HID = 64
HC = HEADS * HID
TILES_PER_GROUP = U = 4
SLOTS = 4
NP_ = 53248
NODE_GROUPS = NP_ // (P * U)
EDGE_TILES = 208
EDGE_GROUPS = EDGE_TILES // U
EP = EDGE_TILES * P
SORT_F = 256
SORT_N = P * SORT_F
HALF_T = EDGE_TILES // 2
H2W = 132
SKIP = 1000000.0
NEG = -1.0e30
SLOPE = 0.2
EPS = 1e-5
LOG2 = 0.6931471805599453
SPLIT = 17664
ENC_NEG = float(0x8000 + SPLIT)
ENC_ADD = float(0x80 - SPLIT)


def done(q):
    return q + 1 + SLOTS


def behind(q):
    return q + SLOTS


def two_behind(q):
    return q + SLOTS - 1


def free(q):
    return q + 1


class Phase:

    def __init__(self, nc, name):
        self.nc, self.name, self.ctx, self.own_sems = nc, name, ExitStack(), []

    def __enter__(self):
        self.ctx.__enter__()
        return self

    def __exit__(self, *a):
        self.ctx.__exit__(*a)
        self.nc.clear_and_free_semaphores(self.own_sems)
        self.nc.all_engine_barrier()

    def sb(self, name, shape, dt=F32):
        return self.ctx.enter_context(self.nc.sbuf_tensor(f"{self.name}_{name}", shape, dt))

    def ps(self, name, shape):
        return self.ctx.enter_context(self.nc.psum_tensor(f"{self.name}_{name}", shape, F32))

    def sem(self, name):
        self.own_sems.append(self.nc.alloc_semaphore(f"{self.name}_{name}"))
        return self.own_sems[-1]

    def sems(self, name, n=SLOTS):
        return [self.sem(f"{name}{i}") for i in range(n)]

    def block(self):
        return self.ctx.enter_context(self.nc.Block())


def groups_of(table, g0=0):
    return table.rearrange("(g u p) w -> g p u w", u=U, p=P)


def prime_stores(f, stored, n, ident, name="spare"):
    spare = f.sb(name, [1, SLOTS, 16])

    def issue(eng):
        for s in range(SLOTS):
            eng.dma_start(spare[:, s, :], ident[0:1, 0:16]).then_inc(stored[s], 16 * n)
    return issue


def gather(pool, out, table, index):
    return pool.indirect_dma_start(out, None, table, bass.IndirectOffsetOnAxis(ap=index, axis=0))


def scatter(pool, table, index, rows, values):
    return pool.indirect_dma_start(table, bass.IndirectOffsetOnAxis(ap=index, axis=0), values, None,
                                   bounds_check=rows - 1, oob_is_err=False)


def sort_phase(nc, T, A):
    with Phase(nc, "sort") as f:
        raw = f.sb("raw", [P, 3, SORT_F], I32)
        keyf = f.sb("keyf", [P, 2, SORT_F])
        offs = f.sb("offs", [P, 2, SORT_F])
        top = f.sb("top", [P, 2, SORT_F], I32)
        words = f.sb("words", [P, 2, 3 * SORT_F])
        signs = f.sb("signs", [P, 8, SORT_F])
        signs_t = f.sb("signs_t", [P, 7, P])
        ident = f.sb("ident", [P, P])
        turned = f.ps("turned", [P, 2, 512])
        loaded, stage, turn, out = f.sem("loaded"), f.sem("stage"), f.sem("turn"), f.sem("out")
        block = f.block()
        turns = []

        @block.sync
        def _(sp):
            sp.dma_start(raw[:, 0, :], A["dst"]).then_inc(loaded, 16)
            sp.dma_start(raw[:, 1, :], A["src"]).then_inc(loaded, 16)
            sp.dma_start(raw[:, 2, :], A["edge_no"]).then_inc(loaded, 16)
            sp.dma_start(signs[:], A["sort_signs"]).then_inc(loaded, 16)
            sp.dma_start(signs_t[:], A["sort_signs_t"]).then_inc(loaded, 16)
            sp.dma_start(ident[:], A["ident"]).then_inc(loaded, 16)

        @block.vector
        def _(dve):
            n = 0

            def step(*ins):
                nonlocal n
                for x in ins:
                    x.then_inc(stage, 1)
                n += len(ins)
                dve.wait_ge(stage, n)

            dve.wait_ge(loaded, 96)
            step(dve.tensor_copy(keyf[:], raw[:, 0:2, :]))
            step(dve.tensor_scalar(offs[:], keyf[:], float(SPLIT), ENC_NEG, ALU.is_lt, ALU.mult))
            step(dve.scalar_tensor_tensor(top[:], keyf[:], ENC_ADD, offs[:], ALU.add, ALU.add))
            w0 = words[:, 0, :].bitcast(I32).rearrange("p (a f) -> p a f", a=3)
            step(*[dve.scalar_tensor_tensor(w0[:, a, :], top[:, k, :], 16, raw[:, pay, :],
                                            ALU.logical_shift_left, ALU.bitwise_or)
                   for a, k, pay in ((0, 0, 2), (1, 0, 1), (2, 1, 0))])
            cur = 0

            def compare(d):
                nonlocal cur
                a = words[:, cur, :].rearrange("p (g t d) -> p g t d", t=2, d=d)
                b = words[:, 1 - cur, :].rearrange("p (g t d) -> p g t d", t=2, d=d)
                step(dve.tensor_tensor(b[:, :, 0, :], a[:, :, 0, :], a[:, :, 1, :], ALU.min),
                     dve.tensor_tensor(b[:, :, 1, :], a[:, :, 0, :], a[:, :, 1, :], ALU.max))
                cur = 1 - cur

            turn_no = 0

            def turn_over(mask):
                nonlocal turn_no, cur
                turns.append((cur, n))
                turn_no += 1
                dve.wait_ge(turn, turn_no)
                new = words[:, 1 - cur, :]
                if mask is None:
                    step(dve.tensor_copy(new[:, 0:512], turned[:, 0, :]),
                         dve.tensor_copy(new[:, 512:768], turned[:, 1, 0:256]))
                else:
                    m = mask.unsqueeze(1)
                    step(dve.tensor_tensor(new[:, 0:512].rearrange("p (a q) -> p a q", q=P),
                                           turned[:, 0, :].rearrange("p (a q) -> p a q", q=P),
                                           m.to_broadcast([P, 4, P]), ALU.mult),
                         dve.tensor_tensor(new[:, 512:768].rearrange("p (a q) -> p a q", q=P),
                                           turned[:, 1, 0:256].rearrange("p (a q) -> p a q", q=P),
                                           m.to_broadcast([P, 2, P]), ALU.mult))
                cur = 1 - cur

            for level in range(1, 9):
                a = words[:, cur, :].rearrange("p (a f) -> p a f", a=3)
                b = words[:, 1 - cur, :].rearrange("p (a f) -> p a f", a=3)
                step(dve.tensor_tensor(b, a, signs[:, level - 1, :].unsqueeze(1).to_broadcast([P, 3, SORT_F]),
                                       ALU.mult))
                cur = 1 - cur
                for m in reversed(range(level)):
                    compare(1 << m)
            for level in range(9, 16):
                turn_over(signs_t[:, level - 9, :])
                for m in reversed(range(level - 8)):
                    compare(1 << m)
                turn_over(None)
                for m in reversed(range(8)):
                    compare(1 << m)
            f.final, f.final_n = cur, n

        @block.tensor
        def _(pe):
            for buf, n in turns:
                pe.wait_ge(stage, n)
                for b in range(6):
                    t = pe.transpose(turned[:, b // 4, (b % 4) * P:(b % 4 + 1) * P],
                                     words[:, buf, b * P:(b + 1) * P], ident[:])
                t.then_inc(turn, 1)

        @block.scalar
        def _(act):
            act.wait_ge(stage, f.final_n)
            act.dma_start(T["sorted"], words[:, f.final, :]).then_inc(out, 16)
            act.wait_ge(out, 16)


def constants():
    import numpy as np
    j = np.arange(SORT_N).reshape(P, SORT_F)

    def sgn(k):
        return np.where((j >> k) & 1, -1.0, 1.0) if k else np.ones(j.shape)

    full = [sgn(k) * sgn(k - 1) if k > 1 else sgn(1) for k in range(1, 16)]
    signs = np.stack(full[:8], 1).astype(np.float32)
    signs_t = np.broadcast_to(np.stack([m[:, 0] for m in full[8:]])[None], (P, 7, P)).astype(np.float32)
    return {
        "edge_no": j.astype(np.int32),
        "sort_signs": signs,
        "sort_signs_t": np.ascontiguousarray(signs_t),
        "ident": np.eye(P, dtype=np.float32),
        "is_last": (j % P == P - 1).astype(np.float32),
        "later": (np.arange(EDGE_TILES).reshape(2, HALF_T).T[:, :, None] > np.arange(EDGE_TILES)
                  ).astype(np.float32),
    }



KD, SF, KS, SM = range(4)
SRC, SCD, SCE, PERM, DST, HYP, SCS, NOD, SRCO = range(9)


class Tables:

    def __init__(self, nc, ctx, ident_dram):
        self.ident_dram = ident_dram

        def sb(name, shape, dt=F32):
            return ctx.enter_context(nc.sbuf_tensor(name, shape, dt))

        self.colf = sb("colf", [P, 4, EDGE_TILES])
        self.coli = sb("coli", [P, 9, EDGE_TILES], I32)
        self.joins = sb("joins", [HALF_T, 2, 2, EDGE_TILES])
        self.ident = sb("identity", [P, P])
        self.ws = sb("w_src", [P, EDGE_TILES, HEADS])
        self.wd = sb("w_self", [P, EDGE_TILES, HEADS])
        self.wt = sb("w_total", [P, EDGE_TILES, HEADS])
        self.affine = sb("affine", [P, 2, C])
        self.affine_sums = sb("affine_sums", [P, 2, U * C])
        self.W1 = sb("W1", [P, HC])
        self.WA = sb("WA", [P, 2 * HEADS])
        self.W2x = sb("W2x", [P, 2, H2W])
        self.b1col = sb("b1col", [P, 2])
        self.b0 = sb("b0", [P, C])
        self.b2 = sb("b2", [P, C])
        self.c2 = sb("c2", [P, C])
        self.c3 = sb("c3", [P, C])


def index_phase(nc, T, A, S):
    with Phase(nc, "index") as f:
        words = f.sb("words", [P, 3, SORT_F], I32)
        bits = f.sb("bits", [P, 3, 2, SORT_F], I32)
        key = f.sb("key", [P, 3, SORT_F])
        off = f.sb("off", [P, 3, SORT_F])
        prv = f.sb("prv", [P, 2, SORT_F])
        nxt = f.sb("nxt", [P, 2, SORT_F])
        new = f.sb("new", [P, 2, SORT_F])
        rep = f.sb("rep", [P, 2, SORT_F])
        tmp = f.sb("tmp", [P, 2, SORT_F])
        is_last = f.sb("is_last", [P, SORT_F])
        arr = f.sb("arr", [P, 12, SORT_F])
        guard = f.sb("guard", [1, 2])
        zeros = f.sb("zeros", [80, 2000])
        later = f.sb("later", [HALF_T, 2, EDGE_TILES])
        last_row = f.sb("last_row", [HALF_T, 2, EDGE_TILES])
        first_col = f.sb("first_col", [HALF_T, 2, 2])
        eq = f.sb("eq", [HALF_T, 2, 2, EDGE_TILES])
        psT = f.ps("turned", [P, 4, 512])
        filled, loaded, stage, kept, back, tile_keys, turned = (f.sem(n) for n in (
            "filled", "loaded", "stage", "kept", "back", "tile_keys", "turned"))
        block = f.block()
        marks = {}

        @block.vector
        def _(dve):
            n = 0

            def step(*ins):
                nonlocal n
                for x in ins:
                    x.then_inc(stage, 1)
                n += len(ins)
                dve.wait_ge(stage, n)

            step(dve.memset(guard[:], -1.0), dve.memset(zeros[:], 0.0))
            marks["guard"] = n
            dve.wait_ge(loaded, 16 * 5)
            step(dve.tensor_scalar(bits[:, :, 0, :], words[:], 16, None, ALU.logical_shift_right),
                 dve.tensor_scalar(bits[:, :, 1, :], words[:], 0xFFFF, None, ALU.bitwise_and))
            step(dve.tensor_scalar(off[:], bits[:, :, 0, :], 32768.0, ENC_NEG, ALU.is_ge, ALU.mult))
            step(dve.scalar_tensor_tensor(key[:], bits[:, :, 0, :], -ENC_ADD, off[:], ALU.add, ALU.subtract))
            marks["key"] = n
            dve.wait_ge(back, 16 * 4)
            kk = key[:, 1:3, :]
            step(dve.tensor_tensor(new[:], kk, prv[:], ALU.not_equal),
                 dve.tensor_tensor(rep[:], kk, nxt[:], ALU.not_equal))
            step(dve.tensor_tensor(rep[:], rep[:], is_last[:].unsqueeze(1).to_broadcast([P, 2, SORT_F]), ALU.max))
            def tiles(x, o):
                return x[:, o, :].rearrange("p (h e) -> p h e", h=2)
            step(*[dve.tensor_tensor(tiles(tmp, o), tiles(key, o + 1),
                                     tiles(prv, o)[:, :, 0:1].to_broadcast([P, 2, P]), ALU.not_equal)
                   for o in range(2)])
            step(dve.tensor_tensor(rep[:], rep[:], tmp[:], ALU.mult))
            step(dve.tensor_copy(arr[:, 0, :], key[:, 1, :]),
                 dve.tensor_copy(arr[:, 1, :], new[:, 0, :]),
                 dve.tensor_copy(arr[:, 2, :], key[:, 2, :]),
                 dve.scalar_tensor_tensor(arr[:, 3, :], key[:, 2, :], float(N_NODES), rep[:, 1, :],
                                          ALU.is_lt, ALU.mult),
                 dve.tensor_copy(arr[:, 4, :], bits[:, 1, 1, :]),
                 dve.scalar_tensor_tensor(arr[:, 5, :], key[:, 1, :], -SKIP, rep[:, 0, :], ALU.add, ALU.mult),
                 dve.scalar_tensor_tensor(tmp[:, 0, :], key[:, 1, :], float(N_HYPER), rep[:, 0, :],
                                          ALU.is_lt, ALU.mult),
                 dve.tensor_copy(arr[:, 7, :], bits[:, 0, 1, :]),
                 dve.tensor_copy(arr[:, 8, :], key[:, 1, :]),
                 dve.tensor_scalar(arr[:, 9, :], bits[:, 2, 1, :], float(N_HYPER - 1), None, ALU.min),
                 dve.scalar_tensor_tensor(arr[:, 10, :], key[:, 2, :], -SKIP, rep[:, 1, :], ALU.add, ALU.mult),
                 dve.tensor_copy(arr[:, 11, :], key[:, 2, :]))
            step(dve.scalar_tensor_tensor(arr[:, 6, :], key[:, 1, :], -SKIP, tmp[:, 0, :], ALU.add, ALU.mult))
            step(*[dve.tensor_scalar(arr[:, a, :], arr[:, a, :], SKIP, None, ALU.add) for a in (5, 6, 10)])
            marks["arr"] = n
            dve.wait_ge(tile_keys, 16 * 4)
            for o in range(2):
                step(*[dve.tensor_scalar(eq[:, o, c, :], last_row[:, o, :], first_col[:, o, c:c + 1], None,
                                         ALU.is_equal) for c in range(2)])
            step(*[dve.tensor_tensor(S.joins[:, o, :, :], eq[:, o, :, :], later[:], ALU.mult)
                   for o in range(2)])
            for a in range(12):
                dve.wait_ge(turned, a + 1)
                col = S.colf[:, a, :] if a < 4 else S.coli[:, a - 4, :]
                dve.tensor_copy(col.rearrange("e (p h) -> e h p", h=2),
                                psT[:, a % 4, 0:2 * P].rearrange("e (h p) -> e h p", h=2)[:, :, 0:HALF_T]
                                ).then_inc(stage, 1)
            marks["columns"] = n

        @block.tensor
        def _(pe):
            pe.wait_ge(stage, marks["arr"])
            for a in range(12):
                if a >= 4:
                    pe.wait_ge(stage, marks["columns"] + a - 3)
                for h in range(2):
                    t = pe.transpose(psT[:, a % 4, h * P:(h + 1) * P], arr[:, a, h * P:(h + 1) * P], S.ident[:])
                t.then_inc(turned, 1)

        @block.sync
        def _(sp):
            sp.dma_start(words[:], T["sorted"].bitcast(I32).rearrange("p (a f) -> p a f", a=3)).then_inc(loaded, 16)
            sp.dma_start(is_last[:], A["is_last"]).then_inc(loaded, 16)
            sp.dma_start(later[:], A["later"]).then_inc(loaded, 16)
            sp.dma_start(S.coli[:, SRCO, :], A["src_cols"]).then_inc(loaded, 16)
            sp.dma_start(S.ident[:], A["ident"]).then_inc(loaded, 16)
            sp.wait_ge(stage, marks["guard"])
            e_rows = T["E"].rearrange("(p r) c -> p (r c)", p=80)
            fills = N_HYPER * C // (80 * 2000)
            for k in range(fills):
                sp.dma_start(e_rows[:, k * 2000:(k + 1) * 2000], zeros[:]).then_inc(filled, 16)
            for o in range(2):
                sp.dma_start(T["keys"][o:o + 1, 0:1], guard[:, 0:1]).then_inc(kept, 16)
                sp.dma_start(T["keys"][o:o + 1, SORT_N + 1:SORT_N + 2], guard[:, 1:2]).then_inc(kept, 16)
            sp.wait_ge(stage, marks["key"])
            for o in range(2):
                sp.dma_start(T["keys"][o, 1:SORT_N + 1].rearrange("(p f) -> p f", p=P),
                             key[:, o + 1, :]).then_inc(kept, 16)
                with nc.allow_non_contiguous_dma(reason="two keys per partition"):
                    for h in range(2):
                        sp.dma_start(T["last"][o].rearrange("(p h) -> p h", h=2)[:, h:h + 1],
                                     key[:, o + 1, h * P + P - 1:h * P + P]).then_inc(kept, 16)
            sp.wait_ge(kept, 16 * 10)
            with nc.allow_non_contiguous_dma(reason="a column of the table"):
                sp.dma_start(T["EW"][:, C:C + 1], A["hw"]).then_inc(filled, 16)
            sp.wait_ge(filled, (fills + 1) * 16)
            for o in range(2):
                sp.dma_start(prv[:, o, :], T["keys"][o, 0:SORT_N].rearrange("(p f) -> p f", p=P)
                             ).then_inc(back, 16)
                sp.dma_start(nxt[:, o, :], T["keys"][o, 2:SORT_N + 2].rearrange("(p f) -> p f", p=P)
                             ).then_inc(back, 16)
            for o in range(2):
                sp.dma_start(last_row[:, o, :], T["last"][o:o + 1, 0:EDGE_TILES].to_broadcast([HALF_T, EDGE_TILES])
                             ).then_inc(tile_keys, 16)
                with nc.allow_non_contiguous_dma(reason="first key of each tile"):
                    sp.dma_start(first_col[:, o, :],
                                 T["keys"][o, 1:1 + EDGE_TILES * P].rearrange("(c p e) -> p c e", p=HALF_T, e=P)
                                 [:, :, 0]).then_inc(tile_keys, 16)



class SegmentSum:

    def __init__(self, f, T, S, order, table, idx, w, out, extra=None):
        self.T, self.S, self.order, self.table, self.idx, self.w, self.extra = T, S, order, table, idx, w, extra
        self.wt = table.shape[1]
        self.iters = EDGE_GROUPS // SLOTS
        self.out_g = groups_of(out)
        self.slot = f.sb("sum_slot", [P, SLOTS, U], I32)
        self.v = f.sb("sum_v", [P, SLOTS, U, w])
        self.krow = f.sb("sum_krow", [P, SLOTS, U * P])
        self.same = f.sb("sum_same", [P, SLOTS, U, P])
        self.sums = f.sb("sum_sums", [P, SLOTS, U, w])
        self.acc = [f.ps(f"sum_acc{s}", [P, U, 256]) for s in range(2)]
        self.picked, self.tick, self.ones_set = f.sem("sum_picked"), f.sem("sum_tick"), f.sem("sum_ones_set")
        self.matched, self.summed, self.copied = f.sem("sum_matched"), f.sem("sum_summed"), f.sem("sum_copied")
        self.gathered, self.keyed, self.stored = (f.sems("sum_gathered"), f.sems("sum_keyed"),
                                                  f.sems("sum_stored"))
        self.prime_stores = prime_stores(f, self.stored, 1, S.ident_dram, "sum_spare")

    def sync_start(self, sp):
        for m in (self.matched, self.summed, self.copied):
            sp.sem_inc(m, SLOTS)

    def sync_steps(self, sp):
        def key_rows(i, s):
            q = i * SLOTS + s
            sp.wait_ge(self.matched, free(q))
            sp.dma_start(self.krow[:, s], self.T["keys"][self.order:self.order + 1, bass.ds(q * (U * P) + 1, U * P)]
                         .to_broadcast([P, U * P])).then_inc(self.keyed[s], 16)
        return [(4, key_rows)]

    def sync_end(self, sp):
        for s in range(SLOTS):
            sp.wait_ge(self.stored[s], 16 * (self.iters + 1))

    def pool_loop(self, pool):
        with pool.Fori(0, self.iters) as i:
            for s in range(SLOTS):
                q = i * SLOTS + s
                pool.wait_ge(self.summed, free(q))
                pool.tensor_copy(self.slot[:, s], self.S.coli[:, self.idx, bass.ds(q * U, U)]
                                 ).then_inc(self.picked, 1)
                pool.wait_ge(self.picked, q + 1)
                pool.sem_inc(self.tick, 1)
                for u in range(U):
                    gather(pool, self.v[:, s, u, 0:self.wt], self.table, self.slot[:, s, u:u + 1]
                           ).then_inc(self.gathered[s], 16)

    def vector_start(self, dve):
        if self.extra == "ones":
            dve.memset(self.v[:, :, :, self.wt:self.wt + 1], 1.0).then_inc(self.ones_set, 1)

    def vector_steps(self, dve):
        key = (KD, KS)[self.order]

        def match(i, s):
            q = i * SLOTS + s
            dve.wait_ge(self.keyed[s], (i + 1) * 16)
            dve.wait_ge(self.summed, free(q))
            dve.tensor_tensor(self.same[:, s], self.krow[:, s].rearrange("p (u e) -> p u e", u=U),
                              self.S.colf[:, key, bass.ds(q * U, U)].unsqueeze(2).to_broadcast([P, U, P]),
                              ALU.is_equal).then_inc(self.matched, 1)
        return [(1, match)]

    def tensor_start(self, pe):
        if self.extra == "ones":
            pe.wait_ge(self.ones_set, 1)

    def tensor_steps(self, pe):
        def add_up(i, s):
            q = i * SLOTS + s
            pe.wait_ge(self.matched, done(q))
            pe.wait_ge(self.gathered[s], (i + 1) * (16 * U))
            pe.wait_ge(self.copied, two_behind(q))
            for u in range(U):
                m = pe.matmul(self.acc[s % 2][:, u, 0:self.w], self.same[:, s, u, :], self.v[:, s, u, :],
                              start=True, stop=True)
            m.then_inc(self.summed, 1)
        return [(0, add_up)]

    def scalar_steps(self, act):
        def take_sums(i, s):
            q = i * SLOTS + s
            act.wait_ge(self.summed, done(q))
            act.wait_ge(self.stored[s], (i + 1) * 16)
            act.activation(self.sums[:, s], self.acc[s % 2][:, :, 0:self.w], ACT.Copy).then_inc(self.copied, 1)
            act.wait_ge(self.copied, done(q))
            act.dma_start(self.out_g[q], self.sums[:, s]).then_inc(self.stored[s], 16)
        return [(0, take_sums)]


def steps_of(work, engine, eng):
    return {"sync": work.sync_steps, "vector": work.vector_steps, "tensor": work.tensor_steps,
            "scalar": work.scalar_steps}[engine](eng)


def sum_pass(nc, T, S, name, *of, norm=None):
    with Phase(nc, name) as f:
        sums = SegmentSum(f, T, S, *of)
        norm = norm(f) if norm else None
        block = f.block()

        def run(eng, steps, beside):
            if norm and not norm.twice:
                pipelined(eng, sums.iters, steps + beside)
            else:
                pipelined(eng, sums.iters, steps, beside)

        @block.sync
        def _(sp):
            sums.sync_start(sp)
            if norm:
                norm.sync_start(sp)
            run(sp, sums.sync_steps(sp), norm.sync_steps(sp) if norm else [])
            sums.sync_end(sp)
            if norm:
                norm.r.finish(sp)

        @block.gpsimd
        def _(pool):
            sums.pool_loop(pool)

        @block.vector
        def _(dve):
            sums.vector_start(dve)
            if norm:
                norm.ln.setup(dve)
            run(dve, sums.vector_steps(dve), norm.vector_steps(dve) if norm else [])

        @block.tensor
        def _(pe):
            sums.tensor_start(pe)
            pipelined(pe, sums.iters, sums.tensor_steps(pe))

        @block.scalar
        def _(act):
            sums.prime_stores(act)
            if norm:
                norm.scalar_start(act)
            run(act, sums.scalar_steps(act), norm.scalar_steps(act) if norm else [])


def fix_pass(nc, S, name, order, out, w):
    with Phase(nc, name) as f:
        first = f.sb("first", [HALF_T, 2, w])
        last = f.sb("last", [HALF_T, 2, w])
        full = f.sb("full", [HALF_T, 2, w])
        acc = f.ps("acc", [P, 2, 512])
        loaded, carried, added, stored = (f.sem(n) for n in ("loaded", "carried", "added", "stored"))
        block = f.block()
        rows = out.rearrange("(c p e) w -> p c e w", p=HALF_T, e=P)

        @block.sync
        def _(sp):
            sp.dma_start(first[:], rows[:, :, 0, :]).then_inc(loaded, 16)
            sp.dma_start(last[:], rows[:, :, P - 1, :]).then_inc(loaded, 16)
            sp.wait_ge(added, 1)
            sp.dma_start(rows[:, :, P - 1, :], full[:]).then_inc(stored, 16)
            sp.wait_ge(stored, 16)

        @block.tensor
        def _(pe):
            pe.wait_ge(loaded, 32)
            for c in range(2):
                for later in range(2):
                    m = pe.matmul(acc[0:HALF_T, c, 0:w], S.joins[:, order, later, c * HALF_T:(c + 1) * HALF_T],
                                  first[:, later, :], start=(later == 0), stop=(later == 1))
            m.then_inc(carried, 1)

        @block.vector
        def _(dve):
            dve.wait_ge(carried, 1)
            dve.tensor_tensor(full[:], last[:], acc[0:HALF_T, :, 0:w], ALU.add).then_inc(added, 1)



def bc_rows(row, n=U):
    return row.unsqueeze(1).to_broadcast([P, n, C])


def pipelined(eng, iters, steps, twice=()):
    lead = max([n for n, _ in steps] + [-(-n // 2) for n, _ in twice])
    last = iters * SLOTS

    def at(q):
        for n, step in steps:
            if 0 <= q + n < last:
                step((q + n) // SLOTS, (q + n) % SLOTS)
        for k in range(2):
            for n, step in twice:
                g = 2 * q + k + n
                if 0 <= g < 2 * last:
                    step(g // SLOTS, g % SLOTS)

    for q in range(-lead, 0):
        at(q)
    whole = iters - -(-lead // SLOTS)
    with eng.Fori(0, whole) as i:
        for s in range(SLOTS):
            for n, step in steps:
                step(i + (s + n) // SLOTS, (s + n) % SLOTS)
            for k in range(2):
                for n, step in twice:
                    g = 2 * s + k + n
                    step(i * 2 + g // SLOTS, g % SLOTS)
    for q in range(whole * SLOTS, last):
        at(q)


def in_pairs(*steps):
    def run(i, s):
        if s % 2:
            for step in steps:
                step(i, s - 1)
                step(i, s)
    return run


class Rows:

    def __init__(self, f, S, dense, stores, groups=None, name="", own_parts=U, copy=None):
        self.f, self.S, self.dense = f, S, dense
        self.iters = (groups or (NODE_GROUPS if dense else EDGE_GROUPS)) // SLOTS
        self.loaded = f.sems(f"{name}loaded")
        self.gathered = f.sems(f"{name}gathered")
        self.stored = f.sems(f"{name}stored")
        self.used = f.sem(f"{name}used")
        self.ready = f.sem(f"{name}ready")
        self.picked, self.picked_out, self.tick = (f.sem(f"{name}{n}") for n in ("picked", "picked_out", "tick"))
        self.weights = f.sem(f"{name}weights")
        self.stores = stores
        self.own_parts = own_parts
        self.copy = copy
        if copy is not None:
            self.kept = f.sems(f"{name}kept")
            self.prime_kept = prime_stores(f, self.kept, 1, S.ident_dram, f"{name}spare_kept")
        self.prime_stores = prime_stores(f, self.stored, stores, S.ident_dram, f"{name}spare")
        self.slot = f.sb(f"{name}slot", [P, SLOTS, U], I32)
        self.slot_out = f.sb(f"{name}slot_out", [P, SLOTS, U], I32)

    def prime(self, sp, sems):
        for m in (self.used, self.ready, *sems):
            sp.sem_inc(m, SLOTS)

    def load(self, sp, pairs):
        load = self.load_step(sp, pairs)
        with sp.Fori(0, self.iters) as i:
            for s in range(SLOTS):
                load(i, s)

    def load_step(self, sp, pairs):
        def load(i, s):
            q = i * SLOTS + s
            sp.wait_ge(self.used, free(q))
            for buf, table in pairs:
                sp.dma_start(buf[:, s], table[q]).then_inc(self.loaded[s], 16)
        return load

    def own_step(self, sp, buf, table, buf_used):
        rows = groups_of(table)

        def load_own(i, s):
            q = i * SLOTS + s
            sp.wait_ge(buf_used, free(q))
            sp.dma_start(buf[:, s], rows[q]).then_inc(self.gathered[s], 16)
        return load_own

    def finish(self, sp):
        for s in range(SLOTS):
            sp.wait_ge(self.stored[s], 16 * self.stores * (self.iters + 1))
            if self.copy is not None:
                sp.wait_ge(self.kept[s], 16 * (self.iters + 1))

    def gather_group(self, pool, q, s, buf, table, idx, buf_used):
        pool.wait_ge(buf_used, free(q))
        pool.tensor_copy(self.slot[:, s], self.S.coli[:, idx, bass.ds(q * U, U)]).then_inc(self.picked, 1)
        pool.wait_ge(self.picked, q + 1)
        pool.sem_inc(self.tick, 1)
        for u in range(U):
            gather(pool, buf[:, s, u, :], table, self.slot[:, s, u:u + 1]).then_inc(self.gathered[s], 16)

    def scatter_group(self, pool, i, s, buf, table, idx, rows):
        q = i * SLOTS + s
        pool.wait_ge(self.stored[s], (i + 1) * (16 * U))
        pool.tensor_copy(self.slot_out[:, s], self.S.coli[:, idx, bass.ds(q * U, U)]).then_inc(self.picked_out, 1)
        pool.wait_ge(self.picked_out, q + 1)
        pool.sem_inc(self.tick, 1)
        pool.wait_ge(self.ready, done(q))
        pool.sem_inc(self.tick, 1)
        for u in range(U):
            scatter(pool, table, self.slot_out[:, s, u:u + 1], rows, buf[:, s, u, :]).then_inc(self.stored[s], 16)

    def pool_loop(self, pool, gathers=None, scatters=None, ahead=0):
        pipelined(pool, self.iters, [
            *([(0, lambda i, s: self.scatter_group(pool, i, s, *scatters))] if scatters else []),
            *([(ahead, lambda i, s: self.gather_group(pool, i * SLOTS + s, s, *gathers))] if gathers else []),
        ])

    def store(self, eng, i, s, *pairs):
        q = i * SLOTS + s
        eng.wait_ge(self.ready, done(q))
        for buf, table in pairs:
            eng.dma_start(table[q], buf[:, s]).then_inc(self.stored[s], 16)

    def wait_loads(self, eng, i, s, plain, gathers=0):
        if plain:
            eng.wait_ge(self.loaded[s], (i + 1) * (16 * plain))
        if gathers:
            eng.wait_ge(self.gathered[s], (i + 1) * (16 * self.own_parts * gathers))

    def out_free(self, eng, i, s):
        eng.wait_ge(self.stored[s], (i + 1) * (16 * self.stores))
        if self.copy is not None:
            eng.wait_ge(self.kept[s], (i + 1) * 16)


class LayerNorm:

    def __init__(self, f, name=""):
        self.stats = f.sb(f"stats{name}", [P, SLOTS, U, 6])
        self.mv = f.sb(f"mv{name}", [P, SLOTS, U, 2])
        self.std = f.sb(f"std{name}", [P, SLOTS, U])
        self.rstd = f.sb(f"rstd{name}", [P, SLOTS, U])
        self.shift = f.sb(f"shift{name}", [P, SLOTS, U])
        self.eps = f.sb(f"eps{name}", [P, 1])
        self.z_ready, self.stats_ready, self.mv_ready, self.std_ready, self.rstd_ready, self.shift_ready = (
            f.sem(f"{n}{name}") for n in ("z_ready", "stats_ready", "mv_ready", "std_ready", "rstd_ready",
                                          "shift_ready"))
        self.eps_set = f.sem(f"eps_set{name}")
        self.sems = [self.z_ready, self.stats_ready, self.mv_ready, self.std_ready, self.rstd_ready,
                     self.shift_ready]

    def setup(self, dve):
        dve.memset(self.eps[:], EPS).then_inc(self.eps_set, 1)

    def statistics(self, dve, i, s, z):
        q = i * SLOTS + s
        dve.wait_ge(self.z_ready, done(q))
        for u in range(U):
            b = dve.bn_stats(self.stats[:, s, u, :], z[:, s, u, :])
        b.then_inc(self.stats_ready, 1)

    def aggregate(self, dve, i, s, tick):
        q = i * SLOTS + s
        dve.wait_ge(self.stats_ready, done(q))
        dve.sem_inc(tick, 1)
        for u in range(U):
            b = dve.bn_aggr(self.mv[:, s, u, :], self.stats[:, s, u, :])
        b.then_inc(self.mv_ready, 1)

    def deviation(self, act, i, s):
        q = i * SLOTS + s
        act.wait_ge(self.mv_ready, done(q))
        act.activation(self.std[:, s], self.mv[:, s, :, 1], ACT.Sqrt, bias=self.eps[:]).then_inc(self.std_ready, 1)

    def invert(self, dve, i, s):
        q = i * SLOTS + s
        dve.wait_ge(self.std_ready, done(q))
        dve.reciprocal(self.rstd[:, s], self.std[:, s]).then_inc(self.rstd_ready, 1)

    def offset(self, dve, i, s):
        q = i * SLOTS + s
        dve.wait_ge(self.rstd_ready, done(q))
        dve.scalar_tensor_tensor(self.shift[:, s], self.mv[:, s, :, 0], -1.0, self.rstd[:, s],
                                 ALU.mult, ALU.mult).then_inc(self.shift_ready, 1)

    def scale(self, act, i, s, z, out, ready, r=None, table=None):
        q = i * SLOTS + s
        if r:
            r.out_free(act, i, s)
        act.wait_ge(self.shift_ready, done(q))
        for u in range(U):
            b = act.activation(out[:, s, u, :], z[:, s, u, :], ACT.Identity, bias=self.shift[:, s, u:u + 1],
                               scale=self.rstd[:, s, u:u + 1])
        b.then_inc(ready, 1)
        if table is not None:
            r.store(act, i, s, (out, table))
        if r and r.copy is not None:
            act.wait_ge(ready, done(q))
            act.dma_start(groups_of(r.copy)[q], out[:, s]).then_inc(r.kept[s], 16)


def hyper_rows(nc, T, S, name, raw, out, affine):
    with Phase(nc, name) as f:
        r = Rows(f, S, dense=False, stores=U)
        rows = f.sb("rows", [P, SLOTS, U, C + 1])
        inv = f.sb("inv", [P, SLOTS, U, 1])
        mean = f.sb("mean", [P, SLOTS, U, C])
        inverted, scaled, shifted = f.sem("inverted"), f.sem("scaled"), f.sem("shifted")
        block = f.block()

        @block.sync
        def _(sp):
            r.prime(sp, (inverted, scaled, shifted))
            r.load(sp, [(rows, groups_of(raw))])
            r.finish(sp)

        @block.gpsimd
        def _(pool):
            r.prime_stores(pool)
            r.pool_loop(pool, scatters=(mean, out, SCE, N_HYPER))

        @block.vector
        def _(dve):
            def invert(i, s):
                q = i * SLOTS + s
                dve.wait_ge(r.ready, free(q))
                r.wait_loads(dve, i, s, 1)
                dve.reciprocal(inv[:, s], rows[:, s, :, C:C + 1]).then_inc(inverted, 1)

            def divide(i, s):
                q = i * SLOTS + s
                dve.wait_ge(inverted, done(q))
                r.out_free(dve, i, s)
                m = dve.tensor_tensor(mean[:, s], rows[:, s, :, 0:C], inv[:, s].to_broadcast([P, U, C]),
                                      ALU.mult)
                m.then_inc(r.used, 1)
                if affine:
                    dve.wait_ge(r.used, done(q))
                    dve.tensor_tensor(mean[:, s], mean[:, s], bc_rows(S.affine[:, 0, :]), ALU.mult
                                      ).then_inc(scaled, 1)
                    dve.wait_ge(scaled, done(q))
                    dve.tensor_tensor(mean[:, s], mean[:, s], bc_rows(S.affine[:, 1, :]), ALU.add
                                      ).then_inc(shifted, 1)
                dve.wait_ge(shifted if affine else r.used, done(q))
                dve.sem_inc(r.ready, 1)

            pipelined(dve, r.iters, [
                (0, divide),
                (1, invert),
            ])


def join_weights(nc, T, name):
    with Phase(nc, name) as f:
        joined = f.sem("joined")
        block = f.block()
        part = N_HYPER // 10

        @block.sync
        def _(sp):
            for k in range(10):
                sp.dma_start(T["EW"][k * part:(k + 1) * part, 0:C], T["E"][k * part:(k + 1) * part, :]
                             ).then_inc(joined, 16)
            sp.wait_ge(joined, 160)


def node_rows(nc, T, A, S, name, raw, layer):
    with Phase(nc, name) as f:
        r = Rows(f, S, dense=False, stores=U)
        rows = f.sb("rows", [P, SLOTS, U, C + 1])
        own = f.sb("own", [P, SLOTS, U, C])
        pos = f.sb("pos", [P, SLOTS, U, 1])
        safe = f.sb("safe", [P, SLOTS, U, 1])
        inv = f.sb("inv", [P, SLOTS, U, 1])
        mean = f.sb("mean", [P, SLOTS, U, C])
        mean_t = f.sb("mean_t", [P, SLOTS, U * P])
        w = f.sb("w", [P, C])
        bias = f.sb("bias", [P, C])
        z = f.sb("z", [P, SLOTS, U, C])
        res = f.sb("res", [P, SLOTS, U, C])
        flagged = f.sb("flagged", [P, SLOTS, U, C])
        squares = f.sb("squares", [P, SLOTS, U, C])
        ones = f.sb("ones", [P, P])
        zeros = f.sb("zeros", [P, U * C])
        ps_t = [f.ps(f"ps_t{s}", [P, 512]) for s in range(2)]
        ps_o = [f.ps(f"ps_o{s}", [P, 512]) for s in range(2)]
        ps_sum = f.ps("ps_sum", [P, 512])
        ps_sq = f.ps("ps_sq", [P, 512])
        masked, inverted, scaled, turned, turned_out, product = (f.sem(n) for n in (
            "masked", "inverted", "scaled", "turned", "turned_out", "product"))
        flag_set, squared, counted, ones_set, summed = (f.sem(n) for n in (
            "flag_set", "squared", "counted", "ones_set", "summed"))
        ln = LayerNorm(f) if layer == 2 else None
        block = f.block()

        @block.sync
        def _(sp):
            sp.dma_start(w[:], A[f"L0_W{layer}T"]).then_inc(r.weights, 16)
            sp.dma_start(bias[:], A["L0_b2_rows"]).then_inc(r.weights, 16)
            sp.wait_ge(r.weights, 32)
            r.prime(sp, (masked, inverted, scaled, turned, turned_out, product, flag_set, squared, counted,
                         *(ln.sems if ln else ())))
            r.load(sp, [(rows, groups_of(raw))])
            r.finish(sp)

        @block.gpsimd
        def _(pool):
            r.prime_stores(pool)
            if layer == 1:
                r.pool_loop(pool, scatters=(res, T["X1"], SCS, NP_))
            else:
                r.pool_loop(pool, gathers=(own, A["x"], NOD, flag_set), scatters=(res, T["X1"], SCS, NP_),
                            ahead=5)

        @block.vector
        def _(dve):
            dve.memset(ones[:], 1.0).then_inc(ones_set, 1)
            dve.memset(zeros[:], 0.0).then_inc(ones_set, 1)
            if ln:
                ln.setup(dve)
            dve.wait_ge(r.weights, 32)

            def mask(i, s):
                q = i * SLOTS + s
                dve.wait_ge(r.used, free(q))
                r.wait_loads(dve, i, s, 1)
                dve.tensor_scalar(pos[:, s], rows[:, s, :, C:C + 1], 0.0, None, ALU.is_gt)
                dve.tensor_scalar(safe[:, s], rows[:, s, :, C:C + 1], 1.1754944e-38, None, ALU.max
                                  ).then_inc(masked, 1)

            def invert(i, s):
                q = i * SLOTS + s
                dve.wait_ge(masked, done(q))
                dve.reciprocal(inv[:, s], safe[:, s]).then_inc(inverted, 1)

            def gate(i, s):
                q = i * SLOTS + s
                dve.wait_ge(inverted, done(q))
                dve.tensor_tensor(safe[:, s], inv[:, s], pos[:, s], ALU.mult).then_inc(scaled, 1)

            def divide(i, s):
                q = i * SLOTS + s
                dve.wait_ge(scaled, done(q))
                dve.wait_ge(turned, free(q))
                dve.tensor_tensor(mean[:, s], rows[:, s, :, 0:C], safe[:, s].to_broadcast([P, U, C]),
                                  ALU.mult).then_inc(r.used, 1)

            def take_product(i, s):
                q = i * SLOTS + s
                if layer == 1:
                    dve.wait_ge(product, done(q))
                    r.out_free(dve, i, s)
                    dve.tensor_copy(res[:, s], ps_o[s % 2][:].rearrange("p (u c) -> p u c", u=U)
                                    ).then_inc(r.ready, 1)
                    dve.wait_ge(counted, free(q))
                    dve.tensor_tensor(flagged[:, s], ps_o[s % 2][:].rearrange("p (u c) -> p u c", u=U),
                                      S.colf[:, SM, bass.ds(q * U, U)].unsqueeze(2).to_broadcast([P, U, C]),
                                      ALU.mult).then_inc(flag_set, 1)
                else:
                    dve.wait_ge(product, done(q))
                    r.wait_loads(dve, i, s, 0, 1)
                    dve.wait_ge(r.ready, free(q))
                    dve.tensor_tensor(z[:, s], ps_o[s % 2][:].rearrange("p (u c) -> p u c", u=U), own[:, s],
                                      ALU.add).then_inc(flag_set, 1)
                    dve.wait_ge(flag_set, done(q))
                    dve.tensor_tensor(z[:, s], z[:, s], bc_rows(bias[:]), ALU.add).then_inc(ln.z_ready, 1)

            def statistics(i, s):
                ln.statistics(dve, i, s, z)

            def aggregate(i, s):
                ln.aggregate(dve, i, s, r.tick)

            def invert_std(i, s):
                ln.invert(dve, i, s)

            def offset(i, s):
                ln.offset(dve, i, s)

            pipelined(dve, r.iters, [
                *([(0, invert_std)] if ln else []),
                (4, mask),
                *([(0, offset)] if ln else []),
                (4, invert),
                (2, take_product),
                *([(2, statistics)] if ln else []),
                (4, gate),
                *([(2, aggregate)] if ln else []),
                (4, divide),
            ])

        @block.tensor
        def _(pe):
            pe.wait_ge(r.weights, 32)
            pe.wait_ge(ones_set, 2)
            if layer == 1:
                for p in (ps_sum, ps_sq):
                    pe.matmul(p[:], ones[:], zeros[:], start=True, stop=False, skip_group_check=True)

            def turn(i, s):
                q = i * SLOTS + s
                pe.wait_ge(r.used, done(q))
                pe.wait_ge(turned_out, two_behind(q))
                for u in range(U):
                    t = pe.transpose(ps_t[s % 2][:, u * P:(u + 1) * P], mean[:, s, u, :], S.ident[:])
                t.then_inc(turned, 1)

            def multiply(i, s):
                q = i * SLOTS + s
                pe.wait_ge(turned_out, done(q))
                pe.wait_ge(flag_set, two_behind(q))
                for u in range(U):
                    t = pe.matmul(ps_o[s % 2][:, u * C:(u + 1) * C], mean_t[:, s, u * P:(u + 1) * P], w[:],
                                  start=True, stop=True)
                t.then_inc(product, 1)

            def count(i, s):
                q = i * SLOTS + s
                pe.wait_ge(squared, done(q))
                pe.matmul(ps_sum[:], ones[:], flagged[:, s].rearrange("p u c -> p (u c)"),
                          start=False, stop=False, skip_group_check=True)
                pe.matmul(ps_sq[:], ones[:], squares[:, s].rearrange("p u c -> p (u c)"),
                          start=False, stop=False, skip_group_check=True).then_inc(counted, 1)

            pipelined(pe, r.iters, [
                *([(0, count)] if layer == 1 else []),
                (2, multiply),
                (3, turn),
            ])

        @block.scalar
        def _(act):
            if ln:
                act.wait_ge(ln.eps_set, 1)

            def take_turned(i, s):
                q = i * SLOTS + s
                act.wait_ge(turned, done(q))
                act.wait_ge(product, free(q))
                act.activation(mean_t[:, s], ps_t[s % 2][:], ACT.Copy).then_inc(turned_out, 1)

            def square(i, s):
                q = i * SLOTS + s
                act.wait_ge(flag_set, done(q))
                act.wait_ge(counted, free(q))
                act.activation(squares[:, s], flagged[:, s], ACT.Square).then_inc(squared, 1)

            def deviation(i, s):
                ln.deviation(act, i, s)

            def scale(i, s):
                ln.scale(act, i, s, z, res, r.ready, r)

            pipelined(act, r.iters, [
                *([(1, square)] if layer == 1 else []),
                *([(1, deviation)] if layer == 2 else []),
                *([(0, scale)] if layer == 2 else []),
                (3, take_turned),
            ])
            if layer == 1:
                act.wait_ge(counted, r.iters * SLOTS + SLOTS)
                act.activation(S.affine_sums[:, 0, :], ps_sum[:], ACT.Copy).then_inc(summed, 1)
                act.activation(S.affine_sums[:, 1, :], ps_sq[:], ACT.Copy).then_inc(summed, 1)


def batch_norm(nc, A, S):
    with Phase(nc, "bn") as f:
        rows = f.sb("rows", [P, 3, C])
        tot = f.sb("tot", [P, 2, C])
        mean = f.sb("mean", [P, 2, C])
        sq = f.sb("sq", [P, C])
        var = f.sb("var", [P, C])
        std = f.sb("std", [P, C])
        inv = f.sb("inv", [P, C])
        mu = f.sb("mu", [P, C])
        eps = f.sb("eps", [P, 1])
        loaded, stage, rooted = f.sem("loaded"), f.sem("stage"), f.sem("rooted")
        block = f.block()
        marks = {}

        @block.sync
        def _(sp):
            for k, n in enumerate(("L0_b1_rows", "L0_gamma_rows", "L0_beta_rows")):
                sp.dma_start(rows[:, k, :], A[n]).then_inc(loaded, 16)

        @block.vector
        def _(dve):
            n = 0

            def step(x):
                nonlocal n
                x.then_inc(stage, 1)
                n += 1
                dve.wait_ge(stage, n)

            step(dve.memset(eps[:], EPS))
            step(dve.tensor_reduce(tot[:], S.affine_sums[:].rearrange("p k (u c) -> p k c u", u=U), AX_X, ALU.add))
            step(dve.tensor_scalar(mean[:], tot[:], 1.0 / N_NODES, None, ALU.mult))
            step(dve.tensor_tensor(sq[:], mean[:, 0, :], mean[:, 0, :], ALU.mult))
            step(dve.tensor_tensor(var[:], mean[:, 1, :], sq[:], ALU.subtract))
            step(dve.tensor_scalar(var[:], var[:], 0.0, None, ALU.max))
            marks["var"] = n
            dve.wait_ge(rooted, 1)
            dve.wait_ge(loaded, 48)
            step(dve.reciprocal(inv[:], std[:]))
            step(dve.tensor_tensor(S.affine[:, 0, :], rows[:, 1, :], inv[:], ALU.mult))
            step(dve.tensor_tensor(mu[:], mean[:, 0, :], rows[:, 0, :], ALU.add))
            step(dve.tensor_tensor(mu[:], rows[:, 0, :], mu[:], ALU.subtract))
            step(dve.tensor_tensor(mu[:], mu[:], S.affine[:, 0, :], ALU.mult))
            step(dve.tensor_tensor(S.affine[:, 1, :], mu[:], rows[:, 2, :], ALU.add))

        @block.scalar
        def _(act):
            act.wait_ge(stage, marks["var"])
            act.activation(std[:], var[:], ACT.Sqrt, bias=eps[:]).then_inc(rooted, 1)


class NodeNorm:

    def __init__(self, f, S, adds, bias, out, half=None):
        self.twice = half is None
        if half is not None:
            rows = slice(half * NP_ // 2, (half + 1) * NP_ // 2)
            adds, out = [t[rows, :] for t in adds], out[rows, :]
        self.adds, self.bias, self.out = adds, bias, out
        self.r = Rows(f, S, dense=True, stores=1, groups=None if self.twice else NODE_GROUPS // 2, name="norm_")
        self.bufs = [f.sb(f"norm_in{k}", [P, SLOTS, U, t.shape[1]]) for k, t in enumerate(adds)]
        self.z = f.sb("norm_z", [P, SLOTS, U, C])
        self.res = f.sb("norm_res", [P, SLOTS, U, C])
        self.ln = LayerNorm(f, "norm_")
        self.added = f.sem("norm_added")

    def sync_start(self, sp):
        self.r.prime(sp, (self.added, *self.ln.sems))

    def sync_steps(self, sp):
        return [(6, self.r.load_step(sp, [(b, groups_of(t)) for b, t in zip(self.bufs, self.adds)]))]

    def vector_steps(self, dve):
        r, ln, z, bufs = self.r, self.ln, self.z, self.bufs

        def add(i, s):
            q = i * SLOTS + s
            dve.wait_ge(r.ready, free(q))
            r.wait_loads(dve, i, s, len(bufs))
            dve.tensor_tensor(z[:, s], bufs[0][:, s, :, 0:C], bc_rows(self.bias), ALU.add
                              ).then_inc(self.added if len(bufs) == 2 else ln.z_ready, 1)
            if len(bufs) == 2:
                dve.wait_ge(self.added, done(q))
                dve.tensor_tensor(z[:, s], z[:, s], bufs[1][:, s, :, 0:C], ALU.add).then_inc(ln.z_ready, 1)

        def statistics(i, s):
            ln.statistics(dve, i, s, z)
            dve.sem_inc(r.used, 1)

        return [(0, lambda i, s: ln.invert(dve, i, s)),
                (0, lambda i, s: ln.offset(dve, i, s)),
                (2, add),
                (2, statistics),
                (2, lambda i, s: ln.aggregate(dve, i, s, r.tick))]

    def scalar_start(self, act):
        act.wait_ge(self.ln.eps_set, 1)
        self.r.prime_stores(act)

    def scalar_steps(self, act):
        r, ln = self.r, self.ln
        return [(1, lambda i, s: ln.deviation(act, i, s)),
                (0, lambda i, s: ln.scale(act, i, s, self.z, self.res, r.ready, r, groups_of(self.out)))]


def weights_phase(nc, A, S):
    with Phase(nc, "weights") as f:
        att1 = f.sb("att1", [P, 2, HC])
        att2 = f.sb("att2", [P, 2, C])
        prod1 = f.sb("prod1", [P, 2, HC])
        prod2 = f.sb("prod2", [P, 2, 2, C])
        cols = f.sb("cols", [P, 2])
        w = f.sb("w", [P, 2, C])
        rows = f.sb("rows", [P, 3, C])
        hid = f.sb("hid", [P, 2])
        absx = f.sb("absx", [P, 1])
        ex = f.sb("ex", [P, 1])
        lg = f.sb("lg", [P, 1])
        spread = f.sb("spread", [P, 2, P])
        one = f.sb("one", [P, 1])
        acc = f.ps("acc", [P, 2, C])
        loaded, stage, logs, multiplied = f.sem("loaded"), f.sem("stage"), f.sem("logs"), f.sem("multiplied")
        block = f.block()
        marks = {}

        @block.sync
        def _(sp):
            for out, src in ((S.W1[:], A["L1_W1"]), (S.W2x[:, :, 0:C], A["L1_W2"]), (S.b1col[:], A["L1_b1_cols"]),
                             (att1[:, 0, :], A["L1_as1"]), (att1[:, 1, :], A["L1_ad1"]),
                             (att2[:, 0, :], A["L1_as2"]), (att2[:, 1, :], A["L1_ad2"]),
                             (cols[:, 0:1], A["L2_b1_col"]), (cols[:, 1:2], A["L3_bfc1_col"]),
                             (w[:, 0, :], A["L2_W2"]), (w[:, 1, :], A["L3_Wfc2T"]),
                             (rows[:, 0, :], A["L2_b2_rows"]), (rows[:, 1, :], A["L2_bpre_rows"]),
                             (rows[:, 2, :], A["L3_bfc2_rows"]), (S.b0[:], A["L0_b2_rows"]),
                             (S.b2[:], A["L1_b2_rows"])):
                sp.dma_start(out, src).then_inc(loaded, 16)

        @block.vector
        def _(dve):
            n = 0

            def step(*ins):
                nonlocal n
                for x in ins:
                    x.then_inc(stage, 1)
                n += len(ins)
                dve.wait_ge(stage, n)

            dve.wait_ge(loaded, 16 * 16)
            step(dve.memset(one[:], 1.0), dve.memset(S.W2x[:, :, C + 2:H2W], 0.0))
            marks["one"] = n
            step(*[dve.tensor_tensor(prod1[:, k, :], S.W1[:], att1[:, k, :], ALU.mult) for k in range(2)],
                 *[dve.tensor_tensor(prod2[:, k, :, :], S.W2x[:, :, 0:C],
                                     att2[:, k, :].unsqueeze(1).to_broadcast([P, 2, C]), ALU.mult)
                   for k in range(2)])
            step(*[dve.tensor_reduce(S.WA[:, k * HEADS:(k + 1) * HEADS],
                                     prod1[:, k, :].rearrange("p (h c) -> p h c", h=HEADS), AX_X, ALU.add)
                   for k in range(2)],
                 *[dve.tensor_reduce(S.W2x[:, :, C + k:C + k + 1], prod2[:, k, :, :], AX_X, ALU.add)
                   for k in range(2)])
            step(dve.tensor_scalar(hid[:], cols[:], 0.0, None, ALU.max))
            dve.wait_ge(logs, 3)
            step(dve.scalar_tensor_tensor(hid[:, 1:2], lg[:], -LOG2, hid[:, 1:2], ALU.add, ALU.add))
            step(dve.tensor_copy(spread[:], hid[:].unsqueeze(2).to_broadcast([P, 2, P])))
            marks["spread"] = n
            dve.wait_ge(multiplied, 1)
            step(dve.tensor_tensor(S.c2[:], acc[:, 0, :], rows[:, 0, :], ALU.add),
                 dve.tensor_tensor(S.c3[:], acc[:, 1, :], rows[:, 2, :], ALU.add))
            step(dve.tensor_scalar(S.c2[:], S.c2[:], 0.0, None, ALU.max))
            step(dve.tensor_tensor(S.c2[:], S.c2[:], rows[:, 1, :], ALU.add))

        @block.scalar
        def _(act):
            act.wait_ge(stage, marks["one"])
            act.activation(absx[:], cols[:, 1:2], ACT.Abs).then_inc(logs, 1)
            act.wait_ge(logs, 1)
            act.activation(ex[:], absx[:], ACT.Exp, scale=-1.0).then_inc(logs, 1)
            act.wait_ge(logs, 2)
            act.activation(lg[:], ex[:], ACT.Ln, bias=one[:]).then_inc(logs, 1)

        @block.tensor
        def _(pe):
            pe.wait_ge(stage, marks["spread"])
            for k in range(2):
                m = pe.matmul(acc[:, k, :], spread[:, k, :], w[:, k, :], start=True, stop=True)
            m.then_inc(multiplied, 1)



def gat_rows(nc, T, S, name, dense):
    with Phase(nc, name) as f:
        r = Rows(f, S, dense, stores=2 if dense else U)
        w_in = C if dense else HC + HEADS
        rows = f.sb("rows", [P, SLOTS, U, w_in])
        x_t = f.sb("x_t", [P, SLOTS, U * P])
        inv = f.sb("inv", [P, SLOTS, U, HEADS])
        den = f.sb("den", [P, SLOTS, U, HEADS])
        mean = f.sb("mean", [P, SLOTS, U, HC])
        aa = f.sb("aa", [P, SLOTS, U, 2 * HEADS])
        pos = f.sb("pos", [P, SLOTS, 2, U * P])
        neg = f.sb("neg", [P, SLOTS, 2, U * P])
        elu = f.sb("elu", [P, SLOTS, 2, U * P])
        res = f.sb("res", [P, SLOTS, U, H2W])
        ps_t = f.ps("ps_t", [P, U * P])
        ps_a = f.ps("ps_a", [P, 512])
        ps_h = [f.ps(f"ps_h{s}", [P, 2, U * P]) for s in range(2)]
        ps_o = f.ps("ps_o", [P, U, 256])
        x_ready, hidden, aa_out, relued, clipped, exped, elu_ready, product, safe, inverted, normed = (
            f.sem(n) for n in ("x_ready", "hidden", "aa_out", "relued", "clipped", "exped", "elu_ready",
                               "product", "safe", "inverted", "normed"))
        joined = f.sem("joined")
        block = f.block()

        @block.sync
        def _(sp):
            r.prime(sp, (x_ready, hidden, aa_out, relued, clipped, exped, elu_ready, product, safe, inverted,
                         normed))
            r.load(sp, [(rows, groups_of(T["X1"] if dense else T["RAW260"]))])
            r.finish(sp)
            if dense:
                sp.wait_ge(joined, 16 * 13)

        @block.gpsimd
        def _(pool):
            if dense:
                part = NP_ // 13
                for k in range(13):
                    pool.dma_start(T["X1A"][k * part:(k + 1) * part, 0:C], T["X1"][k * part:(k + 1) * part, :]
                                   ).then_inc(joined, 16)
            if not dense:
                r.prime_stores(pool)
                r.pool_loop(pool, scatters=(res, T["H2"], SCD, NP_))

        @block.tensor
        def _(pe):
            def turn(i, s):
                q = i * SLOTS + s
                if dense:
                    r.wait_loads(pe, i, s, 1)
                    pe.wait_ge(x_ready, behind(q))
                    for u in range(U):
                        t = pe.transpose(ps_t[:, u * P:(u + 1) * P], rows[:, s, u, :], S.ident[:])
                    t.then_inc(r.used, 1)

            def hidden_layer(i, s):
                q = i * SLOTS + s
                pe.wait_ge(relued, two_behind(q))
                pe.wait_ge(clipped, two_behind(q))
                if dense:
                    pe.wait_ge(aa_out, behind(q))
                    pe.wait_ge(x_ready, done(q))
                    for u in range(U):
                        pe.matmul(ps_a[:, u * 8:(u + 1) * 8], x_t[:, s, u * P:(u + 1) * P], S.WA[:],
                                  start=True, stop=True)
                    for c in range(2):
                        t = pe.matmul(ps_h[s % 2][:, c, :], S.W1[:, c * P:(c + 1) * P], x_t[:, s],
                                      start=True, stop=True)
                else:
                    pe.wait_ge(normed, done(q))
                    for c in range(2):
                        for u in range(U):
                            t = pe.transpose(ps_h[s % 2][:, c, u * P:(u + 1) * P],
                                             mean[:, s, u, c * P:(c + 1) * P], S.ident[:])
                t.then_inc(hidden, 1)

            def multiply(i, s):
                q = i * SLOTS + s
                pe.wait_ge(elu_ready, done(q))
                pe.wait_ge(r.ready, behind(q))
                for u in range(U):
                    for c in range(2):
                        t = pe.matmul(ps_o[:, u, 0:H2W], elu[:, s, c, u * P:(u + 1) * P], S.W2x[:, c, :],
                                      start=(c == 0), stop=(c == 1))
                t.then_inc(product, 1)

            pipelined(pe, r.iters, [
                (0, multiply),
                (3, hidden_layer),
                (4, turn),
            ])

        @block.vector
        def _(dve):
            def guard(i, s):
                q = i * SLOTS + s
                dve.wait_ge(normed, free(q))
                r.wait_loads(dve, i, s, 1)
                dve.tensor_scalar(den[:, s], rows[:, s, :, HC:HC + HEADS], 1e-30, None, ALU.max
                                  ).then_inc(safe, 1)

            def invert(i, s):
                q = i * SLOTS + s
                dve.wait_ge(safe, done(q))
                dve.reciprocal(inv[:, s], den[:, s]).then_inc(inverted, 1)

            def divide(i, s):
                q = i * SLOTS + s
                dve.wait_ge(inverted, done(q))
                dve.wait_ge(hidden, free(q))
                for u in range(U):
                    t = dve.tensor_tensor(mean[:, s, u, :].rearrange("p (h c) -> p h c", h=HEADS),
                                          rows[:, s, u, 0:HC].rearrange("p (h c) -> p h c", h=HEADS),
                                          inv[:, s, u, :].unsqueeze(2).to_broadcast([P, HEADS, HID]),
                                          ALU.mult)
                t.then_inc(normed, 1)
                dve.wait_ge(normed, done(q))
                dve.sem_inc(r.used, 1)

            def clip(i, s):
                q = i * SLOTS + s
                dve.wait_ge(hidden, done(q))
                if dense:
                    r.out_free(dve, i, s)
                    dve.tensor_copy(aa[:, s].rearrange("p u k -> p (u k)"), ps_a[:, 0:U * 8]).then_inc(aa_out, 1)
                dve.wait_ge(exped, free(q))
                for c in range(2):
                    t = dve.tensor_scalar(neg[:, s, c, :], ps_h[s % 2][:, c, :], S.b1col[:, c:c + 1], 0.0,
                                          ALU.add, ALU.min)
                t.then_inc(clipped, 1)

            def add(i, s):
                q = i * SLOTS + s
                dve.wait_ge(exped, done(q))
                dve.wait_ge(product, free(q))
                dve.scalar_tensor_tensor(elu[:, s].rearrange("p c r -> p (c r)"),
                                         neg[:, s].rearrange("p c r -> p (c r)"), -1.0,
                                         pos[:, s].rearrange("p c r -> p (c r)"), ALU.add, ALU.add
                                         ).then_inc(elu_ready, 1)

            pipelined(dve, r.iters, [
                (1, add),
                (3, clip),
                *([(4, guard)] if not dense else []),
                *([(4, invert)] if not dense else []),
                *([(4, divide)] if not dense else []),
            ])

        @block.scalar
        def _(act):
            if dense:
                r.prime_stores(act)

            def take_turned(i, s):
                q = i * SLOTS + s
                act.wait_ge(r.used, done(q))
                act.wait_ge(hidden, free(q))
                act.activation(x_t[:, s], ps_t[:], ACT.Copy).then_inc(x_ready, 1)

            def positive(i, s):
                q = i * SLOTS + s
                act.wait_ge(clipped, done(q))
                act.wait_ge(elu_ready, free(q))
                for c in range(2):
                    t = act.activation(pos[:, s, c, :], ps_h[s % 2][:, c, :], ACT.Relu, bias=S.b1col[:, c:c + 1])
                t.then_inc(relued, 1)

            def exponent(i, s):
                q = i * SLOTS + s
                act.wait_ge(clipped, done(q))
                act.wait_ge(elu_ready, free(q))
                act.activation(neg[:, s].rearrange("p c r -> p (c r)"),
                               neg[:, s].rearrange("p c r -> p (c r)"), ACT.Exp).then_inc(exped, 1)

            def take_product(i, s):
                q = i * SLOTS + s
                act.wait_ge(product, done(q))
                r.out_free(act, i, s)
                act.activation(res[:, s], ps_o[:, :, 0:H2W], ACT.Copy).then_inc(r.ready, 1)
                if dense:
                    act.wait_ge(aa_out, done(q))
                    r.store(act, i, s, (res, groups_of(T["H2"])), (aa, groups_of(T["X1A"])[:, :, :, C:]))

            pipelined(act, r.iters, [
                (2, positive),
                (2, exponent),
                (0, take_product),
                *([(4, take_turned)] if dense else []),
            ])


def attention_phase(nc, T, S, name, H, table, kept, norm=None):
    ET, HT = EDGE_TILES, HALF_T
    tw = table.shape[1]
    with Phase(nc, name) as f:
        slot = f.sb("slot", [P, SLOTS, 2, U], I32)
        got = f.sb("got", [P, SLOTS, 2, U, tw])
        terms = f.sb("terms", [P, 2, 2 * H, ET])
        keys = f.sb("keys", [HT, 2, P])
        prv = f.sb("prv", [HT, 2, P])
        nxt = f.sb("nxt", [HT, 2, P])
        pen = f.sb("pen", [HT, 2, 4, P])
        line = f.sb("line", [HT, 2, H, P])
        fwd = f.sb("fwd", [HT, 2, H, P])
        seg = f.sb("seg", [HT, 2, H, P])
        edge_keys = f.sb("edge_keys", [HT, 2, ET])
        own_keys = f.sb("own_keys", [HT, 2, 2])
        apart = f.sb("apart", [HT, 2, 2, 2 * ET])
        ends = f.sb("ends", [HT, H, 2 * ET])
        cand = f.sb("cand", [HT, H, 2 * ET])
        best = f.sb("best", [HT, 2, 2, H])
        most = f.sb("most", [P, H, ET])
        t1 = f.sb("t1", [P, H, ET])
        t2 = f.sb("t2", [P, H, ET])
        m = f.sb("m", [P, H, ET])
        ps_line = f.ps("ps_line", [P, 4, 512])
        ps_back = f.ps("ps_back", [P, 4, 512])
        picked, tick, copied = (f.sem(n) for n in ("picked", "tick", "copied"))
        loaded, stage, turned, turned_back, sent, fetched, exps = (
            f.sem(n) for n in ("loaded", "stage", "turned", "turned_back", "sent", "fetched", "exps"))
        gathered, stored = f.sems("gathered"), f.sems("stored")
        primed = prime_stores(f, stored, 2, S.ident_dram)
        norm = norm(f) if norm else None
        block = f.block()
        iters = EDGE_GROUPS // SLOTS
        marks = {}
        K = T["keys"]

        @block.gpsimd
        def _(pool):
            pool.sem_inc(copied, SLOTS)
            with pool.Fori(0, EDGE_GROUPS // SLOTS) as i:
                for s in range(SLOTS):
                    q = i * SLOTS + s
                    pool.wait_ge(copied, free(q))
                    pool.wait_ge(stored[s], (i + 1) * 32)
                    for k, col in enumerate((SRC, DST)):
                        t = pool.tensor_copy(slot[:, s, k], S.coli[:, col, bass.ds(q * U, U)])
                    t.then_inc(picked, 1)
                    pool.wait_ge(picked, q + 1)
                    pool.sem_inc(tick, 1)
                    for k in range(2):
                        for u in range(U):
                            gather(pool, got[:, s, k, u, :], table, slot[:, s, k, u:u + 1]
                                   ).then_inc(gathered[s], 16)

        @block.vector
        def _(dve):
            if norm:
                norm.ln.setup(dve)

            def take_terms(i, s):
                dve.wait_ge(gathered[s], (i + 1) * (16 * 2 * U))
                for k in range(2):
                    t = dve.tensor_copy(terms[:, k, :, bass.ds((i * SLOTS + s) * U, U)],
                                        got[:, s, k, :, C:C + 2 * H].rearrange("p u k -> p k u"))
                t.then_inc(copied, 1)

            pipelined(dve, iters, [(0, take_terms)], norm.vector_steps(dve) if norm else ())
            n = 0

            def step(*ins):
                nonlocal n
                for x in ins:
                    x.then_inc(stage, 1)
                n += len(ins)
                dve.wait_ge(stage, n)

            def differ(out, a, b):
                return [dve.tensor_tensor(out, a, b, ALU.not_equal)]

            dve.wait_ge(loaded, 16 * 5)
            step(*differ(pen[:, :, 0, :], keys[:], prv[:]), *differ(pen[:, :, 1, :], keys[:], nxt[:]),
                 *differ(pen[:, :, 2, :], keys[:], keys[:, :, 0:1].to_broadcast([HT, 2, P])),
                 *differ(pen[:, :, 3, :], keys[:], keys[:, :, P - 1:P].to_broadcast([HT, 2, P])),
                 dve.tensor_copy(own_keys[:, :, 0:1], keys[:, :, 0:1]),
                 dve.tensor_copy(own_keys[:, :, 1:2], keys[:, :, P - 1:P]))
            step(*[dve.tensor_scalar(apart[:, c, k, :], edge_keys[:].rearrange("p a t -> p (a t)"),
                                     own_keys[:, c, k:k + 1], NEG, ALU.not_equal, ALU.mult)
                   for c in range(2) for k in range(2)],
                 dve.tensor_scalar(pen[:], pen[:], NEG, None, ALU.mult))
            for c in range(2):
                for h in range(H):
                    dve.wait_ge(turned, c * H + h + 1)
                    dve.tensor_copy(line[:, c, h, :], ps_line[0:HT, (c * H + h) % 4, 0:P]).then_inc(stage, 1)
                    n += 1
            marks["lines"] = n
            dve.wait_ge(stage, n)
            step(*[dve.tensor_tensor_scan(fwd[:, c, h, :], pen[:, c, 0, :], line[:, c, h, :], NEG, ALU.add, ALU.max)
                   for c in range(2) for h in range(H)])
            step(*[dve.tensor_tensor_scan(seg[:, c, h, ::-1], pen[:, c, 1, ::-1], fwd[:, c, h, ::-1], NEG,
                                          ALU.add, ALU.max)
                   for c in range(2) for h in range(H)])
            marks["tiles"] = n
            dve.wait_ge(fetched, 16)
            for c in range(2):
                for k in range(2):
                    step(dve.tensor_tensor(cand[:], ends[:], apart[:, c, k, :].unsqueeze(1)
                                           .to_broadcast([HT, H, 2 * ET]), ALU.add))
                    step(dve.tensor_reduce(best[:, c, k, :], cand[:], AX_X, ALU.max))
            for k in range(2):
                step(*[dve.scalar_tensor_tensor(seg[:, c, h, :], pen[:, c, 2 + k, :], best[:, c, k, h:h + 1],
                                                seg[:, c, h, :], ALU.add, ALU.max)
                       for c in range(2) for h in range(H)])
            marks["segments"] = n
            for c in range(2):
                for h in range(H):
                    dve.wait_ge(turned_back, c * H + h + 1)
                    dve.tensor_copy(most[:, h, c * HT:(c + 1) * HT], ps_back[:, (c * H + h) % 4, 0:HT]
                                    ).then_inc(stage, 1)
                    n += 1
            dve.wait_ge(stage, n)

            def leaky(x, y):
                return dve.scalar_tensor_tensor(x, y, SLOPE, y, ALU.mult, ALU.max)

            src_s, dst_s, dst_d = terms[:, 0, 0:H, :], terms[:, 1, 0:H, :], terms[:, 1, H:2 * H, :]
            step(dve.tensor_tensor(most[:], most[:], dst_s, ALU.max))
            step(dve.tensor_tensor(most[:], most[:], dst_d, ALU.add), dve.tensor_tensor(t1[:], src_s, dst_d, ALU.add),
                 dve.tensor_tensor(t2[:], dst_s, dst_d, ALU.add))
            step(leaky(m[:], most[:]), leaky(t1[:], t1[:]), leaky(t2[:], t2[:]))
            step(dve.tensor_tensor(t1[:], t1[:], m[:], ALU.subtract),
                 dve.tensor_tensor(t2[:], t2[:], m[:], ALU.subtract))
            marks["logits"] = n
            dve.wait_ge(exps, 2)

            def by_tile(x):
                return x[:, :, 0:H].rearrange("p t h -> p h t")

            step(dve.tensor_copy(by_tile(S.ws), t1[:]),
                 dve.tensor_tensor(by_tile(S.wd), t2[:], S.colf[:, SF, :].unsqueeze(1).to_broadcast([P, H, ET]),
                                   ALU.mult))
            step(dve.tensor_tensor(by_tile(S.wt), by_tile(S.ws), by_tile(S.wd), ALU.add))

        @block.tensor
        def _(pe):
            pe.wait_ge(copied, EDGE_GROUPS + SLOTS)
            for c in range(2):
                for h in range(H):
                    b = c * H + h
                    if b >= 4:
                        pe.wait_ge(stage, marks["lines"] - 2 * H + b - 3)
                    pe.transpose(ps_line[0:HT, b % 4, 0:P], terms[:, 0, h, c * HT:(c + 1) * HT], S.ident[:]
                                 ).then_inc(turned, 1)
            pe.wait_ge(stage, marks["segments"])
            for c in range(2):
                for h in range(H):
                    b = c * H + h
                    if b >= 4:
                        pe.wait_ge(stage, marks["segments"] + b - 3)
                    pe.transpose(ps_back[:, b % 4, 0:HT], seg[:, c, h, :], S.ident[0:HT, 0:HT]
                                 ).then_inc(turned_back, 1)

        @block.scalar
        def _(act):
            primed(act)
            if norm:
                norm.scalar_start(act)

            def keep(i, s):
                act.wait_ge(gathered[s], (i + 1) * (16 * 2 * U))
                for k in range(2):
                    act.dma_start(groups_of(kept[k])[i * SLOTS + s], got[:, s, k, :, 0:C]).then_inc(stored[s], 16)

            pipelined(act, iters, [(0, keep)], norm.scalar_steps(act) if norm else ())
            act.wait_ge(stage, marks["logits"])
            act.activation(t1[:], t1[:], ACT.Exp).then_inc(exps, 1)
            act.activation(t2[:], t2[:], ACT.Exp).then_inc(exps, 1)

        @block.sync
        def _(sp):
            for out, at in ((prv, 0), (keys, 1), (nxt, 2)):
                sp.dma_start(out[:], K[0, at:at + ET * P].rearrange("(c p e) -> p c e", p=HT, e=P)
                             ).then_inc(loaded, 16)
            with nc.allow_non_contiguous_dma(reason="first key of each tile"):
                sp.dma_start(edge_keys[:, 0, :], K[0:1, 1:1 + ET * P].rearrange("o (t e) -> o t e", e=P)[:, :, 0]
                             .to_broadcast([HT, ET])).then_inc(loaded, 16)
            sp.dma_start(edge_keys[:, 1, :], T["last"][0:1, 0:ET].to_broadcast([HT, ET])).then_inc(loaded, 16)
            if norm:
                norm.sync_start(sp)
                pipelined(sp, iters, [], norm.sync_steps(sp))
            sp.wait_ge(stage, marks["tiles"])
            dst = T["ends"][0:H, :].rearrange("h (k c p) -> k p c h", k=2, p=HT)
            with nc.allow_non_contiguous_dma(reason="one value per tile, head and end"):
                for k, e in ((0, 0), (1, P - 1)):
                    for c in range(2):
                        sp.dma_start(dst[k, :, c, :], seg[:, c, :, e]).then_inc(sent, 16)
            sp.wait_ge(sent, 64)
            sp.dma_start(ends[:], T["ends"][0:H, :].unsqueeze(0).to_broadcast([HT, H, 2 * ET])).then_inc(fetched, 16)
            for s in range(SLOTS):
                sp.wait_ge(stored[s], 32 * (iters + 1))
            if norm:
                norm.r.finish(sp)


def gat_sum(nc, T, S, name, layer):
    first = layer == 1
    tables = (T["XS"], T["XD"]) if first else (T["HS"], T["HD"])
    out = T["RAW260"] if first else T["RAW129"]
    H = HEADS if first else 1
    w = out.shape[1]
    D = w - H
    with Phase(nc, name) as f:
        rows = f.sb("rows", [P, SLOTS, 2, U, C])
        x_t = f.sb("x_t", [P, 2, 2, U * P])
        v = f.sb("v", [P, SLOTS, U, w])
        part = f.sb("part", [P, SLOTS, U, D])
        krow = f.sb("krow", [P, SLOTS, U * P])
        same = f.sb("same", [P, SLOTS, U, P])
        sums = f.sb("sums", [P, SLOTS, U, w])
        ps_t = f.ps("ps_t", [P, 2, 512])
        ps_h = f.ps("ps_h", [P, 2, U, 256]) if first else None
        acc = f.ps("acc", [P, 2, 512])
        matched, summed, copied, turned, x_ready, hidden_src, hidden_dst, weighted, parted, valued = (
            f.sem(n) for n in ("matched", "summed", "copied", "turned", "x_ready", "hidden_src", "hidden_dst",
                               "weighted", "parted", "valued"))
        loaded, keyed, stored = f.sems("rows_loaded"), f.sems("keyed"), f.sems("stored")
        primed = prime_stores(f, stored, 1, S.ident_dram)
        block = f.block()
        iters = EDGE_GROUPS // SLOTS
        out_g = groups_of(out)
        rows_used = turned if first else valued

        @block.sync
        def _(sp):
            for m in (matched, turned, x_ready, hidden_src, hidden_dst, weighted, parted, valued):
                sp.sem_inc(m, SLOTS)
            for m in (summed, copied):
                sp.sem_inc(m, 2 * SLOTS)

            def key_rows(i, s):
                q = i * SLOTS + s
                sp.wait_ge(matched, free(q))
                sp.dma_start(krow[:, s], T["keys"][0:1, bass.ds(q * (U * P) + 1, U * P)]
                             .to_broadcast([P, U * P])).then_inc(keyed[s], 16)

            def load(i, s):
                q = i * SLOTS + s
                sp.wait_ge(rows_used, free(q))
                for k in range(2):
                    sp.dma_start(rows[:, s, k], groups_of(tables[k])[q]).then_inc(loaded[s], 16)

            pipelined(sp, iters, [(4, key_rows), (6, load)])
            for s in range(SLOTS):
                sp.wait_ge(stored[s], 16 * (iters + 1))

        @block.tensor
        def _(pe):
            def turn(i, s):
                q = i * SLOTS + s
                pe.wait_ge(loaded[s], (i + 1) * 32)
                pe.wait_ge(x_ready, behind(q))
                for k in range(2):
                    for u in range(U):
                        t = pe.transpose(ps_t[:, k, u * P:(u + 1) * P], rows[:, s, k, u, :], S.ident[:])
                t.then_inc(turned, 1)

            def hidden(i, s):
                q = i * SLOTS + s
                pe.wait_ge(x_ready, done(q))
                for k, (left, ready) in enumerate(((weighted, hidden_src), (parted, hidden_dst))):
                    pe.wait_ge(left, behind(q))
                    for u in range(U):
                        t = pe.matmul(ps_h[:, k, u, :], x_t[:, s % 2, k, u * P:(u + 1) * P], S.W1[:],
                                      start=True, stop=True)
                    t.then_inc(ready, 1)

            def add_up(half):
                def step(i, s):
                    q = i * SLOTS + s
                    pe.wait_ge(valued, done(q))
                    pe.wait_ge(matched, done(q))
                    pe.wait_ge(copied, q * 2 + (half + 2 * SLOTS))
                    for b in range(2):
                        u = 2 * half + b
                        t = pe.matmul(acc[:, b, 0:w], same[:, s, u, :], v[:, s, u, :], start=True, stop=True)
                    t.then_inc(summed, 1)
                return step

            pipelined(pe, iters, [
                (0, add_up(0)),
                *([(3, turn)] if first else []),
                (0, add_up(1)),
                *([(2, hidden)] if first else []),
            ])

        @block.vector
        def _(dve):
            def match(i, s):
                q = i * SLOTS + s
                dve.wait_ge(keyed[s], (i + 1) * 16)
                dve.wait_ge(summed, q * 2 + 2)
                dve.tensor_tensor(same[:, s], krow[:, s].rearrange("p (u e) -> p u e", u=U),
                                  S.colf[:, KD, bass.ds(q * U, U)].unsqueeze(2).to_broadcast([P, U, P]),
                                  ALU.is_equal).then_inc(matched, 1)

            def heads(x):
                return x.rearrange("p u (h c) -> p u h c", h=H)

            def values(i, s):
                q = i * SLOTS + s
                dve.wait_ge(summed, q * 2 + 2)
                if not first:
                    dve.wait_ge(loaded[s], (i + 1) * 32)
                dve.tensor_copy(v[:, s, :, D:w], S.wt[:, bass.ds(q * U, U), 0:H])
                for k, (dest, wgt, mark) in enumerate(((v[:, s, :, 0:D], S.ws, weighted),
                                                       (part[:, s], S.wd, parted))):
                    wcol = wgt[:, bass.ds(q * U, U), 0:H]
                    if first:
                        dve.wait_ge((hidden_src, hidden_dst)[k], done(q))
                        dve.tensor_tensor(heads(dest), heads(ps_h[:, k]),
                                          wcol.unsqueeze(3).to_broadcast([P, U, H, HID]), ALU.mult
                                          ).then_inc(mark, 1)
                    else:
                        dve.tensor_tensor(dest, rows[:, s, k, :, :], wcol.to_broadcast([P, U, C]), ALU.mult
                                          ).then_inc(mark, 1)
                dve.wait_ge(weighted, done(q))
                dve.wait_ge(parted, done(q))
                dve.tensor_tensor(v[:, s, :, 0:D], v[:, s, :, 0:D], part[:, s], ALU.add).then_inc(valued, 1)

            pipelined(dve, iters, [(1, match), (2, values)])

        @block.scalar
        def _(act):
            primed(act)

            def take_turned(i, s):
                q = i * SLOTS + s
                act.wait_ge(turned, done(q))
                act.wait_ge(hidden_dst, two_behind(q))
                act.activation(x_t[:, s % 2], ps_t[:], ACT.Copy).then_inc(x_ready, 1)

            def take_sums(half):
                def step(i, s):
                    q = i * SLOTS + s
                    if half == 0:
                        act.wait_ge(stored[s], (i + 1) * 16)
                    act.wait_ge(summed, q * 2 + (half + 2 * SLOTS + 1))
                    act.activation(sums[:, s, 2 * half:2 * half + 2, :], acc[:, :, 0:w], ACT.Copy
                                   ).then_inc(copied, 1)
                    if half == 1:
                        act.wait_ge(copied, q * 2 + (2 * SLOTS + 2))
                        act.dma_start(out_g[q], sums[:, s]).then_inc(stored[s], 16)
                return step

            pipelined(act, iters, [
                (0, take_sums(0)),
                *([(3, take_turned)] if first else []),
                (0, take_sums(1)),
            ])


def gat_nodes(nc, T, S):
    with Phase(nc, "gatnodes") as f:
        r = Rows(f, S, dense=False, stores=U, own_parts=1, copy=T["X2E"])
        rows = f.sb("rows", [P, SLOTS, U, C + 1])
        own = f.sb("own", [P, SLOTS, U, C])
        den = f.sb("den", [P, SLOTS, U, 1])
        inv = f.sb("inv", [P, SLOTS, U, 1])
        z = f.sb("z", [P, SLOTS, U, C])
        res = f.sb("res", [P, SLOTS, U, C])
        ln = LayerNorm(f)
        safe, inverted, owned = f.sem("safe"), f.sem("inverted"), f.sem("owned")
        block = f.block()

        @block.sync
        def _(sp):
            r.prime(sp, (safe, inverted, owned, *ln.sems))
            pipelined(sp, r.iters, [
                (5, r.own_step(sp, own, T["XD"], owned)),
                (6, r.load_step(sp, [(rows, groups_of(T["RAW129"]))])),
            ])
            r.finish(sp)

        @block.gpsimd
        def _(pool):
            r.prime_stores(pool)
            r.pool_loop(pool, scatters=(res, T["X2"], SCD, NP_))

        @block.vector
        def _(dve):
            ln.setup(dve)

            def guard(i, s):
                q = i * SLOTS + s
                dve.wait_ge(r.ready, free(q))
                r.wait_loads(dve, i, s, 1)
                dve.tensor_scalar(den[:, s], rows[:, s, :, C:C + 1], 1e-30, None, ALU.max).then_inc(safe, 1)

            def invert(i, s):
                q = i * SLOTS + s
                dve.wait_ge(safe, done(q))
                dve.reciprocal(inv[:, s], den[:, s]).then_inc(inverted, 1)

            def divide(i, s):
                q = i * SLOTS + s
                dve.wait_ge(inverted, done(q))
                dve.tensor_tensor(z[:, s], rows[:, s, :, 0:C], inv[:, s].to_broadcast([P, U, C]), ALU.mult
                                  ).then_inc(r.used, 1)

            def add_own(i, s):
                q = i * SLOTS + s
                r.wait_loads(dve, i, s, 0, 1)
                dve.wait_ge(r.used, done(q))
                dve.tensor_tensor(z[:, s], z[:, s], own[:, s], ALU.add).then_inc(owned, 1)

            def add_bias(i, s):
                q = i * SLOTS + s
                dve.wait_ge(owned, done(q))
                dve.tensor_tensor(z[:, s], z[:, s], bc_rows(S.b2[:]), ALU.add).then_inc(ln.z_ready, 1)

            def statistics(i, s):
                ln.statistics(dve, i, s, z)

            def aggregate(i, s):
                ln.aggregate(dve, i, s, r.tick)

            def invert_std(i, s):
                ln.invert(dve, i, s)

            def offset(i, s):
                ln.offset(dve, i, s)

            pipelined(dve, r.iters, [
                (0, invert_std),
                (3, guard),
                (0, offset),
                (3, invert),
                (2, add_own),
                (3, divide),
                (2, add_bias),
                (2, statistics),
                (2, aggregate),
            ])

        @block.scalar
        def _(act):
            act.wait_ge(ln.eps_set, 1)
            r.prime_kept(act)

            def deviation(i, s):
                ln.deviation(act, i, s)

            def scale(i, s):
                ln.scale(act, i, s, z, res, r.ready, r)

            pipelined(act, r.iters, [
                (1, deviation),
                (0, scale),
            ])



def gin_rows(nc, T, A, S, name, dense, beside=None):
    with Phase(nc, name) as f:
        r = Rows(f, S, dense, stores=1 if dense else U, own_parts=1, copy=None if dense else T["X3E"])
        x = f.sb("x", [P, SLOTS, U, C])
        agg = None if dense else f.sb("agg", [P, SLOTS, U, C + 1])
        turned_t = f.sb("turned_t", [P, SLOTS, U * P])
        agg_t = None if dense else f.sb("agg_t", [P, SLOTS, U * P])
        pre_t = None if dense else f.sb("pre_t", [P, SLOTS, U * P])
        pre = None if dense else f.sb("pre", [P, SLOTS, U, C])
        hid = None if dense else f.sb("hid", [P, SLOTS, U * P])
        add = None if dense else f.sb("add", [P, SLOTS, U, C])
        w = f.sb("w", [P, 3, C])
        rows = f.sb("rows", [P, 4, C])
        b1 = f.sb("b1", [P, 1])
        z = f.sb("z", [P, SLOTS, U, C])
        y = f.sb("y", [P, SLOTS, U, C])
        shifted = f.sb("shifted", [P, SLOTS, U, C])
        z2 = f.sb("z2", [P, SLOTS, U, C])
        res = f.sb("res", [P, SLOTS, U, C])
        ps_t = f.ps("ps_t", [P, U * P])
        ps_o = [f.ps(f"ps_o{s}", [P, U * P]) for s in range(2)]
        ps_g = None if dense else f.ps("ps_g", [P, U * P])
        ps_p = None if dense else f.ps("ps_p", [P, U * P])
        ps_r = None if dense else f.ps("ps_r", [P, U * P])
        ps_1 = None if dense else f.ps("ps_1", [P, U * P])
        ps_2 = None if dense else f.ps("ps_2", [P, U * P])
        ln, ln2 = LayerNorm(f), LayerNorm(f, "2")
        turned, turned_out, own_h, normed, gained = (f.sem(n) for n in (
            "turned", "turned_out", "own_h", "normed", "gained"))
        shifted_x = f.sem("shifted_x")
        agg_turned, agg_out, pre_ready, counted, pre_turned, pre_out, layer1, relued, layer2, biased, added = (
            f.sem(n) for n in ("agg_turned", "agg_out", "pre_ready", "counted", "pre_turned", "pre_out", "layer1",
                               "relued", "layer2", "biased", "added"))
        sums = beside(f) if beside else None
        block = f.block()

        def run(eng, engine, steps):
            if sums:
                pipelined(eng, sums.iters, steps_of(sums, engine, eng), steps)
            else:
                pipelined(eng, r.iters, steps)

        @block.sync
        def _(sp):
            for out, src in ((w[:, 0, :], A["L2_Wpre"]), (w[:, 1, :], A["L2_W1"]), (w[:, 2, :], A["L2_W2"]),
                             (rows[:, 0, :], A["L2_bpre_rows"]), (rows[:, 1, :], A["L2_b2_rows"]),
                             (rows[:, 2, :], A["L2_gamma_rows"]), (rows[:, 3, :], A["L2_beta_rows"]),
                             (b1[:], A["L2_b1_col"])):
                sp.dma_start(out, src).then_inc(r.weights, 16)
            r.prime(sp, (shifted_x, turned, turned_out, own_h, normed, gained, agg_turned, agg_out, pre_ready, counted,
                         pre_turned, pre_out, layer1, relued, layer2, biased, added, *ln.sems, *ln2.sems))
            if sums:
                sums.sync_start(sp)
            if dense:
                run(sp, "sync", [(10, r.load_step(sp, [(x, groups_of(T["X2"]))]))])
            else:
                run(sp, "sync", [
                    (9, r.own_step(sp, x, T["X2E"], shifted_x)),
                    (11, r.load_step(sp, [(agg, groups_of(T["RAW129"]))])),
                ])
            r.finish(sp)
            if sums:
                sums.sync_end(sp)

        @block.gpsimd
        def _(pool):
            if sums:
                sums.pool_loop(pool)
            if not dense:
                r.prime_stores(pool)
                r.pool_loop(pool, scatters=(res, T["X3"], SCD, NP_))

        @block.tensor
        def _(pe):
            pe.wait_ge(r.weights, 16 * 8)
            if sums:
                sums.tensor_start(pe)

            def aggregate(i, s):
                q = i * SLOTS + s
                r.wait_loads(pe, i, s, 1)
                pe.wait_ge(agg_out, behind(q))
                for u in range(U):
                    t = pe.transpose(ps_g[:, u * P:(u + 1) * P], agg[:, s, u, 0:C], S.ident[:])
                t.then_inc(agg_turned, 1)

            def pre_layer(i, s):
                q = i * SLOTS + s
                pe.wait_ge(agg_out, done(q))
                pe.wait_ge(counted, behind(q))
                for u in range(U):
                    t = pe.matmul(ps_p[:, u * P:(u + 1) * P], agg_t[:, s, u * P:(u + 1) * P], w[:, 0, :],
                                  start=True, stop=True)
                t.then_inc(pre_ready, 1)

            def turn(i, s):
                q = i * SLOTS + s
                r.wait_loads(pe, i, s, 1 if dense else 0, 0 if dense else 1)
                pe.wait_ge(turned_out, behind(q))
                for u in range(U):
                    t = pe.transpose(ps_t[:, u * P:(u + 1) * P], x[:, s, u, :], S.ident[:])
                t.then_inc(turned, 1)

            def turn_pre(i, s):
                q = i * SLOTS + s
                pe.wait_ge(counted, done(q))
                pe.wait_ge(pre_out, behind(q))
                for u in range(U):
                    t = pe.transpose(ps_r[:, u * P:(u + 1) * P], pre[:, s, u, :], S.ident[:])
                t.then_inc(pre_turned, 1)

            def layer_1(i, s):
                q = i * SLOTS + s
                pe.wait_ge(pre_out, done(q))
                pe.wait_ge(relued, behind(q))
                pe.matmul(ps_1[:], w[:, 1, :], pre_t[:, s], start=True, stop=True).then_inc(layer1, 1)

            def layer_2(i, s):
                q = i * SLOTS + s
                pe.wait_ge(relued, done(q))
                pe.wait_ge(biased, behind(q))
                for u in range(U):
                    t = pe.matmul(ps_2[:, u * P:(u + 1) * P], hid[:, s, u * P:(u + 1) * P], w[:, 2, :],
                                  start=True, stop=True)
                t.then_inc(layer2, 1)

            def own(i, s):
                q = i * SLOTS + s
                pe.wait_ge(turned_out, done(q))
                pe.wait_ge(ln.z_ready, two_behind(q))
                for u in range(U):
                    t = pe.matmul(ps_o[s % 2][:, u * P:(u + 1) * P], turned_t[:, s, u * P:(u + 1) * P], w[:, 0, :],
                                  start=True, stop=True)
                t.then_inc(own_h, 1)

            run(pe, "tensor", [
                (5, own),
                *([(5, layer_2), (6, layer_1)] if not dense else []),
                (6, turn),
                *([(7, turn_pre), (8, pre_layer), (9, aggregate)] if not dense else []),
            ])

        @block.scalar
        def _(act):
            act.wait_ge(r.weights, 16 * 8)
            act.wait_ge(ln.eps_set, 1)
            act.wait_ge(ln2.eps_set, 1)
            if dense:
                r.prime_stores(act)
            else:
                r.prime_kept(act)
            if sums:
                sums.prime_stores(act)

            def take_agg(i, s):
                q = i * SLOTS + s
                act.wait_ge(agg_turned, done(q))
                act.wait_ge(pre_ready, free(q))
                act.activation(agg_t[:, s], ps_g[:], ACT.Copy).then_inc(agg_out, 1)

            def take_turned(i, s):
                q = i * SLOTS + s
                act.wait_ge(turned, done(q))
                act.wait_ge(own_h, free(q))
                act.activation(turned_t[:, s], ps_t[:], ACT.Copy).then_inc(turned_out, 1)

            def take_pre(i, s):
                q = i * SLOTS + s
                act.wait_ge(pre_turned, done(q))
                act.wait_ge(layer1, free(q))
                act.activation(pre_t[:, s], ps_r[:], ACT.Copy).then_inc(pre_out, 1)

            def take_hidden(i, s):
                q = i * SLOTS + s
                act.wait_ge(layer1, done(q))
                act.wait_ge(layer2, free(q))
                act.activation(hid[:, s], ps_1[:], ACT.Relu, bias=b1[:]).then_inc(relued, 1)

            def deviation(i, s):
                ln.deviation(act, i, s)

            def scale(i, s):
                ln.scale(act, i, s, z, y, normed)

            def deviation2(i, s):
                ln2.deviation(act, i, s)

            def scale2(i, s):
                ln2.scale(act, i, s, z2, res, r.ready, r, groups_of(T["X3"]) if dense else None)

            run(act, "scalar", [
                (1, deviation2),
                (4, deviation),
                (0, scale2),
                (3, scale),
                *([(6, take_hidden)] if not dense else []),
                (6, take_turned),
                *([(7, take_pre), (9, take_agg)] if not dense else []),
            ])

        @block.vector
        def _(dve):
            ln.setup(dve)
            ln2.setup(dve)
            if sums:
                sums.vector_start(dve)
            dve.wait_ge(r.weights, 16 * 8)

            def add_counted(i, s):
                q = i * SLOTS + s
                dve.wait_ge(pre_turned, free(q))
                dve.wait_ge(pre_ready, done(q))
                for u in range(U):
                    t = dve.scalar_tensor_tensor(pre[:, s, u, :], rows[:, 0, :], agg[:, s, u, C:C + 1],
                                                 ps_p[:, u * P:(u + 1) * P], ALU.mult, ALU.add)
                t.then_inc(counted, 1)
                dve.wait_ge(counted, done(q))
                dve.sem_inc(r.used, 1)

            def add_b2(i, s):
                q = i * SLOTS + s
                dve.wait_ge(layer2, done(q))
                dve.wait_ge(ln.z_ready, free(q))
                dve.tensor_tensor(add[:, s], ps_2[:].rearrange("p (u c) -> p u c", u=U),
                                  bc_rows(rows[:, 1, :]), ALU.add).then_inc(biased, 1)

            def relu(i, s):
                q = i * SLOTS + s
                dve.wait_ge(biased, done(q))
                for u in range(U):
                    t = dve.scalar_tensor_tensor(add[:, s, u, :], add[:, s, u, :], 0.0, rows[:, 0, :],
                                                 ALU.max, ALU.add)
                t.then_inc(added, 1)

            def add_hidden(i, s):
                q = i * SLOTS + s
                dve.wait_ge(own_h, done(q))
                dve.wait_ge(normed, free(q))
                if not dense:
                    dve.wait_ge(added, done(q))
                dve.tensor_tensor(z[:, s], ps_o[s % 2][:].rearrange("p (u c) -> p u c", u=U),
                                  bc_rows(S.c2[:]) if dense else add[:, s], ALU.add).then_inc(ln.z_ready, 1)

            def statistics(i, s):
                ln.statistics(dve, i, s, z)

            def aggregate(i, s):
                ln.aggregate(dve, i, s, r.tick)

            def invert_std(i, s):
                ln.invert(dve, i, s)

            def offset(i, s):
                ln.offset(dve, i, s)

            def gain(i, s):
                q = i * SLOTS + s
                dve.wait_ge(normed, done(q))
                dve.wait_ge(r.ready, free(q))
                dve.tensor_tensor(z2[:, s], y[:, s], bc_rows(rows[:, 2, :]), ALU.mult).then_inc(gained, 1)

            def shift(i, s):
                q = i * SLOTS + s
                dve.wait_ge(turned, done(q))
                r.wait_loads(dve, i, s, 1 if dense else 0, 0 if dense else 1)
                dve.wait_ge(ln2.z_ready, free(q))
                dve.tensor_tensor(shifted[:, s], x[:, s], bc_rows(rows[:, 3, :]), ALU.add
                                  ).then_inc(r.used if dense else shifted_x, 1)

            def add_own(i, s):
                q = i * SLOTS + s
                dve.wait_ge(gained, done(q))
                dve.wait_ge(r.used if dense else shifted_x, done(q))
                dve.tensor_tensor(z2[:, s], z2[:, s], shifted[:, s], ALU.add).then_inc(ln2.z_ready, 1)

            def statistics2(i, s):
                ln2.statistics(dve, i, s, z2)

            def aggregate2(i, s):
                ln2.aggregate(dve, i, s, r.tick)

            def invert_std2(i, s):
                ln2.invert(dve, i, s)

            def offset2(i, s):
                ln2.offset(dve, i, s)

            run(dve, "vector", [
                (0, invert_std2),
                (3, invert_std),
                (0, offset2),
                (3, offset),
                (2, gain),
                *([(5, add_b2)] if not dense else []),
                (2, add_own),
                *([(5, relu)] if not dense else []),
                *([(2, statistics2)] if not dense else []),
                (5, add_hidden),
                *([(2, statistics2)] if dense else []),
                (5, statistics),
                (2, aggregate2),
                (6, shift),
                (5, aggregate),
                *([(8, add_counted)] if not dense else []),
            ])


class Softplus:

    def __init__(self, f, name):
        self.absx = f.sb(f"absx{name}", [P, SLOTS, U * P])
        self.lg = f.sb(f"lg{name}", [P, SLOTS, U * P])
        self.abs_ready, self.exp_ready, self.log_ready = (f.sem(f"{n}{name}") for n in (
            "abs_ready", "exp_ready", "log_ready"))
        self.sems = [self.abs_ready, self.exp_ready, self.log_ready]

    def magnitude(self, act, i, s, x, x_ready, bias=0.0):
        q = i * SLOTS + s
        act.wait_ge(x_ready, done(q))
        act.wait_ge(self.log_ready, free(q))
        act.activation(self.absx[:, s], x, ACT.Abs, bias=bias).then_inc(self.abs_ready, 1)

    def exponential(self, act, i, s):
        q = i * SLOTS + s
        act.wait_ge(self.abs_ready, done(q))
        act.activation(self.absx[:, s], self.absx[:, s], ACT.Exp, scale=-1.0).then_inc(self.exp_ready, 1)

    def logarithm(self, act, i, s, used, one):
        q = i * SLOTS + s
        act.wait_ge(self.exp_ready, done(q))
        act.wait_ge(used, free(q))
        act.activation(self.lg[:, s], self.absx[:, s], ACT.Ln, bias=one).then_inc(self.log_ready, 1)


def messages(nc, T, A, S):
    with Phase(nc, "messages") as f:
        r = Rows(f, S, dense=True, stores=1, groups=EDGE_GROUPS)
        e = f.sb("e", [P, SLOTS, U, C])
        x = f.sb("x", [P, SLOTS, U, C])
        e_t = f.sb("e_t", [P, SLOTS, U * P])
        x_t = f.sb("x_t", [P, SLOTS, U * P])
        w = f.sb("w", [P, 3, C])
        rows = f.sb("rows", [P, 2, C])
        be1 = f.sb("be1", [P, 1])
        one = f.sb("one", [P, 1])
        pos = f.sb("pos", [P, SLOTS, U * P])
        act1 = f.sb("act1", [P, SLOTS, U * P])
        y = f.sb("y", [P, SLOTS, U, C])
        filt = f.sb("filt", [P, SLOTS, U, C])
        hn = f.sb("hn", [P, SLOTS, U, C])
        res = f.sb("res", [P, SLOTS, U, C])
        ps_e = f.ps("ps_e", [P, U * P])
        ps_x = f.ps("ps_x", [P, U * P])
        ps_1 = [f.ps(f"ps_1{s}", [P, U * P]) for s in range(2)]
        ps_2 = [f.ps(f"ps_2{s}", [P, U * P]) for s in range(2)]
        ps_n = f.ps("ps_n", [P, U * P])
        sp1, sp2 = Softplus(f, "1"), Softplus(f, "2")
        x_used, e_out, x_out, layer1, clipped, act1_ready, layer2, y_ready, node, hn_ready, filt_ready, one_set = (
            f.sem(n) for n in ("x_used", "e_out", "x_out", "layer1", "clipped", "act1_ready", "layer2", "y_ready",
                               "node", "hn_ready", "filt_ready", "one_set"))
        block = f.block()

        @block.sync
        def _(sp):
            for out, src in ((w[:, 0, :], A["L3_We1T"]), (w[:, 1, :], A["L3_We2T"]), (w[:, 2, :], A["L3_WnT"]),
                             (rows[:, 0, :], A["L3_be2_rows"]), (rows[:, 1, :], A["L3_bn_rows"]),
                             (be1[:], A["L3_be1_col"])):
                sp.dma_start(out, src).then_inc(r.weights, 16)
            r.prime(sp, (x_used, e_out, x_out, layer1, clipped, act1_ready, layer2, y_ready, node, hn_ready,
                         filt_ready, *sp1.sems, *sp2.sems))
            r.load(sp, [(e, groups_of(A["edge_attr"]))])
            r.finish(sp)

        @block.gpsimd
        def _(pool):
            r.pool_loop(pool, gathers=(x, T["X3"], SRCO, x_used))

        @block.tensor
        def _(pe):
            pe.wait_ge(r.weights, 16 * 6)

            def turn_e(i, s):
                q = i * SLOTS + s
                r.wait_loads(pe, i, s, 1)
                pe.wait_ge(e_out, behind(q))
                for u in range(U):
                    t = pe.transpose(ps_e[:, u * P:(u + 1) * P], e[:, s, u, :], S.ident[:])
                t.then_inc(r.used, 1)

            def turn_x(i, s):
                q = i * SLOTS + s
                r.wait_loads(pe, i, s, 0, 1)
                pe.wait_ge(x_out, behind(q))
                for u in range(U):
                    t = pe.transpose(ps_x[:, u * P:(u + 1) * P], x[:, s, u, :], S.ident[:])
                t.then_inc(x_used, 1)

            def layer_1(i, s):
                q = i * SLOTS + s
                pe.wait_ge(e_out, done(q))
                pe.wait_ge(clipped, two_behind(q))
                pe.wait_ge(sp1.abs_ready, two_behind(q))
                pe.matmul(ps_1[s % 2][:], w[:, 0, :], e_t[:, s], start=True, stop=True).then_inc(layer1, 1)

            def node_layer(i, s):
                q = i * SLOTS + s
                pe.wait_ge(x_out, done(q))
                pe.wait_ge(hn_ready, behind(q))
                for u in range(U):
                    t = pe.matmul(ps_n[:, u * P:(u + 1) * P], x_t[:, s, u * P:(u + 1) * P], w[:, 2, :],
                                  start=True, stop=True)
                t.then_inc(node, 1)

            def layer_2(i, s):
                q = i * SLOTS + s
                pe.wait_ge(act1_ready, done(q))
                pe.wait_ge(y_ready, two_behind(q))
                for u in range(U):
                    t = pe.matmul(ps_2[s % 2][:, u * P:(u + 1) * P], act1[:, s, u * P:(u + 1) * P], w[:, 1, :],
                                  start=True, stop=True)
                t.then_inc(layer2, 1)

            pipelined(pe, r.iters, [
                (6, layer_2),
                (6, node_layer),
                (7, turn_x),
                (10, layer_1),
                (11, turn_e),
            ])

        @block.scalar
        def _(act):
            act.wait_ge(r.weights, 16 * 6)
            act.wait_ge(one_set, 1)
            r.prime_stores(act)

            def take_e(i, s):
                q = i * SLOTS + s
                act.wait_ge(r.used, done(q))
                act.wait_ge(layer1, free(q))
                act.activation(e_t[:, s], ps_e[:], ACT.Copy).then_inc(e_out, 1)

            def take_x(i, s):
                q = i * SLOTS + s
                act.wait_ge(x_used, done(q))
                act.wait_ge(node, free(q))
                act.activation(x_t[:, s], ps_x[:], ACT.Copy).then_inc(x_out, 1)

            def abs_1(i, s):
                sp1.magnitude(act, i, s, ps_1[s % 2][:], clipped, bias=be1[:])

            def abs_2(i, s):
                sp2.magnitude(act, i, s, y[:, s].rearrange("p u c -> p (u c)"), y_ready)

            def store(i, s):
                r.store(act, i, s, (res, groups_of(T["M"])))

            pipelined(act, r.iters, [
                (0, store),
                (4, in_pairs(lambda i, s: sp2.exponential(act, i, s))),
                (8, in_pairs(lambda i, s: sp1.exponential(act, i, s))),
                (4, in_pairs(lambda i, s: sp2.logarithm(act, i, s, filt_ready, one[:]))),
                (8, in_pairs(lambda i, s: sp1.logarithm(act, i, s, act1_ready, one[:]))),
                (5, abs_2),
                (7, take_x),
                (9, abs_1),
                (11, take_e),
            ])

        @block.vector
        def _(dve):
            dve.memset(one[:], 1.0).then_inc(one_set, 1)
            dve.wait_ge(r.weights, 16 * 6)

            def clip(i, s):
                q = i * SLOTS + s
                dve.wait_ge(act1_ready, free(q))
                dve.wait_ge(layer1, done(q))
                dve.tensor_scalar(pos[:, s], ps_1[s % 2][:], be1[:], 0.0, ALU.add, ALU.max).then_inc(clipped, 1)

            def node_bias(i, s):
                q = i * SLOTS + s
                dve.wait_ge(node, done(q))
                dve.wait_ge(r.ready, free(q))
                dve.tensor_tensor(hn[:, s], ps_n[:].rearrange("p (u c) -> p u c", u=U), bc_rows(rows[:, 1, :]),
                                  ALU.add).then_inc(hn_ready, 1)

            def activate(i, s):
                q = i * SLOTS + s
                dve.wait_ge(sp1.log_ready, done(q))
                dve.wait_ge(clipped, done(q))
                dve.wait_ge(layer2, free(q))
                dve.scalar_tensor_tensor(act1[:, s], sp1.lg[:, s], -LOG2, pos[:, s], ALU.add, ALU.add
                                         ).then_inc(act1_ready, 1)

            def bias2(i, s):
                q = i * SLOTS + s
                dve.wait_ge(layer2, done(q))
                dve.wait_ge(sp2.abs_ready, free(q))
                dve.wait_ge(filt_ready, free(q))
                dve.tensor_tensor(y[:, s], ps_2[s % 2][:].rearrange("p (u c) -> p u c", u=U), bc_rows(rows[:, 0, :]),
                                  ALU.add).then_inc(y_ready, 1)

            def filter(i, s):
                q = i * SLOTS + s
                dve.wait_ge(sp2.log_ready, done(q))
                dve.wait_ge(r.ready, free(q))
                dve.scalar_tensor_tensor(filt[:, s].rearrange("p u c -> p (u c)"),
                                         y[:, s].rearrange("p u c -> p (u c)"), 0.0, sp2.lg[:, s],
                                         ALU.max, ALU.add).then_inc(filt_ready, 1)

            def message(i, s):
                q = i * SLOTS + s
                dve.wait_ge(filt_ready, done(q))
                dve.wait_ge(hn_ready, done(q))
                r.out_free(dve, i, s)
                dve.scalar_tensor_tensor(res[:, s].rearrange("p u c -> p (u c)"),
                                         filt[:, s].rearrange("p u c -> p (u c)"), -LOG2,
                                         hn[:, s].rearrange("p u c -> p (u c)"), ALU.add, ALU.mult
                                         ).then_inc(r.ready, 1)

            pipelined(dve, r.iters, [
                (5, bias2),
                (2, filter),
                (6, activate),
                (2, message),
                (6, node_bias),
                (10, clip),
            ])


def schnet_rows(nc, T, A, S, out):
    with Phase(nc, "schnet") as f:
        r = Rows(f, S, dense=False, stores=U, own_parts=1)
        agg = f.sb("agg", [P, SLOTS, U, C])
        own = f.sb("own", [P, SLOTS, U, C])
        agg_t = f.sb("agg_t", [P, SLOTS, U * P])
        w = f.sb("w", [P, 2, C])
        brow = f.sb("brow", [P, C])
        b1 = f.sb("b1", [P, 1])
        one = f.sb("one", [P, 1])
        pos = f.sb("pos", [P, SLOTS, U * P])
        hid = f.sb("hid", [P, SLOTS, U * P])
        z = f.sb("z", [P, SLOTS, U, C])
        res = f.sb("res", [P, SLOTS, U, C])
        ps_t = f.ps("ps_t", [P, U * P])
        ps_1 = [f.ps(f"ps_1{s}", [P, U * P]) for s in range(2)]
        ps_2 = [f.ps(f"ps_2{s}", [P, U * P]) for s in range(2)]
        sp1 = Softplus(f, "1")
        ln = LayerNorm(f)
        agg_out, layer1, clipped, hid_ready, layer2, owned, one_set = (f.sem(n) for n in (
            "agg_out", "layer1", "clipped", "hid_ready", "layer2", "owned", "one_set"))
        block = f.block()

        @block.sync
        def _(sp):
            for dst, src in ((w[:, 0, :], A["L3_Wfc1T"]), (w[:, 1, :], A["L3_Wfc2T"]),
                             (brow[:], A["L3_bfc2_rows"]), (b1[:], A["L3_bfc1_col"])):
                sp.dma_start(dst, src).then_inc(r.weights, 16)
            r.prime(sp, (agg_out, layer1, clipped, hid_ready, layer2, owned, *sp1.sems, *ln.sems))
            pipelined(sp, r.iters, [
                (6, r.own_step(sp, own, T["X3E"], owned)),
                (12, r.load_step(sp, [(agg, groups_of(T["RAW128"]))])),
            ])
            r.finish(sp)

        @block.gpsimd
        def _(pool):
            r.prime_stores(pool)
            r.pool_loop(pool, scatters=(res, out, SCD, NP_))

        @block.tensor
        def _(pe):
            pe.wait_ge(r.weights, 16 * 4)

            def turn(i, s):
                q = i * SLOTS + s
                r.wait_loads(pe, i, s, 1)
                pe.wait_ge(agg_out, behind(q))
                for u in range(U):
                    t = pe.transpose(ps_t[:, u * P:(u + 1) * P], agg[:, s, u, :], S.ident[:])
                t.then_inc(r.used, 1)

            def layer_1(i, s):
                q = i * SLOTS + s
                pe.wait_ge(agg_out, done(q))
                pe.wait_ge(clipped, two_behind(q))
                pe.wait_ge(sp1.abs_ready, two_behind(q))
                pe.matmul(ps_1[s % 2][:], w[:, 0, :], agg_t[:, s], start=True, stop=True).then_inc(layer1, 1)

            def layer_2(i, s):
                q = i * SLOTS + s
                pe.wait_ge(hid_ready, done(q))
                pe.wait_ge(owned, two_behind(q))
                for u in range(U):
                    t = pe.matmul(ps_2[s % 2][:, u * P:(u + 1) * P], hid[:, s, u * P:(u + 1) * P], w[:, 1, :],
                                  start=True, stop=True)
                t.then_inc(layer2, 1)

            pipelined(pe, r.iters, [
                (3, layer_2),
                (8, layer_1),
                (9, turn),
            ])

        @block.scalar
        def _(act):
            act.wait_ge(r.weights, 16 * 4)
            act.wait_ge(one_set, 1)
            act.wait_ge(ln.eps_set, 1)

            def take_agg(i, s):
                q = i * SLOTS + s
                act.wait_ge(r.used, done(q))
                act.wait_ge(layer1, free(q))
                act.activation(agg_t[:, s], ps_t[:], ACT.Copy).then_inc(agg_out, 1)

            def absolute(i, s):
                sp1.magnitude(act, i, s, ps_1[s % 2][:], clipped, bias=b1[:])

            def exponential(i, s):
                sp1.exponential(act, i, s)

            def logarithm(i, s):
                sp1.logarithm(act, i, s, hid_ready, one[:])

            def deviation(i, s):
                ln.deviation(act, i, s)

            def scale(i, s):
                ln.scale(act, i, s, z, res, r.ready, r)

            pipelined(act, r.iters, [
                (2, in_pairs(deviation)),
                (6, in_pairs(exponential)),
                (0, scale),
                (6, in_pairs(logarithm)),
                (7, absolute),
                (9, take_agg),
            ])

        @block.vector
        def _(dve):
            ln.setup(dve)
            dve.memset(one[:], 1.0).then_inc(one_set, 1)
            dve.wait_ge(r.weights, 16 * 4)

            def clip(i, s):
                q = i * SLOTS + s
                dve.wait_ge(hid_ready, free(q))
                dve.wait_ge(layer1, done(q))
                dve.tensor_scalar(pos[:, s], ps_1[s % 2][:], b1[:], 0.0, ALU.add, ALU.max).then_inc(clipped, 1)

            def activate(i, s):
                q = i * SLOTS + s
                dve.wait_ge(sp1.log_ready, done(q))
                dve.wait_ge(clipped, done(q))
                dve.wait_ge(layer2, free(q))
                dve.scalar_tensor_tensor(hid[:, s], sp1.lg[:, s], -LOG2, pos[:, s], ALU.add, ALU.add
                                         ).then_inc(hid_ready, 1)

            def add_own(i, s):
                q = i * SLOTS + s
                dve.wait_ge(layer2, done(q))
                r.wait_loads(dve, i, s, 0, 1)
                dve.wait_ge(r.ready, free(q))
                dve.tensor_tensor(z[:, s], ps_2[s % 2][:].rearrange("p (u c) -> p u c", u=U), own[:, s], ALU.add
                                  ).then_inc(owned, 1)

            def add_bias(i, s):
                q = i * SLOTS + s
                dve.wait_ge(owned, done(q))
                dve.tensor_tensor(z[:, s], z[:, s], bc_rows(brow[:]), ALU.add).then_inc(ln.z_ready, 1)

            def statistics(i, s):
                ln.statistics(dve, i, s, z)

            def aggregate(i, s):
                ln.aggregate(dve, i, s, r.tick)

            def invert_std(i, s):
                ln.invert(dve, i, s)

            def offset(i, s):
                ln.offset(dve, i, s)

            pipelined(dve, r.iters, [
                (0, invert_std),
                (0, offset),
                (3, add_own),
                (4, activate),
                (3, add_bias),
                (8, clip),
                (3, statistics),
                (3, aggregate),
            ])



SCRATCH = {"sorted": (P, 3 * SORT_F), "keys": (2, SORT_N + 2), "last": (2, 2 * P), "ends": (HEADS, 2 * EDGE_TILES),
           "E": (N_HYPER, C), "EW": (N_HYPER, C + 1), "X1": (NP_, C), "X1A": (NP_, C + 2 * HEADS), "H2": (NP_, H2W),
           "XS": (EP, C), "XD": (EP, C), "HS": (EP, C), "HD": (EP, C), "X2E": (EP, C), "X3E": (EP, C),
           "X2": (NP_, C), "X3": (NP_, C), "M": (EP, C),
           "RAW129": (EP, C + 1), "RAW128": (EP, C), "RAW260": (EP, HC + HEADS)}


def build(nc, A, out, upto=None):
    T = {n: nc.dram_tensor(n, s, F32, kind="Internal").ap() for n, s in SCRATCH.items()}
    raw = T["RAW129"]
    with ExitStack() as ctx:
        S = Tables(nc, ctx, A["ident"])
        sort_phase(nc, T, A)
        index_phase(nc, T, A, S)
        if upto == "index":
            return T
        weights_phase(nc, A, S)
        sum_pass(nc, T, S, "e1", 0, A["x"], SRC, C + 1, raw, "ones",
                 norm=lambda f: NodeNorm(f, S, [A["x"]], S.b0[:], T["X1"], half=0))
        fix_pass(nc, S, "e1fix", 0, raw, C + 1)
        hyper_rows(nc, T, S, "e1rows", raw, T["E"], affine=False)
        join_weights(nc, T, "e1join")
        sum_pass(nc, T, S, "n1", 1, T["EW"], HYP, C + 1, raw,
                 norm=lambda f: NodeNorm(f, S, [A["x"]], S.b0[:], T["X1"], half=1))
        fix_pass(nc, S, "n1fix", 1, raw, C + 1)
        node_rows(nc, T, A, S, "n1rows", raw, 1)
        batch_norm(nc, A, S)
        if upto == "bn":
            return T
        sum_pass(nc, T, S, "e2", 0, T["X1"], SRC, C + 1, raw, "ones")
        fix_pass(nc, S, "e2fix", 0, raw, C + 1)
        hyper_rows(nc, T, S, "e2rows", raw, T["E"], affine=True)
        join_weights(nc, T, "e2join")
        sum_pass(nc, T, S, "n2", 1, T["EW"], HYP, C + 1, raw)
        fix_pass(nc, S, "n2fix", 1, raw, C + 1)
        node_rows(nc, T, A, S, "n2rows", raw, 2)
        if upto == "x1":
            return T
        gat_rows(nc, T, S, "gat1dense", dense=True)
        attention_phase(nc, T, S, "att1", HEADS, T["X1A"], (T["XS"], T["XD"]))
        gat_sum(nc, T, S, "gat1sum", 1)
        fix_pass(nc, S, "gat1fix", 0, T["RAW260"], HC + HEADS)
        gat_rows(nc, T, S, "gat1rows", dense=False)
        if upto == "h2":
            return T
        attention_phase(nc, T, S, "att2", 1, T["H2"], (T["HS"], T["HD"]),
                        norm=lambda f: NodeNorm(f, S, [T["X1"], T["H2"]], S.b2[:], T["X2"]))
        gat_sum(nc, T, S, "gat2sum", 2)
        fix_pass(nc, S, "gat2fix", 0, raw, C + 1)
        gat_nodes(nc, T, S)
        if upto == "x2":
            return T
        gin_rows(nc, T, A, S, "gindense", dense=True,
                 beside=lambda f: SegmentSum(f, T, S, 0, T["X2"], SRC, C + 1, raw, "ones"))
        fix_pass(nc, S, "ginfix", 0, raw, C + 1)
        gin_rows(nc, T, A, S, "ginrows", dense=False)
        if upto == "x3":
            return T
        messages(nc, T, A, S)
        sum_pass(nc, T, S, "sch", 0, T["M"], PERM, C, T["RAW128"],
                 norm=lambda f: NodeNorm(f, S, [T["X3"]], S.c3[:], out))
        fix_pass(nc, S, "schfix", 0, T["RAW128"], C)
        schnet_rows(nc, T, A, S, out)
    return T


def lay_out(inputs):
    import numpy as np

    a = {k: np.asarray(v) for k, v in inputs.items()}

    def padded(x, rows, fill=0):
        out = np.full((rows, *x.shape[1:]), fill, x.dtype)
        out[:len(x)] = x
        return out

    def rows(x):
        return np.ascontiguousarray(np.broadcast_to(x.reshape(1, -1), (P, x.size)))

    def turned(x):
        return np.ascontiguousarray(x.T)

    src, dst = a["src"].astype(np.int32), a["dst"].astype(np.int32)
    src_p, dst_p = padded(src, SORT_N, N_NODES), padded(dst, SORT_N, N_NODES)
    out = dict(constants())
    out.update(
        x=padded(a["x"], NP_), edge_attr=padded(a["edge_attr_128"], EP),
        src=src_p.reshape(P, SORT_F), dst=dst_p.reshape(P, SORT_F),
        src_cols=turned(src_p[:EP].reshape(EDGE_TILES, P)),
        hw=np.ascontiguousarray(a["L0_gnn_hyperedge_weight"].reshape(-1, 1)),
        L0_W1T=turned(a["L0_gnn_W1"]), L0_W2T=turned(a["L0_gnn_W2"]),
        L0_b1_rows=rows(a["L0_gnn_b1"]), L0_gamma_rows=rows(a["L0_gnn_gamma"]),
        L0_beta_rows=rows(a["L0_gnn_beta"]), L0_b2_rows=rows(a["L0_gnn_b2"]),
        L1_W1=a["L1_gnn_W1"], L1_W2=np.ascontiguousarray(a["L1_gnn_W2"].reshape(2, P, C).transpose(1, 0, 2)),
        L1_b1_cols=turned(a["L1_gnn_b1"].reshape(2, P)),
        L1_as1=rows(a["L1_gnn_att_src1"]), L1_ad1=rows(a["L1_gnn_att_dst1"]),
        L1_as2=rows(a["L1_gnn_att_src2"]), L1_ad2=rows(a["L1_gnn_att_dst2"]), L1_b2_rows=rows(a["L1_gnn_b2"]),
        L2_Wpre=a["L2_gnn_W_pre"], L2_W1=a["L2_gnn_W1"], L2_W2=a["L2_gnn_W2"],
        L2_b1_col=np.ascontiguousarray(a["L2_gnn_b1"].reshape(-1, 1)),
        L2_b2_rows=rows(a["L2_gnn_b2"]), L2_bpre_rows=rows(a["L2_gnn_b_pre"]),
        L2_gamma_rows=rows(a["L2_gnn_gamma"]), L2_beta_rows=rows(a["L2_gnn_beta"]),
        L3_WnT=turned(a["L3_gnn_W_node"]), L3_bn_rows=rows(a["L3_gnn_b_node"]),
        L3_We1T=turned(a["L3_gnn_W_e1"]), L3_be1_col=np.ascontiguousarray(a["L3_gnn_b_e1"].reshape(-1, 1)),
        L3_We2T=turned(a["L3_gnn_W_e2"]), L3_be2_rows=rows(a["L3_gnn_b_e2"]),
        L3_Wfc1T=turned(a["L3_gnn_W_fc1"]), L3_bfc1_col=np.ascontiguousarray(a["L3_gnn_b_fc1"].reshape(-1, 1)),
        L3_Wfc2T=turned(a["L3_gnn_W_fc2"]), L3_bfc2_rows=rows(a["L3_gnn_b_fc2"]),
    )
    return out


def kernel(**inputs):
    import numpy as np
    import concourse.bacc as bacc
    from concourse.bass_utils import run_bass_kernel_spmd

    nc = bacc.Bacc("TRN2", target_bir_lowering=False, num_devices=1)
    arrays = {f"in_{n}": x for n, x in lay_out(inputs).items()}
    A = {n[3:]: nc.dram_tensor(n, x.shape, mybir.dt.from_np(x.dtype), kind="ExternalInput").ap()
         for n, x in arrays.items()}
    out = nc.dram_tensor("out", (NP_, C), F32, kind="ExternalOutput").ap()
    build(nc, A, out)
    ran = run_bass_kernel_spmd(nc, [arrays], core_ids=[0])
    return np.asarray(ran.results[0]["out"])[:N_NODES]
```
